# Optimizing a Trainium2 kernel written in Bass

```python
import numpy as np
import jax
import jax.numpy as jnp

def _softmax(x, axis=-1):
    return jax.nn.softmax(x, axis=axis)

def _gelu(x):
    return jax.nn.gelu(x, approximate=True)

def _silu(x):
    return jax.nn.silu(x)

def _sigmoid(x):
    return jax.nn.sigmoid(x)

def _layernorm(x, axis=-1, eps=1e-05):
    m = jnp.mean(x, axis=axis, keepdims=True)
    v = jnp.var(x, axis=axis, keepdims=True)
    return (x - m) / jnp.sqrt(v + eps)

def _scatter_add(tgt, idx, src, axis=0):
    return tgt.at[idx].add(src)

def _segment_sum(src, seg, n):
    return jax.ops.segment_sum(src, seg, n)
kernel_name = 'mk_sandwich_d1_jaxref_r8_d59c61'

def setup_inputs(seed: int=0):
    np.random.seed(seed)
    _w = jnp.asarray

    def _L0_attn_setup():
        import jax, jax.numpy as jnp
        import numpy as np
        B, S, D, H, NB = (2, 256, 128, 16, 32)
        DH = D // H
        MLP = 512
        CLUSTER_SCORE = 0.1
        LN_EPS = 1e-06

        def _layernorm(x, g, b):
            mu = jnp.mean(x, axis=-1, keepdims=True)
            var = jnp.mean(jnp.square(x - mu), axis=-1, keepdims=True)
            return (x - mu) * jax.lax.rsqrt(var + LN_EPS) * g + b

        def _lha_attention(x, Wq, Wk, Wv, Whq, Whk, Wo):
            q = jnp.einsum('bsd,dhf->bshf', x, Wq)
            k = jnp.einsum('bsd,dhf->bshf', x, Wk)
            v = jnp.einsum('bsd,dhf->bshf', x, Wv)
            qb = jax.nn.softmax(jnp.einsum('bshf,hfn->bshn', q, Whq), axis=-1)
            kb = jax.nn.softmax(jnp.einsum('bshf,hfn->bshn', k, Whk), axis=-1)
            logits = jnp.einsum('bqhf,bkhf->bhqk', q, k) / jnp.sqrt(jnp.float32(DH))
            aff = jnp.einsum('bqhn,bkhn->bhqk', qb, kb)
            logits = logits + CLUSTER_SCORE * aff
            attn = jax.nn.softmax(logits, axis=-1)
            out = jnp.einsum('bhqk,bkhf->bqhf', attn, v)
            out = jnp.einsum('bqhf,hfd->bqd', out, Wo)
            mq = jnp.mean(qb, axis=(0, 1))
            mk = jnp.mean(kb, axis=(0, 1))
            extra_loss = 0.5 * NB * (jnp.mean(jnp.sum(mq * mq, -1)) + jnp.mean(jnp.sum(mk * mk, -1)))
            return (out, extra_loss)

        def _reference_tuple_inner(inputs, ln1_g, ln1_b, Wq, Wk, Wv, Whq, Whk, Wo, ln2_g, ln2_b, W1, b1, W2, b2):
            x = _layernorm(inputs, ln1_g, ln1_b)
            attn_out, extra_loss = _lha_attention(x, Wq, Wk, Wv, Whq, Whk, Wo)
            x = attn_out + inputs
            y = _layernorm(x, ln2_g, ln2_b)
            y = jax.nn.relu(jnp.einsum('bsd,dm->bsm', y, W1) + b1)
            y = jnp.einsum('bsm,md->bsd', y, W2) + b2
            return (x + y, extra_loss)
        key = jax.random.key(seed)
        ks = jax.random.split(key, 10)
        std = 0.02
        return {'inputs': jax.random.normal(ks[0], (B, S, D), jnp.float32), 'ln1_g': jnp.ones((D,), jnp.float32), 'ln1_b': jnp.zeros((D,), jnp.float32), 'Wq': jax.random.normal(ks[1], (D, H, DH), jnp.float32) * std, 'Wk': jax.random.normal(ks[2], (D, H, DH), jnp.float32) * std, 'Wv': jax.random.normal(ks[3], (D, H, DH), jnp.float32) * std, 'Whq': jax.random.normal(ks[4], (H, DH, NB), jnp.float32) * std, 'Whk': jax.random.normal(ks[5], (H, DH, NB), jnp.float32) * std, 'Wo': jax.random.normal(ks[6], (H, DH, D), jnp.float32) * std, 'ln2_g': jnp.ones((D,), jnp.float32), 'ln2_b': jnp.zeros((D,), jnp.float32), 'W1': jax.random.normal(ks[7], (D, MLP), jnp.float32) * std, 'b1': jnp.zeros((MLP,), jnp.float32), 'W2': jax.random.normal(ks[8], (MLP, D), jnp.float32) * std, 'b2': jnp.zeros((D,), jnp.float32)}
    _L0_attn_in = _L0_attn_setup()

    def _L0_ffn_setup():
        import jax, jax.numpy as jnp
        import numpy as np
        L, H, NH, NKV, HD, FF, E, K = (4, 128, 16, 4, 64, 256, 8, 2)
        B, S = (2, 256)
        THETA, EPS = (10000.0, 1e-05)

        def _rms(x, w):
            return x * jax.lax.rsqrt(jnp.mean(x * x, axis=-1, keepdims=True) + EPS) * w

        def _rope_cos_sin(seq_len, head_dim, theta):
            inv = 1.0 / theta ** (jnp.arange(0, head_dim, 2, dtype=jnp.float32) / head_dim)
            f = jnp.arange(seq_len, dtype=jnp.float32)[:, None] * inv
            emb = jnp.concatenate([f, f], axis=-1)
            return (jnp.cos(emb), jnp.sin(emb))

        def _rot_half(x):
            h = x.shape[-1] // 2
            return jnp.concatenate([-x[..., h:], x[..., :h]], axis=-1)

        def _attention(x, wq, wk, wv, wo, cos, sin, causal_bias):
            b, s, _ = x.shape
            q = (x @ wq).reshape(b, s, NH, HD).transpose(0, 2, 1, 3)
            k = (x @ wk).reshape(b, s, NKV, HD).transpose(0, 2, 1, 3)
            v = (x @ wv).reshape(b, s, NKV, HD).transpose(0, 2, 1, 3)
            c = cos[None, None]
            sn = sin[None, None]
            q = q * c + _rot_half(q) * sn
            k = k * c + _rot_half(k) * sn
            rep = NH // NKV
            k = jnp.repeat(k, rep, axis=1)
            v = jnp.repeat(v, rep, axis=1)
            scores = jnp.einsum('bhqd,bhkd->bhqk', q, k) / jnp.sqrt(jnp.asarray(HD, x.dtype))
            scores = scores + causal_bias
            attn = jax.nn.softmax(scores, axis=-1)
            out = jnp.einsum('bhqk,bhkd->bhqd', attn, v)
            out = out.transpose(0, 2, 1, 3).reshape(b, s, NH * HD)
            return out @ wo

        def _moe(x, wr, wg, wu, wd):
            logits = x @ wr
            probs = jax.nn.softmax(logits, axis=-1)
            topv, topi = jax.lax.top_k(probs, K)
            topv = topv / jnp.sum(topv, axis=-1, keepdims=True)
            comb = jnp.sum(jax.nn.one_hot(topi, E, dtype=x.dtype) * topv[..., None], axis=-2)
            out = jnp.zeros_like(x)
            for e in range(E):
                h = jax.nn.silu(x @ wg[e]) * (x @ wu[e])
                out = out + comb[..., e:e + 1] * (h @ wd[e])
            return out
        key = jax.random.key(seed)
        ks = jax.random.split(key, 12)
        sc = 0.02
        inp = {'hidden_states': jax.random.normal(ks[0], (B, S, H), jnp.float32), 'ln1_w': jnp.ones((L, H), jnp.float32), 'ln2_w': jnp.ones((L, H), jnp.float32), 'wq': jax.random.normal(ks[1], (L, H, NH * HD), jnp.float32) * sc, 'wk': jax.random.normal(ks[2], (L, H, NKV * HD), jnp.float32) * sc, 'wv': jax.random.normal(ks[3], (L, H, NKV * HD), jnp.float32) * sc, 'wo': jax.random.normal(ks[4], (L, NH * HD, H), jnp.float32) * sc, 'wr': jax.random.normal(ks[5], (L, H, E), jnp.float32) * sc, 'wg': jax.random.normal(ks[6], (L, E, H, FF), jnp.float32) * sc, 'wu': jax.random.normal(ks[7], (L, E, H, FF), jnp.float32) * sc, 'wd': jax.random.normal(ks[8], (L, E, FF, H), jnp.float32) * sc}
        return inp
    _L0_ffn_in = _L0_ffn_setup()
    _d = {'L0_attn_inputs': _L0_attn_in['inputs'], 'L0_attn_ln1_g': _L0_attn_in['ln1_g'], 'L0_attn_ln1_b': _L0_attn_in['ln1_b'], 'L0_attn_Wq': _L0_attn_in['Wq'], 'L0_attn_Wk': _L0_attn_in['Wk'], 'L0_attn_Wv': _L0_attn_in['Wv'], 'L0_attn_Whq': _L0_attn_in['Whq'], 'L0_attn_Whk': _L0_attn_in['Whk'], 'L0_attn_Wo': _L0_attn_in['Wo'], 'L0_attn_ln2_g': _L0_attn_in['ln2_g'], 'L0_attn_ln2_b': _L0_attn_in['ln2_b'], 'L0_attn_W1': _L0_attn_in['W1'], 'L0_attn_b1': _L0_attn_in['b1'], 'L0_attn_W2': _L0_attn_in['W2'], 'L0_attn_b2': _L0_attn_in['b2'], 'L0_ffn_ln1_w': _L0_ffn_in['ln1_w'], 'L0_ffn_ln2_w': _L0_ffn_in['ln2_w'], 'L0_ffn_wq': _L0_ffn_in['wq'], 'L0_ffn_wk': _L0_ffn_in['wk'], 'L0_ffn_wv': _L0_ffn_in['wv'], 'L0_ffn_wo': _L0_ffn_in['wo'], 'L0_ffn_wr': _L0_ffn_in['wr'], 'L0_ffn_wg': _L0_ffn_in['wg'], 'L0_ffn_wu': _L0_ffn_in['wu'], 'L0_ffn_wd': _L0_ffn_in['wd']}
    _x0 = _d['L0_attn_inputs']
    _d['L0_attn_inputs'] = jax.random.normal(jax.random.fold_in(jax.random.key(seed), 1), (2, 1024, 128), dtype=_x0.dtype)
    del _x0
    return _d

def reference(L0_attn_inputs, L0_attn_ln1_g, L0_attn_ln1_b, L0_attn_Wq, L0_attn_Wk, L0_attn_Wv, L0_attn_Whq, L0_attn_Whk, L0_attn_Wo, L0_attn_ln2_g, L0_attn_ln2_b, L0_attn_W1, L0_attn_b1, L0_attn_W2, L0_attn_b2, L0_ffn_ln1_w, L0_ffn_ln2_w, L0_ffn_wq, L0_ffn_wk, L0_ffn_wv, L0_ffn_wo, L0_ffn_wr, L0_ffn_wg, L0_ffn_wu, L0_ffn_wd):

    def _L0_attn_ref(inputs, ln1_g, ln1_b, Wq, Wk, Wv, Whq, Whk, Wo, ln2_g, ln2_b, W1, b1, W2, b2):
        import jax, jax.numpy as jnp
        import numpy as np
        B, S, D, H, NB = (2, 256, 128, 16, 32)
        DH = D // H
        MLP = 512
        CLUSTER_SCORE = 0.1
        LN_EPS = 1e-06

        def _layernorm(x, g, b):
            mu = jnp.mean(x, axis=-1, keepdims=True)
            var = jnp.mean(jnp.square(x - mu), axis=-1, keepdims=True)
            return (x - mu) * jax.lax.rsqrt(var + LN_EPS) * g + b

        def _lha_attention(x, Wq, Wk, Wv, Whq, Whk, Wo):
            q = jnp.einsum('bsd,dhf->bshf', x, Wq)
            k = jnp.einsum('bsd,dhf->bshf', x, Wk)
            v = jnp.einsum('bsd,dhf->bshf', x, Wv)
            qb = jax.nn.softmax(jnp.einsum('bshf,hfn->bshn', q, Whq), axis=-1)
            kb = jax.nn.softmax(jnp.einsum('bshf,hfn->bshn', k, Whk), axis=-1)
            logits = jnp.einsum('bqhf,bkhf->bhqk', q, k) / jnp.sqrt(jnp.float32(DH))
            aff = jnp.einsum('bqhn,bkhn->bhqk', qb, kb)
            logits = logits + CLUSTER_SCORE * aff
            attn = jax.nn.softmax(logits, axis=-1)
            out = jnp.einsum('bhqk,bkhf->bqhf', attn, v)
            out = jnp.einsum('bqhf,hfd->bqd', out, Wo)
            mq = jnp.mean(qb, axis=(0, 1))
            mk = jnp.mean(kb, axis=(0, 1))
            extra_loss = 0.5 * NB * (jnp.mean(jnp.sum(mq * mq, -1)) + jnp.mean(jnp.sum(mk * mk, -1)))
            return (out, extra_loss)

        def _reference_tuple_inner(inputs, ln1_g, ln1_b, Wq, Wk, Wv, Whq, Whk, Wo, ln2_g, ln2_b, W1, b1, W2, b2):
            x = _layernorm(inputs, ln1_g, ln1_b)
            attn_out, extra_loss = _lha_attention(x, Wq, Wk, Wv, Whq, Whk, Wo)
            x = attn_out + inputs
            y = _layernorm(x, ln2_g, ln2_b)
            y = jax.nn.relu(jnp.einsum('bsd,dm->bsm', y, W1) + b1)
            y = jnp.einsum('bsm,md->bsd', y, W2) + b2
            return (x + y, extra_loss)
        return _reference_tuple_inner(inputs, ln1_g, ln1_b, Wq, Wk, Wv, Whq, Whk, Wo, ln2_g, ln2_b, W1, b1, W2, b2)[0]

    def _L0_ffn_ref(hidden_states, ln1_w, ln2_w, wq, wk, wv, wo, wr, wg, wu, wd):
        import jax, jax.numpy as jnp
        import numpy as np
        L, H, NH, NKV, HD, FF, E, K = (4, 128, 16, 4, 64, 256, 8, 2)
        B, S = (2, 256)
        THETA, EPS = (10000.0, 1e-05)

        def _rms(x, w):
            return x * jax.lax.rsqrt(jnp.mean(x * x, axis=-1, keepdims=True) + EPS) * w

        def _rope_cos_sin(seq_len, head_dim, theta):
            inv = 1.0 / theta ** (jnp.arange(0, head_dim, 2, dtype=jnp.float32) / head_dim)
            f = jnp.arange(seq_len, dtype=jnp.float32)[:, None] * inv
            emb = jnp.concatenate([f, f], axis=-1)
            return (jnp.cos(emb), jnp.sin(emb))

        def _rot_half(x):
            h = x.shape[-1] // 2
            return jnp.concatenate([-x[..., h:], x[..., :h]], axis=-1)

        def _attention(x, wq, wk, wv, wo, cos, sin, causal_bias):
            b, s, _ = x.shape
            q = (x @ wq).reshape(b, s, NH, HD).transpose(0, 2, 1, 3)
            k = (x @ wk).reshape(b, s, NKV, HD).transpose(0, 2, 1, 3)
            v = (x @ wv).reshape(b, s, NKV, HD).transpose(0, 2, 1, 3)
            c = cos[None, None]
            sn = sin[None, None]
            q = q * c + _rot_half(q) * sn
            k = k * c + _rot_half(k) * sn
            rep = NH // NKV
            k = jnp.repeat(k, rep, axis=1)
            v = jnp.repeat(v, rep, axis=1)
            scores = jnp.einsum('bhqd,bhkd->bhqk', q, k) / jnp.sqrt(jnp.asarray(HD, x.dtype))
            scores = scores + causal_bias
            attn = jax.nn.softmax(scores, axis=-1)
            out = jnp.einsum('bhqk,bhkd->bhqd', attn, v)
            out = out.transpose(0, 2, 1, 3).reshape(b, s, NH * HD)
            return out @ wo

        def _moe(x, wr, wg, wu, wd):
            logits = x @ wr
            probs = jax.nn.softmax(logits, axis=-1)
            topv, topi = jax.lax.top_k(probs, K)
            topv = topv / jnp.sum(topv, axis=-1, keepdims=True)
            comb = jnp.sum(jax.nn.one_hot(topi, E, dtype=x.dtype) * topv[..., None], axis=-2)
            out = jnp.zeros_like(x)
            for e in range(E):
                h = jax.nn.silu(x @ wg[e]) * (x @ wu[e])
                out = out + comb[..., e:e + 1] * (h @ wd[e])
            return out
        s = hidden_states.shape[1]
        cos, sin = _rope_cos_sin(s, HD, THETA)
        causal_bias = jnp.where(jnp.tril(jnp.ones((s, s), bool))[None, None], 0.0, -1000000000.0).astype(hidden_states.dtype)
        x = hidden_states
        for l in range(L):
            res = x
            h = _rms(x, ln1_w[l])
            h = _attention(h, wq[l], wk[l], wv[l], wo[l], cos, sin, causal_bias)
            x = jnp.clip(res + h, -100.0, 100.0)
            res = x
            h = _rms(x, ln2_w[l])
            h = _moe(h, wr[l], wg[l], wu[l], wd[l])
            x = jnp.clip(res + h, -100.0, 100.0)
        return x
    x = L0_attn_inputs
    x = x + _layernorm(_L0_attn_ref(_layernorm(x, axis=-1), L0_attn_ln1_g, L0_attn_ln1_b, L0_attn_Wq, L0_attn_Wk, L0_attn_Wv, L0_attn_Whq, L0_attn_Whk, L0_attn_Wo, L0_attn_ln2_g, L0_attn_ln2_b, L0_attn_W1, L0_attn_b1, L0_attn_W2, L0_attn_b2), axis=-1)
    x = x + _layernorm(_L0_ffn_ref(_layernorm(x, axis=-1), L0_ffn_ln1_w, L0_ffn_ln2_w, L0_ffn_wq, L0_ffn_wk, L0_ffn_wv, L0_ffn_wo, L0_ffn_wr, L0_ffn_wg, L0_ffn_wu, L0_ffn_wd), axis=-1)
    return x

_drawn_inputs = setup_inputs


def setup_inputs(seed=0):
    import zlib

    import numpy as np

    out = dict(_drawn_inputs(seed))
    spreads = {'L0_attn_ln1_g': (1.0, 0.6),
     'L0_attn_ln1_b': (0.0, 0.8),
     'L0_attn_ln2_g': (1.0, 0.6),
     'L0_attn_ln2_b': (0.0, 0.8),
     'L0_attn_b1': (0.0, 0.522),
     'L0_attn_b2': (0.0, 0.1),
     'L0_ffn_ln1_w': (1.0, 0.6),
     'L0_ffn_ln2_w': (1.0, 0.6)}
    factors = {'L0_attn_Wq': 8.0,
     'L0_attn_Wk': 8.0,
     'L0_attn_Wv': 8.0,
     'L0_attn_Whq': 8.0,
     'L0_attn_Whk': 8.0,
     'L0_attn_Wo': 8.0,
     'L0_ffn_wq': 8.0,
     'L0_ffn_wk': 8.0,
     'L0_ffn_wv': 5.193,
     'L0_ffn_wo': 5.199,
     'L0_ffn_wr': 8.0,
     'L0_ffn_wg': 8.0,
     'L0_ffn_wu': 8.0,
     'L0_ffn_wd': 8.0}
    for name, (base, spread) in spreads.items():
        noise = np.random.default_rng([zlib.crc32(name.encode()), seed]).standard_normal(out[name].shape)
        drawn = base * np.exp(spread * noise) if base else spread * noise
        out[name] = jnp.asarray(drawn.astype(out[name].dtype))
    for name, factor in factors.items():
        out[name] = (out[name] * factor).astype(out[name].dtype)
    return out
```

```python
from contextlib import ExitStack

import numpy as np

import concourse.bass as bass
from concourse import mybir

F32 = mybir.dt.float32
F32R = mybir.dt.float32r
BF16 = mybir.dt.bfloat16
ALU = mybir.AluOpType
ACT = mybir.ActivationFunctionType
AX = mybir.AxisListType

P = 128
B, SEQ, D = 2, 1024, 128
TPB = SEQ // P
NT = B * TPB
H1, F1, NB, MLP = 16, 8, 32, 512
HG = 4
NG1 = H1 // HG
MCH = MLP // P
CLUSTER = 0.1
L, NH, NKV, HD, FF, E = 4, 16, 4, 64, 256, 8
GQ = NH // NKV
CG = GQ * HD + 2 * HD
WE = 2 * FF + 2 * D
TRI = [t * (t + 1) // 2 for t in range(TPB + 1)]
NEG = -1.0e9


def ds(i, n=1):
    return bass.ds(i, n)


class Norm:

    def __init__(self, sem, name, kind, eps, src, out, turned=None):
        self.square = None
        self.kind, self.eps, self.src, self.out, self.turned = kind, eps, src, out, turned
        self.vec, self.act, self.ten = sem(name + "_vec"), sem(name + "_act"), sem(name + "_ten")
        self.centred = 3 if kind == "ln" else 0
        self.var_ready = self.centred + 2
        self.out_ready = self.centred + 4
        self.steps_vec = self.out_ready + (0 if turned is None else (8 if turned == "split" else 4))
        self.steps_act = 2 + (4 if turned == "split" else 0)
        self.steps_ten = 4 if turned else 0

    def full(self, c):
        return self.out_ready + ([1, 2, 4, 6][c] if self.turned == "split" else c + 1)


def program(nc, x_in, ln1_g, ln1_b, Wq, Wk, Wv, Whq, Whk, Wo, ln2_g, ln2_b, W1, b1, W2, b2,
            f_ln1, f_ln2, wq, wk, wv, wo, wr, wg, wu, wd, cos_in, sin_in, out, debug=None):
    with ExitStack() as ctx:
        def sem(name):
            return ctx.enter_context(nc.semaphore(name))

        def sb(name, shape, dt=F32, where=ctx):
            return where.enter_context(nc.sbuf_tensor(name, shape, dt))

        psS = ctx.enter_context(nc.psum_tensor("psS", [P, 4, 512], F32))
        psO = [ctx.enter_context(nc.psum_tensor(f"psO{i}", [P, 512], F32)) for i in range(2)]
        psM = ctx.enter_context(nc.psum_tensor("psM", [P, 2, 512], F32))

        outer = sb("outer", [P, NT, D])
        inner = sb("inner", [P, NT, D])
        normed = sb("normed", [P, NT, D])
        tot = sb("tot", [P, NT])
        mean = sb("mean", [P, NT])
        vsum = sb("vsum", [P, NT])
        veps = sb("veps", [P, NT])
        std = sb("std", [P, NT])
        rstd = sb("rstd", [P, NT])
        ident = sb("ident", [P, P])
        identb = sb("identb", [P, P], BF16)
        blk = sb("blk", [TPB, TPB, P])
        xw = sb("xw", [P, 2, 512])
        gcol = sb("gcol", [P, 4])
        fcol = sb("fcol", [P, 2 * L])

        s_x = sem("x_loaded")
        s_const = sem("constants_made")
        s_w1 = sem("first_weights_loaded")
        s_out = sem("out_stored")

        n0 = Norm(sem, "n0", "ln", 1e-5, outer, inner)
        n1 = Norm(sem, "n1", "ln", 1e-6, inner, normed, "whole")
        n2 = Norm(sem, "n2", "ln", 1e-6, inner, normed, "whole")
        n3 = Norm(sem, "n3", "ln", 1e-5, inner, normed)
        n4 = Norm(sem, "n4", "ln", 1e-5, outer, inner)
        n5 = Norm(sem, "n5", "rms", 1e-5, inner, normed, "split")
        n6 = Norm(sem, "n6", "rms", 1e-5, inner, normed, "split")
        n7 = Norm(sem, "n7", "ln", 1e-5, inner, normed)

        first = ExitStack()
        xT = sb("xT", [P, NT * P], where=first)
        w_qkv = sb("w_qkv", [P, 3, P], where=first)
        bd = sb("bd", [P, 2, H1 * NB], where=first)
        wo1 = sb("wo1", [P, D], where=first)
        w_up = sb("w_up", [P, MLP], where=first)
        w_dn = sb("w_dn", [P, MCH, D], where=first)
        b1c = sb("b1c", [P, MCH], where=first)
        b2r = sb("b2r", [P, D], where=first)
        qkv = sb("qkv", [P, NT, 3 * P], where=first)
        turned = sb("turned", [P, NT * P], where=first)
        qb = sb("qb", [P, NT, H1 * NB], where=first)
        kb = sb("kb", [P, NT, H1 * NB], where=first)
        smm = sb("smm", [P, 2, H1], where=first)
        sms = sb("sms", [P, 2, H1], where=first)
        smr = sb("smr", [P, 2, H1], where=first)
        tmq = sb("tmq", [P, HG, P], F32R, where=first)
        tmk = sb("tmk", [P, HG, P], F32R, where=first)
        qst = sb("qst", [P, HG, SEQ], F32R, where=first)
        kst = sb("kst", [P, HG, SEQ], F32R, where=first)
        v32 = sb("v32", [P, TPB, HG, 32], where=first)
        mx1 = sb("mx1", [P, HG, TPB], where=first)
        pr1 = sb("pr1", [P, 2, HG, 512], where=first)
        osb = xw
        rd1 = sb("rd1", [P, 4, HG], where=first)
        attn1 = normed
        relu1 = pr1
        square1 = pr1[:, 0, :, :].rearrange("p h n -> p (h n)").rearrange("p (t d) -> p t d", t=NT)
        first.close()

        second = ExitStack()
        xh = sb("xh", [P, NT * P], F32R, where=second)
        xl = sb("xl", [P, NT * P], F32R, where=second)
        wst = sb("wst", [P, NKV, CG], where=second)
        wah = sb("wah", [P, NKV, CG], F32R, where=second)
        wal = sb("wal", [P, NKV, CG], F32R, where=second)
        wos = sb("wos", [P, NKV, 2, D], where=second)
        cosT = sb("cosT", [P, TPB, HD], where=second)
        sinT = sb("sinT", [P, TPB, HD], where=second)
        maskq = sb("maskq", [P, P], BF16, where=second)
        maskk = sb("maskk", [P, P], BF16, where=second)
        ones64 = sb("ones64", [P, HD], where=second)
        qs2 = [sb(f"qs2_{b}", [P, TPB, GQ, P], F32R, where=second) for b in range(B)]
        ks1 = [sb(f"ks1_{b}", [P, SEQ], F32R, where=second) for b in range(B)]
        ks2 = [sb(f"ks2_{b}", [P, SEQ], F32R, where=second) for b in range(B)]
        vv = [sb(f"vv_{b}", [P, TPB, HD], where=second) for b in range(B)]
        mx2 = sb("mx2", [P, GQ], where=second)
        prob = sb("prob", [P, 4, 512], where=second)
        psum_k = sb("psum_k", [P, 2, 512], where=second)
        rden = sb("rden", [P, 256], where=second)
        att = sb("att", [P, 2, 256], where=second)
        wrs = sb("wrs", [P, E], where=second)
        wrh = sb("wrh", [P, E], F32R, where=second)
        wrl = sb("wrl", [P, E], F32R, where=second)
        comb = sb("comb", [P, NT, E], where=second)
        order = sb("order", [P, E], where=second)
        est = sb("est", [P, WE], where=second)
        eh = [sb(f"eh{i}", [P, WE], F32R, where=second) for i in range(2)]
        el = [sb(f"el{i}", [P, WE], F32R, where=second) for i in range(2)]
        attn_only = ExitStack()
        rope_a = sb("rope_a", [P, 5, HD], where=attn_only)
        rope_b = sb("rope_b", [P, 5, HD], where=attn_only)
        roped = sb("roped", [P, 5, HD], where=attn_only)
        tqh = sb("tqh", [P, GQ, 2, HD], F32R, where=attn_only)
        tql = sb("tql", [P, GQ, HD], F32R, where=attn_only)
        tkk = sb("tkk", [P, 2, HD], F32R, where=attn_only)
        qs1 = [sb(f"qs1_{b}", [P, TPB, GQ, P], F32R, where=attn_only) for b in range(B)]
        attn_only.close()
        expert_only = ExitStack()
        square2 = sb("square2", [P, NT, D], where=expert_only)[:, :, :]
        rt = [sb(f"rt{i}", [P, NT, E], where=expert_only) for i in range(6)]
        r1 = [sb(f"r1_{i}", [P, NT], where=expert_only) for i in range(4)]
        gate = sb("gate", [P, 2, 512], where=expert_only)
        hid = sb("hid", [P, 2, 512], where=expert_only)
        hidh = sb("hidh", [P, 2, 2, 512], F32R, where=expert_only)
        hidl = sb("hidl", [P, 2, 2, 512], F32R, where=expert_only)
        expert_only.close()
        second.close()
        for n in (n0, n1, n2, n3):
            n.square = square1
        for n in (n4, n5, n6, n7):
            n.square = square2

        s_qkv, s_qkv_sb = sem("qkv_in_psum"), sem("qkv_in_sbuf")
        s_turn, s_turn_sb = sem("turned_in_psum"), sem("turned_in_sbuf")
        s_lg, s_sma, s_sme, s_smb = sem("logits_in_psum"), sem("cluster_max_off"), sem("cluster_exp"), sem("cluster_normed")
        s_v32c, s_v32 = sem("v32_constants"), sem("v32_filled")
        s_tmc, s_tmh, s_tml = sem("stack1_constants"), sem("stack1_high"), sem("stack1_low")
        s_tt1, s_st, s_stv = sem("stacks1_turned"), sem("q_stack1_stored"), sem("k_stack1_stored")
        s_mm1, s_mr1, s_mt1, s_mw1 = sem("max1_scores"), sem("max1_taken"), sem("max1_turned"), sem("max1_rows_written")
        s_qk1, s_ex1, s_pv1 = sem("scores1"), sem("exp1"), sem("pv1")
        s_oc1, s_ot1, s_on1 = sem("out1_copied"), sem("out1_turned"), sem("out1_normed")
        s_a1t, s_a1s, s_wo1, s_wo1x = sem("attn1_turned"), sem("attn1_stored"), sem("wo1_in_psum"), sem("wo1_added")
        s_up1, s_re1, s_dn1, s_dx1 = sem("up1_in_psum"), sem("relu1"), sem("down1_in_psum"), sem("down1_added")
        s_r1, s_r2 = sem("outer1_updated"), sem("outer2_updated")

        s_cs2, s_cs1, s_c2l = sem("constants2_made"), sem("constants1_zeroed"), sem("constants2_loaded")
        s_aw, s_ew = sem("attention_weights_loaded"), sem("expert_weights_loaded")
        s_wsh, s_wsl = sem("attention_weights_high"), sem("attention_weights_low")
        s_pj, s_rp, s_hi = sem("qkv2_in_psum"), sem("rope_steps"), sem("stack2_high")
        s_tt, s_sa = sem("stacks2_turned"), sem("stacks2_stored")
        s_ms, s_mr, s_mt, s_mw = sem("max2_scores"), sem("max2_taken"), sem("max2_turned"), sem("max2_rows_written")
        s_qk, s_ex, s_su, s_pv = sem("scores2"), sem("exp2"), sem("probabilities_summed"), sem("pv2")
        s_dn, s_rd, s_at, s_wo, s_wx = (sem("denominator_in_psum"), sem("denominator_inverted"),
                                        sem("attention_normed"), sem("wo2_in_psum"), sem("wo2_added"))
        s_cl1, s_cl2 = sem("clipped_after_attention"), sem("clipped_after_experts")
        s_rl, s_rv, s_re = sem("router_logits_in_psum"), sem("router_steps"), sem("router_exp")
        s_eh, s_el = sem("expert_weights_high"), sem("expert_weights_low")
        s_gu, s_si, s_hf, s_hh, s_hl = (sem("gate_up_in_psum"), sem("silu"), sem("hidden_full"),
                                        sem("hidden_high"), sem("hidden_low"))
        s_yd, s_yx = sem("down2_in_psum"), sem("down2_added")
        N_ROUTE = 18

        def b3(ap, n):
            return ap.unsqueeze(2).broadcast_to([P, NT, n])

        def norm_vector(v, n, run=0, gain=None, bias=None, start=()):
            for s, value in start:
                v.wait_ge(s, value)
            base, k = run * n.steps_vec, 0
            abase, tbase = run * n.steps_act, run * n.steps_ten

            def done(ins):
                nonlocal k
                k += 1
                ins.then_inc(n.vec, 1)

            def own():
                v.wait_ge(n.vec, base + k)

            x = n.src
            if n.kind == "ln":
                done(nc.vector.tensor_reduce(tot[:, :], n.src[:, :, :], AX.X, ALU.add))
                own()
                done(nc.vector.tensor_scalar(mean[:, :], tot[:, :], 1.0 / D, None, ALU.mult))
                own()
                done(nc.vector.tensor_tensor(normed[:, :, :], n.src[:, :, :], b3(mean[:, :], D), ALU.subtract))
                x = normed
            v.wait_ge(n.act, abase + 1)
            done(nc.vector.tensor_reduce(vsum[:, :], n.square, AX.X, ALU.add))
            own()
            done(nc.vector.tensor_scalar(veps[:, :], vsum[:, :], 1.0 / D, n.eps, ALU.mult, ALU.add))
            v.wait_ge(n.act, abase + 2)
            done(nc.vector.reciprocal(rstd[:, :], std[:, :]))
            own()
            done(nc.vector.tensor_tensor(n.out[:, :, :], x[:, :, :], b3(rstd[:, :], D), ALU.mult))

            def whole(c, dst):
                v.wait_ge(n.ten, tbase + c + 1)
                if bias is None:
                    done(nc.vector.tensor_scalar(dst, psM[:, c % 2, :], gain, None, ALU.mult))
                else:
                    done(nc.vector.tensor_scalar(dst, psM[:, c % 2, :], gain, bias, ALU.mult, ALU.add))

            def low(c):
                v.wait_ge(n.act, abase + 3 + c)
                done(nc.vector.tensor_tensor(xl[:, c * 512:(c + 1) * 512], xw[:, c % 2, :],
                                             xh[:, c * 512:(c + 1) * 512], ALU.subtract))

            if n.turned == "whole":
                for c in range(4):
                    whole(c, xT[:, c * 512:(c + 1) * 512])
            if n.turned == "split":
                whole(0, xw[:, 0, :])
                whole(1, xw[:, 1, :])
                for c in range(4):
                    low(c)
                    if c < 2:
                        own()
                        whole(c + 2, xw[:, c % 2, :])

        def norm_scalar(a, n, run=0, start=()):
            base, vbase = run * n.steps_act, run * n.steps_vec
            x = n.src
            if n.kind == "ln":
                a.wait_ge(n.vec, vbase + n.centred)
                x = normed
            for s, value in start:
                a.wait_ge(s, value)
            nc.scalar.activation(n.square, x[:, :, :], ACT.Square).then_inc(n.act, 1)
            a.wait_ge(n.vec, vbase + n.var_ready)
            nc.scalar.activation(std[:, :], veps[:, :], ACT.Sqrt).then_inc(n.act, 1)
            if n.turned == "split":
                for c in range(4):
                    a.wait_ge(n.vec, vbase + n.full(c))
                    nc.scalar.activation(xh[:, c * 512:(c + 1) * 512], xw[:, c % 2, :],
                                         ACT.Copy).then_inc(n.act, 1)

        def norm_tensor(t, n, run=0):
            vbase = run * n.steps_vec
            t.wait_ge(n.vec, vbase + n.out_ready)
            for c in range(4):
                if c >= 2:
                    t.wait_ge(n.vec, vbase + n.full(c - 2))
                for i in range(4):
                    ins = nc.tensor.transpose(psM[:, c % 2, i * P:(i + 1) * P], normed[:, 4 * c + i, :], ident[:, :])
                ins.then_inc(n.ten, 1)

        block = ctx.enter_context(nc.Block())

        @block.sync
        def _(sp):
            sp.dma_start(outer[:, :, :], x_in.rearrange("b (t p) d -> p (b t) d", p=P)).then_inc(s_x, 16)
            for i, w in enumerate((Wq, Wk, Wv)):
                sp.dma_start(w_qkv[:, i, :], w.rearrange("d h f -> d (h f)")).then_inc(s_w1, 16)
            for i, c in enumerate((ln1_g, ln1_b, ln2_g, ln2_b)):
                sp.dma_start(gcol[:, i:i + 1], c.rearrange("(d a) -> d a", a=1)).then_inc(s_w1, 16)
            for l in range(L):
                sp.dma_start(fcol[:, l:l + 1], f_ln1[l].rearrange("(d a) -> d a", a=1)).then_inc(s_w1, 16)
                sp.dma_start(fcol[:, L + l:L + l + 1], f_ln2[l].rearrange("(d a) -> d a", a=1)).then_inc(s_w1, 16)
            sp.dma_start(wo1[:, :], Wo.rearrange("h f d -> (h f) d")).then_inc(s_w1, 16)
            sp.dma_start(w_up[:, :], W1).then_inc(s_w1, 16)
            sp.dma_start(w_dn[:, :, :], W2.rearrange("(c p) d -> p c d", p=P)).then_inc(s_w1, 16)
            for m in range(MCH):
                sp.dma_start(b1c[:, m:m + 1], b1[m * P:(m + 1) * P].rearrange("(p a) -> p a", a=1)).then_inc(s_w1, 16)
            sp.dma_start(b2r[:, :], b2.rearrange("(a d) -> a d", a=1).broadcast_to([P, D])).then_inc(s_w1, 16)
            sp.wait_ge(s_const, 1)
            for i, w in enumerate((Whq, Whk)):
                for h in range(H1):
                    sp.dma_start(bd[h * F1:(h + 1) * F1, i, h * NB:(h + 1) * NB], w[h]).then_inc(s_w1, 16)
            sp.wait_ge(s_r1, 1)
            if debug == 1:
                sp.dma_start(out.rearrange("b (t p) d -> p (b t) d", p=P), outer[:, :, :]).then_inc(s_out, 16)
                sp.wait_ge(s_out, 16)
                return
            sp.dma_start(cosT[:, :, :], cos_in.rearrange("(t p) f -> p t f", p=P)).then_inc(s_c2l, 16)
            sp.dma_start(sinT[:, :, :], sin_in.rearrange("(t p) f -> p t f", p=P)).then_inc(s_c2l, 16)
            with sp.Fori(0, L) as l:
                sp.wait_ge(s_cl1, l + 1)
                for g in range(NKV):
                    q0 = g * GQ * HD
                    sp.dma_start(wst[:, g, 0:GQ * HD], wq[ds(l), :, q0:q0 + GQ * HD].rearrange("a d n -> (a d) n")).then_inc(s_aw, 16)
                    sp.dma_start(wst[:, g, GQ * HD:(GQ + 1) * HD], wk[ds(l), :, g * HD:(g + 1) * HD].rearrange("a d n -> (a d) n")).then_inc(s_aw, 16)
                    sp.dma_start(wst[:, g, (GQ + 1) * HD:CG], wv[ds(l), :, g * HD:(g + 1) * HD].rearrange("a d n -> (a d) n")).then_inc(s_aw, 16)
                    for q in range(2):
                        for i in range(2):
                            r0 = q0 + (2 * q + i) * HD
                            sp.dma_start(wos[q * HD:(q + 1) * HD, g, i, :], wo[ds(l), r0:r0 + HD, :].rearrange("a f d -> (a f) d")).then_inc(s_aw, 16)
                sp.dma_start(wrs[:, :], wr[ds(l), :, :].rearrange("a d e -> (a d) e")).then_inc(s_aw, 16)
                with sp.Fori(0, E) as e:
                    sp.wait_ge(s_el, l * E + e + 1)
                    sp.dma_start(est[:, 0:FF], wg[ds(l), ds(e), :, :].rearrange("a e d n -> (a e d) n")).then_inc(s_ew, 16)
                    sp.dma_start(est[:, FF:2 * FF], wu[ds(l), ds(e), :, :].rearrange("a e d n -> (a e d) n")).then_inc(s_ew, 16)
                    for f in range(2):
                        sp.dma_start(est[:, 2 * FF + f * D:2 * FF + (f + 1) * D],
                                     wd[ds(l), ds(e), f * P:(f + 1) * P, :].rearrange("a e p d -> (a e p) d")).then_inc(s_ew, 16)
            sp.wait_ge(s_r2, 1)
            sp.dma_start(out.rearrange("b (t p) d -> p (b t) d", p=P), outer[:, :, :]).then_inc(s_out, 16)
            sp.wait_ge(s_out, 16)

        N_W1 = 16 * (3 + 4 + 2 * L + 4 + MCH + 2 * H1)
        N_AW = 16 * (7 * NKV + 1)

        @block.gpsimd
        def _(g_):
            g = nc.gpsimd
            g_.sem_inc(s_su, 4)
            g.memset(bd[:, :, :], 0.0).then_inc(s_const, 1)
            g.memset(ident[:, :], 0.0).then_inc(s_cs1, 1)
            g.memset(blk[:, :, :], 0.0).then_inc(s_cs1, 1)
            g_.wait_ge(s_cs1, 2)
            g.affine_select(out=ident[:, :], in_=ident[:, :], compare_op=ALU.not_equal, fill=1.0, base=0,
                            pattern=[[-1, P]], channel_multiplier=1).then_inc(s_const, 1)
            g.affine_select(out=blk[:, :, :], in_=blk[:, :, :], compare_op=ALU.not_equal, fill=-1.0, base=0,
                            pattern=[[-1, TPB], [0, P]], channel_multiplier=1).then_inc(s_const, 1)
            g.memset(v32[:, :, :, :], 0.0).then_inc(s_v32c, 1)
            g_.wait_ge(s_v32c, 1)
            g.memset(v32[:, :, :, F1:F1 + 1], 1.0).then_inc(s_v32c, 1)
            g.memset(tmq[:, :, 96:104].bitcast(F32), 0.0).then_inc(s_tmc, 1)
            g.memset(tmk[:, :, 96:104].bitcast(F32), 1.0).then_inc(s_tmc, 1)
            if debug == 1:
                return
            g_.wait_ge(s_r1, 1)
            g.memset(maskq[:, :], 0.0).then_inc(s_cs2, 1)
            g.memset(maskk[:, :], 0.0).then_inc(s_cs2, 1)
            g.memset(ones64[:, :], 1.0).then_inc(s_cs2, 1)
            g.memset(identb[:, :], 0.0).then_inc(s_cs2, 1)
            for b in range(B):
                g.memset(qs2[b][:, :, :, :].bitcast(F32), 0.0).then_inc(s_cs2, 1)
                g.memset(ks2[b][:, :].bitcast(F32), 0.0).then_inc(s_cs2, 1)
            for e in range(E):
                g.memset(order[:, e:e + 1], float(E - e)).then_inc(s_cs2, 1)
            g_.wait_ge(s_cs2, 4 + 2 * B + E)
            g.affine_select(out=identb[:, :], in_=identb[:, :], compare_op=ALU.not_equal, fill=1.0, base=0,
                            pattern=[[-1, P]], channel_multiplier=1).then_inc(s_cs2, 1)
            g.affine_select(out=maskq[:, :], in_=maskq[:, :], compare_op=ALU.is_ge, fill=NEG, base=0,
                            pattern=[[-1, P]], channel_multiplier=1).then_inc(s_cs2, 1)
            g.affine_select(out=maskk[:, :], in_=maskk[:, :], compare_op=ALU.is_ge, fill=NEG, base=0,
                            pattern=[[1, P]], channel_multiplier=-1).then_inc(s_cs2, 1)
            g_.wait_ge(s_cs2, 4 + 2 * B + E + 3)
            for b in range(B):
                g.memset(ks2[b][HD:HD + GQ, :].bitcast(F32), 1.0).then_inc(s_cs2, 1)
            with g_.Fori(0, L) as l:
                with g_.Fori(0, NKV) as gg:
                    for b in range(B):
                        it = (l * NKV + gg) * B + b
                        for t in range(1, TPB):
                            for kt in range(1, t + 1):
                                i = TRI[t] + kt
                                n = it * TRI[TPB] + i
                                g_.wait_ge(s_ex, n + 5)
                                if kt == 1:
                                    g_.wait_ge(s_dn, it * TPB + t + 1)
                                    before = prob[:, (i - 1) % 4, :]
                                else:
                                    g_.wait_ge(s_su, n + 4)
                                    before = psum_k[:, t % 2, :]
                                g.tensor_tensor(psum_k[:, t % 2, :], before, prob[:, i % 4, :],
                                                ALU.add).then_inc(s_su, 1 if kt > 1 else 2 + (t == 1))
                with g_.Fori(0, E // 2) as ep:
                    for ee in range(2):
                        le = (l * (E // 2) + ep) * 2 + ee
                        g_.wait_ge(s_eh, le + 1)
                        g.tensor_tensor(el[ee][:, :], est[:, :], eh[ee][:, :], ALU.subtract).then_inc(s_el, 1)

        @block.scalar
        def _(a):
            act = nc.scalar.activation
            a.sem_inc(s_ex1, 2)
            a.sem_inc(s_st, 1)
            a.sem_inc(s_ex, 4)
            a.sem_inc(s_si, 2)
            a.sem_inc(s_hh, 2)
            a.wait_ge(s_x, 16)
            norm_scalar(a, n0)
            norm_scalar(a, n1)
            for T in range(NT):
                a.wait_ge(s_qkv, T + 1)
                act(qkv[:, T, :], psS[:, T % 4, 0:3 * P], ACT.Copy).then_inc(s_qkv_sb, 1)
            for u in range(2 * NT):
                dst = (qb, kb)[u // NT][:, u % NT, :]
                a.wait_ge(s_sma, 2 * u + 2)
                act(dst, dst, ACT.Exp).then_inc(s_sme, 1)
            a.wait_ge(s_tmc, 2)
            a.wait_ge(s_smb, 3 * 2 * NT)
            with a.Fori(0, NG1) as g:
                for b in range(B):
                    it = g * B + b
                    for t in range(TPB):
                        u, T = it * TPB + t, b * TPB + t
                        qh = qb[:, T, ds(g * (HG * NB), HG * NB)].rearrange("p (h n) -> p h n", h=HG)
                        kh = kb[:, T, ds(g * (HG * NB), HG * NB)].rearrange("p (h n) -> p h n", h=HG)
                        qq = qkv[:, T, ds(g * (HG * F1), HG * F1)].rearrange("p (h f) -> p h f", h=HG)
                        kk = qkv[:, T, ds(g * (HG * F1) + P, HG * F1)].rearrange("p (h f) -> p h f", h=HG)
                        a.wait_ge(s_tt1, 2 * u + 1)
                        act(tmq[:, :, 0:64].rearrange("p h (r n) -> p h r n", r=2),
                            qh.unsqueeze(2).broadcast_to([P, HG, 2, NB]), ACT.Copy, scale=CLUSTER).then_inc(s_tmh, 1)
                        act(tmq[:, :, 104:120].rearrange("p h (r n) -> p h r n", r=2),
                            qq.unsqueeze(2).broadcast_to([P, HG, 2, F1]), ACT.Copy, scale=float(F1) ** -0.5).then_inc(s_tmh, 1)
                        act(tmk[:, :, 0:32], kh, ACT.Copy).then_inc(s_tmh, 1)
                        act(tmk[:, :, 64:96], kh, ACT.Copy).then_inc(s_tmh, 1)
                        act(tmk[:, :, 104:112], kk, ACT.Copy).then_inc(s_tmh, 1)
                        act(tmk[:, :, 120:128], kk, ACT.Copy).then_inc(s_tmh, 1)
                        a.wait_ge(s_tt1, 2 * u + 2)
                        act(qst[:, :, t * P:(t + 1) * P], psM[:, 0, :].rearrange("p (h n) -> p h n", h=HG),
                            ACT.Copy).then_inc(s_st, 1)
                    for c in range(2):
                        for kt in range(TPB):
                            for pair in range(2):
                                step = (it * 2 + c) * TPB + kt
                                a.wait_ge(s_qk1, 2 * step + pair + 1)
                                a.wait_ge(s_pv1, step + 1)
                                act(pr1[:, kt % 2, 2 * pair:2 * pair + 2, :], psS[:, 2 * pair:2 * pair + 2, :],
                                    ACT.Exp).then_inc(s_ex1, 1)
            norm_scalar(a, n2)
            for c in range(4):
                for m in range(MCH):
                    n = c * MCH + m
                    a.wait_ge(s_up1, n + 1)
                    if c >= 2:
                        a.wait_ge(s_dn1, c - 1)
                    act(relu1[:, c % 2, m, :], psS[:, n % 4, :], ACT.Relu, bias=b1c[:, m:m + 1]).then_inc(s_re1, 1)
            norm_scalar(a, n3)
            if debug == 1:
                return
            norm_scalar(a, n4)
            with a.Fori(0, L) as l:
                a.wait_ge(s_aw, N_AW * l + N_AW)
                act(wah[:, :, :], wst[:, :, :], ACT.Copy).then_inc(s_wsh, 1)
                act(wrh[:, :], wrs[:, :], ACT.Copy).then_inc(s_wsh, 1)
                norm_scalar(a, n5, l, start=((n4.vec, n4.out_ready), (s_cl2, l + 1)))
                with a.Fori(0, NKV) as g:
                    for b in range(B):
                        it = (l * NKV + g) * B + b
                        for t in range(TPB):
                            u = it * TPB + t
                            a.wait_ge(s_rp, 8 * u + 5)
                            act(tqh[:, :, :, :], roped[:, 0:GQ, :].unsqueeze(2).broadcast_to([P, GQ, 2, HD]),
                                ACT.Copy).then_inc(s_hi, 1)
                            act(tkk[:, 0, :], roped[:, GQ, :], ACT.Copy).then_inc(s_hi, 1)
                            a.wait_ge(s_tt, 3 * u + 1)
                            act(qs1[b][:, t, :, :], psM[:, 0, :].rearrange("p (h n) -> p h n", h=GQ),
                                ACT.Copy).then_inc(s_sa, 1)
                            a.wait_ge(s_tt, 3 * u + 3)
                            act(ks1[b][:, t * P:(t + 1) * P], psS[:, 3, 384:512], ACT.Copy).then_inc(s_sa, 1)
                            act(ks2[b][0:HD, t * P:(t + 1) * P], psS[0:HD, 3, 384:512], ACT.Copy).then_inc(s_sa, 1)
                        for t in range(TPB):
                            for kt in range(t + 1):
                                i = TRI[t] + kt
                                n = it * TRI[TPB] + i
                                a.wait_ge(s_qk, n + 1)
                                a.wait_ge(s_pv, n + 1)
                                a.wait_ge(s_su, n + 1)
                                act(prob[:, i % 4, :], psS[:, i % 3, :], ACT.Exp, scale=float(HD) ** -0.5).then_inc(s_ex, 1)
                norm_scalar(a, n6, l, start=((s_cl1, l + 2),))
                a.wait_ge(s_rv, N_ROUTE * l + 2)
                act(rt[0][:, :, :], rt[0][:, :, :], ACT.Exp).then_inc(s_re, 1)
                with a.Fori(0, E // 2) as ep:
                    for ee in range(2):
                        le = (l * (E // 2) + ep) * 2 + ee
                        a.wait_ge(s_ew, 64 * le + 64)
                        a.wait_ge(s_yd, 4 * le + 4)
                        act(eh[ee][:, :], est[:, :], ACT.Copy).then_inc(s_eh, 1)
                        for c in range(4):
                            j = le * 4 + c
                            for f in range(2):
                                n = j * 2 + f
                                a.wait_ge(s_gu, n + 1)
                                a.wait_ge(s_hf, n + 1)
                                act(gate[:, f, :], psS[:, f, :], ACT.Silu).then_inc(s_si, 1)
                            a.wait_ge(s_yd, j + 7)
                            for f in range(2):
                                a.wait_ge(s_hf, j * 2 + f + 3)
                                act(hidh[:, c % 2, f, :], hid[:, f, :], ACT.Copy).then_inc(s_hh, 1)
            norm_scalar(a, n7, 0)

        @block.tensor
        def _(t_):
            mm = nc.tensor.matmul
            t_.sem_inc(s_tt1, 1)
            t_.sem_inc(s_pv1, 2)
            t_.sem_inc(s_pv, 4)
            t_.sem_inc(s_dn, 2)
            t_.sem_inc(s_yd, 8)
            t_.wait_ge(s_const, 3)
            norm_tensor(t_, n1)
            t_.wait_ge(s_w1, N_W1)
            for T in range(NT):
                t_.wait_ge(n1.vec, n1.full(T // 4))
                if T >= 4:
                    t_.wait_ge(s_qkv_sb, T - 3)
                mm(psS[:, T % 4, 0:3 * P], xT[:, T * P:(T + 1) * P], w_qkv[:, :, :].rearrange("p a n -> p (a n)"),
                   start=True, stop=True).then_inc(s_qkv, 1)
            for side in range(2):
                for c in range(4):
                    n = side * 4 + c
                    t_.wait_ge(s_qkv_sb, 4 * c + 4)
                    if n >= 2:
                        t_.wait_ge(s_turn_sb, n - 1)
                    for i in range(4):
                        ins = nc.tensor.transpose(psM[:, n % 2, i * P:(i + 1) * P], qkv[:, 4 * c + i, side * P:(side + 1) * P], ident[:, :])
                    ins.then_inc(s_turn, 1)
                    if side == 0 or c < 0:
                        continue
                for T in range(NT):
                    u = side * NT + T
                    t_.wait_ge(s_turn_sb, side * 4 + T // 4 + 1)
                    if u >= 2:
                        t_.wait_ge(s_sma, 2 * (u - 2) + 2)
                    mm(psO[u % 2][:, :], turned[:, T * P:(T + 1) * P], bd[:, side, :], start=True, stop=True).then_inc(s_lg, 1)
            with t_.Fori(0, NG1) as g:
                for b in range(B):
                    it = g * B + b
                    t_.wait_ge(s_on1, 4 * it + 1)
                    for t in range(TPB):
                        u = it * TPB + t
                        t_.wait_ge(s_tml, 4 * u + 4)
                        t_.wait_ge(s_st, u + 1)
                        for h in range(HG):
                            ins = nc.tensor.transpose(psM[:, 0, h * P:(h + 1) * P], tmq[:, h, :].bitcast(F32), ident[:, :])
                        ins.then_inc(s_tt1, 1)
                        t_.wait_ge(s_stv, u + 1)
                        for h in range(HG):
                            ins = nc.tensor.transpose(psM[:, 1, h * P:(h + 1) * P], tmk[:, h, :].bitcast(F32), ident[:, :])
                        ins.then_inc(s_tt1, 1)
                    t_.wait_ge(s_st, it * TPB + TPB + 1)
                    t_.wait_ge(s_stv, it * TPB + TPB + 1)
                    for h in range(HG):
                        for t in range(TPB):
                            m = (it * HG + h) * TPB + t
                            t_.wait_ge(s_mr1, m + 1)
                            for kc in range(2):
                                dst = psM[:, kc, :] if t % 2 == 0 else psS[:, kc, :]
                                ins = mm(dst, qst[:, h, t * P:(t + 1) * P], kst[:, h, kc * 512:(kc + 1) * 512], start=True, stop=True)
                            ins.then_inc(s_mm1, 1)
                        t_.wait_ge(s_mr1, (it * HG + h) * TPB + TPB + 2)
                        t_.wait_ge(s_mw1, it * HG + h + 1)
                        nc.tensor.transpose(psO[h % 2][0:TPB, 0:P], mx1[:, h, :], ident[:, :]).then_inc(s_mt1, 1)
                    t_.wait_ge(s_mw1, it * HG + HG + 2)
                    t_.wait_ge(s_v32, it + 1)

                    def scores(c, kt):
                        for pair in range(2):
                            q = ((it * 2 + c) * TPB + kt) * 2 + pair
                            t_.wait_ge(s_ex1, q + 1)
                            for i in range(2):
                                h = 2 * pair + i
                                ins = mm(psS[:, h, :], kst[:, h, kt * P:(kt + 1) * P], qst[:, h, c * 512:(c + 1) * 512],
                                         start=True, stop=True)
                            ins.then_inc(s_qk1, 1)

                    def result(c):
                        o = it * 2 + c
                        t_.wait_ge(s_oc1, o + 3)
                        for i in range(4):
                            ins = nc.tensor.transpose(psM[:, c, i * P:(i + 1) * P], osb[:, c, i * P:(i + 1) * P], ident[:, :])
                        ins.then_inc(s_ot1, 1)

                    scores(0, 0)
                    for c in range(2):
                        for kt in range(TPB):
                            if c * TPB + kt + 1 < 2 * TPB:
                                scores(c + (kt + 1) // TPB, (kt + 1) % TPB)
                            step = (it * 2 + c) * TPB + kt
                            t_.wait_ge(s_ex1, 2 * step + 4)
                            if kt == 0:
                                t_.wait_ge(s_oc1, it * 2 + c + 1)
                            for h in range(HG):
                                ins = mm(psO[c][32 * h:32 * h + 32, :], v32[:, kt, h, :], pr1[:, kt % 2, h, :],
                                         start=(kt == 0), stop=(kt == TPB - 1))
                            ins.then_inc(s_pv1, 1)
                            if c == 1 and kt == 2:
                                result(0)
                    result(1)
            for c in range(4):
                t_.wait_ge(s_on1, 4 * NG1 * B + 1)
                if c >= 2:
                    t_.wait_ge(s_a1s, c - 1)
                for i in range(4):
                    ins = nc.tensor.transpose(psM[:, c % 2, i * P:(i + 1) * P], attn1[:, 4 * c + i, :], ident[:, :])
                ins.then_inc(s_a1t, 1)
            for c in range(4):
                t_.wait_ge(s_a1s, c + 1)
                for i in range(4):
                    T = 4 * c + i
                    ins = mm(psS[:, c, i * P:(i + 1) * P], turned[:, T * P:(T + 1) * P], wo1[:, :], start=True, stop=True)
                ins.then_inc(s_wo1, 1)
            norm_tensor(t_, n2)

            def up1(c):
                t_.wait_ge(n2.vec, n2.full(c))
                for m in range(MCH):
                    n = c * MCH + m
                    if n >= 4:
                        t_.wait_ge(s_re1, n - 3)
                    mm(psS[:, n % 4, :], w_up[:, m * P:(m + 1) * P], xT[:, c * 512:(c + 1) * 512],
                       start=True, stop=True).then_inc(s_up1, 1)

            up1(0)
            for c in range(4):
                if c < 3:
                    up1(c + 1)
                t_.wait_ge(s_re1, 4 * c + 4)
                if c >= 2:
                    t_.wait_ge(s_dx1, c - 1)
                for i in range(4):
                    for m in range(MCH):
                        ins = mm(psO[c % 2][:, i * P:(i + 1) * P], relu1[:, c % 2, m, i * P:(i + 1) * P], w_dn[:, m, :],
                                 start=(m == 0), stop=(m == MCH - 1))
                ins.then_inc(s_dn1, 1)
            if debug == 1:
                return

            t_.wait_ge(s_cs2, 4 + 2 * B + E + 3 + B)
            with t_.Fori(0, L) as l:
                norm_tensor(t_, n5, l)
                with t_.Fori(0, NKV) as g:
                    wh = wah[:, ds(g), :].rearrange("p a n -> p (a n)")
                    wl = wal[:, ds(g), :].rearrange("p a n -> p (a n)")
                    for b in range(B):
                        it = (l * NKV + g) * B + b

                        def project(t):
                            u, T = it * TPB + t, b * TPB + t
                            if t == 0:
                                t_.wait_ge(n5.vec, n5.steps_vec * l + n5.steps_vec)
                                t_.wait_ge(s_wsl, 2 * l + 2)
                            t_.wait_ge(s_mw, u + 1)
                            mm(psS[:, 3, 0:CG], xh[:, T * P:(T + 1) * P], wh, start=True, stop=False)
                            mm(psS[:, 3, 0:CG], xh[:, T * P:(T + 1) * P], wl, start=False, stop=False)
                            mm(psS[:, 3, 0:CG], xl[:, T * P:(T + 1) * P], wh, start=False, stop=True).then_inc(s_pj, 1)

                        def turn(t):
                            u = it * TPB + t
                            t_.wait_ge(s_rp, 8 * u + 7)
                            for h in range(GQ):
                                ins = nc.tensor.transpose(psM[:, 0, h * P:(h + 1) * P],
                                                          tqh[:, h, :, :].rearrange("p a n -> p (a n)").bitcast(F32), ident[:, :])
                            ins.then_inc(s_tt, 1)
                            for h in range(GQ):
                                ins = nc.tensor.transpose(psM[0:HD, 1, h * P:(h + 1) * P], tql[:, h, :].bitcast(F32), ident[:, :])
                            ins.then_inc(s_tt, 1)
                            nc.tensor.transpose(psS[:, 3, 384:512], tkk[:, :, :].rearrange("p a n -> p (a n)").bitcast(F32),
                                                ident[:, :]).then_inc(s_tt, 1)

                        def maxima(t):
                            u = it * TPB + t
                            keys = (t + 1) * P
                            t_.wait_ge(s_sa, 3 * u + 3)
                            t_.wait_ge(s_rp, 8 * u + 8)
                            for h in range(GQ):
                                if keys <= 512 and h >= 2:
                                    t_.wait_ge(s_mr, 4 * u + h - 1)
                                if keys > 512 and h >= 1:
                                    t_.wait_ge(s_mr, 4 * u + h)
                                q_t = qs1[b][:, t, h, :]
                                for k0 in range(0, keys, 512):
                                    bank = h % 2 if keys <= 512 else k0 // 512
                                    k1 = min(k0 + 512, keys)
                                    mm(psM[:, bank, 0:k1 - k0], q_t, ks1[b][:, k0:k1], start=True, stop=(k1 < keys))
                                ins = mm(psM[:, bank, k1 - k0 - P:k1 - k0], identb[:, :], maskq[:, :], start=False, stop=True)
                                ins.then_inc(s_ms, 1)
                            t_.wait_ge(s_mr, 4 * u + 4)
                            nc.tensor.transpose(psS[0:GQ, 3, 0:P], mx2[:, :], ident[:, :]).then_inc(s_mt, 1)

                        def scores2(t, kt):
                            i = TRI[t] + kt
                            dst = psS[:, i % 3, :]
                            t_.wait_ge(s_ex, it * TRI[TPB] + i + 2)
                            ks = slice(kt * P, (kt + 1) * P)
                            mm(dst, ks1[b][:, ks], qs1[b][:, t, :, :].rearrange("p h n -> p (h n)"), start=True, stop=False)
                            ins = mm(dst, ks2[b][:, ks], qs2[b][:, t, :, :].rearrange("p h n -> p (h n)"), start=False, stop=(kt < t))
                            if kt == t:
                                ins = mm(dst, identb[:, :], maskk[:, :].unsqueeze(1).broadcast_to([P, GQ, P]), start=False, stop=True)
                            ins.then_inc(s_qk, 1)

                        def values(t, kt):
                            i = TRI[t] + kt
                            n = it * TRI[TPB] + i
                            t_.wait_ge(s_ex, n + 5)
                            if kt == 0:
                                t_.wait_ge(s_wx, it * TPB + t + 1)
                            if t == 0:
                                denominator(0)
                            for q in range(2):
                                ins = mm(psO[t % 2][q * HD:(q + 1) * HD, 0:256], vv[b][:, kt, :], prob[:, i % 4, q * 256:(q + 1) * 256],
                                         start=(kt == 0), stop=(kt == t))
                            ins.then_inc(s_pv, 1)

                        def denominator(t):
                            total = prob[:, 0, :] if t == 0 else psum_k[:, t % 2, :]
                            if t > 0:
                                t_.wait_ge(s_su, it * TRI[TPB] + TRI[t] + t + 5)
                            for q in range(2):
                                ins = mm(psO[t % 2][q * HD:(q + 1) * HD, 256:512], ones64[:, :], total[:, q * 256:(q + 1) * 256],
                                         start=True, stop=True)
                            ins.then_inc(s_dn, 1)

                        def out_projection(t):
                            t_.wait_ge(s_at, it * TPB + t + 1)
                            for i in range(2):
                                ins = mm(psO[t % 2][:, 0:D], att[:, t % 2, i * P:(i + 1) * P],
                                         wos[:, ds(g), i, :].rearrange("p a d -> p (a d)"), start=(i == 0), stop=(i == 1))
                            ins.then_inc(s_wo, 1)

                        for t in range(TPB):
                            project(t)
                            turn(t)
                            maxima(t)
                        t_.wait_ge(s_mw, it * TPB + TPB + 1)
                        steps = [(t, kt) for t in range(TPB) for kt in range(t + 1)]
                        scores2(0, 0)
                        for i, (t, kt) in enumerate(steps):
                            if i + 1 < len(steps):
                                scores2(*steps[i + 1])
                            values(t, kt)
                            if kt == 0 and t > 1:
                                denominator(t - 1)
                            if kt == min(3, t) and t > 0:
                                out_projection(t - 1)
                        denominator(TPB - 1)
                        out_projection(TPB - 1)
                norm_tensor(t_, n6, l)
                t_.wait_ge(n6.vec, n6.steps_vec * l + n6.steps_vec)
                for T in range(NT):
                    ts = slice(T * P, (T + 1) * P)
                    o = psO[0][:, T * E:(T + 1) * E]
                    mm(o, xh[:, ts], wrh[:, :], start=True, stop=False)
                    mm(o, xh[:, ts], wrl[:, :], start=False, stop=False)
                    ins = mm(o, xl[:, ts], wrh[:, :], start=False, stop=True)
                ins.then_inc(s_rl, 1)
                with t_.Fori(0, E // 2) as ep:
                    for ee in range(2):
                        le = (l * (E // 2) + ep) * 2 + ee

                        def up2(c):
                            cs = slice(c * 512, (c + 1) * 512)
                            for f in range(2):
                                n = (le * 4 + c) * 2 + f
                                t_.wait_ge(s_si, n + 1)
                                t_.wait_ge(s_hf, n + 1)
                                for bank, w0 in ((f, f * P), (2 + f, FF + f * P)):
                                    mm(psS[:, bank, :], eh[ee][:, w0:w0 + P], xh[:, cs], start=True, stop=False)
                                    mm(psS[:, bank, :], eh[ee][:, w0:w0 + P], xl[:, cs], start=False, stop=False)
                                    ins = mm(psS[:, bank, :], el[ee][:, w0:w0 + P], xh[:, cs], start=False, stop=True)
                                ins.then_inc(s_gu, 1)

                        def down2(c):
                            j = le * 4 + c
                            t_.wait_ge(s_hl, 2 * j + 4)
                            t_.wait_ge(s_yx, j + 1)
                            for i in range(4):
                                o = psO[c % 2][:, i * D:(i + 1) * D]
                                hs = slice(i * P, (i + 1) * P)
                                for f in range(2):
                                    w0 = 2 * FF + f * D
                                    mm(o, hidh[:, c % 2, f, hs], eh[ee][:, w0:w0 + D], start=(f == 0), stop=False)
                                    mm(o, hidh[:, c % 2, f, hs], el[ee][:, w0:w0 + D], start=False, stop=False)
                                    ins = mm(o, hidl[:, c % 2, f, hs], eh[ee][:, w0:w0 + D], start=False, stop=(f == 1))
                            ins.then_inc(s_yd, 1)

                        t_.wait_ge(s_el, le + 2)
                        up2(0)
                        for c in range(4):
                            if c < 3:
                                up2(c + 1)
                            down2(c)

        @block.vector
        def _(v):
            vec = nc.vector
            v.sem_inc(s_on1, 1)
            v.sem_inc(s_stv, 1)
            v.sem_inc(s_mr1, 2)
            v.sem_inc(s_mw1, 2)
            v.sem_inc(s_oc1, 2)
            v.sem_inc(s_mw, 1)
            v.sem_inc(s_wx, 2)
            v.sem_inc(s_cl1, 1)
            v.sem_inc(s_cl2, 1)
            v.sem_inc(s_hf, 2)
            v.sem_inc(s_hl, 2)
            v.sem_inc(s_yx, 2)
            v.sem_inc(s_el, 1)
            v.wait_ge(s_x, 16)
            norm_vector(v, n0)
            v.wait_ge(s_w1, N_W1)
            norm_vector(v, n1, 0, gcol[:, 0:1], gcol[:, 1:2], start=((n0.vec, n0.steps_vec),))
            for n in range(8):
                v.wait_ge(s_turn, n + 1)
                if n == 4:
                    v.wait_ge(s_lg, NT)
                vec.tensor_copy(turned[:, (n % 4) * 512:(n % 4 + 1) * 512], psM[:, n % 2, :]).then_inc(s_turn_sb, 1)
                if n == 3:
                    softmax_from, softmax_to = 0, NT
                elif n == 7:
                    softmax_from, softmax_to = NT, 2 * NT
                else:
                    continue

                def off(u):
                    dst = (qb, kb)[u // NT][:, u % NT, :].rearrange("p (h n) -> p h n", h=H1)
                    lg = psO[u % 2][:, :].rearrange("p (h n) -> p h n", h=H1)
                    v.wait_ge(s_lg, u + 1)
                    vec.tensor_reduce(smm[:, u % 2, :], lg, AX.X, ALU.max).then_inc(s_sma, 1)
                    v.wait_ge(s_sma, 2 * u + 1)
                    vec.tensor_tensor(dst, lg, smm[:, u % 2, :].unsqueeze(2).broadcast_to([P, H1, NB]), ALU.subtract).then_inc(s_sma, 1)

                off(softmax_from)
                for u in range(softmax_from, softmax_to):
                    if u + 1 < softmax_to:
                        off(u + 1)
                    dst = (qb, kb)[u // NT][:, u % NT, :].rearrange("p (h n) -> p h n", h=H1)
                    v.wait_ge(s_sme, u + 1)
                    vec.tensor_reduce(sms[:, u % 2, :], dst, AX.X, ALU.add).then_inc(s_smb, 1)
                    v.wait_ge(s_smb, 3 * u + 1)
                    vec.reciprocal(smr[:, u % 2, :], sms[:, u % 2, :]).then_inc(s_smb, 1)
                    v.wait_ge(s_smb, 3 * u + 2)
                    vec.tensor_tensor(dst, dst, smr[:, u % 2, :].unsqueeze(2).broadcast_to([P, H1, NB]), ALU.mult).then_inc(s_smb, 1)
            v.wait_ge(s_smb, 3 * 2 * NT)
            v.wait_ge(s_v32c, 2)
            v.wait_ge(s_qkv_sb, NT)
            with v.Fori(0, NG1) as g:
                for b in range(B):
                    it = g * B + b
                    vec.tensor_copy(v32[:, :, :, 0:F1],
                                    qkv[:, b * TPB:(b + 1) * TPB, ds(g * (HG * F1) + 2 * P, HG * F1)]
                                    .rearrange("p t (h f) -> p t h f", h=HG)).then_inc(s_v32, 1)
                    for t in range(TPB):
                        u, T = it * TPB + t, b * TPB + t
                        qh = qb[:, T, ds(g * (HG * NB), HG * NB)].rearrange("p (h n) -> p h n", h=HG)
                        kh = kb[:, T, ds(g * (HG * NB), HG * NB)].rearrange("p (h n) -> p h n", h=HG)
                        qq = qkv[:, T, ds(g * (HG * F1), HG * F1)].rearrange("p (h f) -> p h f", h=HG)
                        kk = qkv[:, T, ds(g * (HG * F1) + P, HG * F1)].rearrange("p (h f) -> p h f", h=HG)
                        v.wait_ge(s_tmh, 6 * u + 6)
                        vec.scalar_tensor_tensor(out=tmq[:, :, 64:96], in0=qh, scalar=CLUSTER, in1=tmq[:, :, 0:32],
                                                 op0=ALU.mult, op1=ALU.subtract).then_inc(s_tml, 1)
                        vec.scalar_tensor_tensor(out=tmq[:, :, 120:128], in0=qq, scalar=float(F1) ** -0.5, in1=tmq[:, :, 104:112],
                                                 op0=ALU.mult, op1=ALU.subtract).then_inc(s_tml, 1)
                        vec.tensor_tensor(tmk[:, :, 32:64], kh, tmk[:, :, 0:32], ALU.subtract).then_inc(s_tml, 1)
                        vec.tensor_tensor(tmk[:, :, 112:120], kk, tmk[:, :, 104:112], ALU.subtract).then_inc(s_tml, 1)
                        v.wait_ge(s_tt1, 2 * u + 3)
                        vec.tensor_copy(kst[:, :, t * P:(t + 1) * P], psM[:, 1, :].rearrange("p (h n) -> p h n", h=HG)).then_inc(s_stv, 1)
                    for h in range(HG):
                        for t in range(TPB):
                            m = (it * HG + h) * TPB + t
                            v.wait_ge(s_mm1, m + 1)
                            src = psM[:, :, :] if t % 2 == 0 else psS[:, 0:2, :]
                            vec.tensor_reduce(mx1[:, h, t:t + 1], src, AX.XY, ALU.max).then_inc(s_mr1, 1)
                        v.wait_ge(s_mt1, it * HG + h + 1)
                        vec.tensor_tensor(qst[96:104, h, :].rearrange("p (t n) -> p t n", t=TPB),
                                          psO[h % 2][0:TPB, 0:P].unsqueeze(1).broadcast_to([TPB, TPB, P]),
                                          blk[0:TPB, :, :], ALU.mult).then_inc(s_mw1, 1)
                    for c in range(2):
                        o = it * 2 + c
                        v.wait_ge(s_pv1, o * TPB + TPB + 2)
                        vec.tensor_copy(osb[:, c, :], psO[c][:, :]).then_inc(s_oc1, 1)
                        v.wait_ge(s_ot1, o + 1)
                        tok = psM[:, c, :].rearrange("p (t h f) -> p t h f", t=4, h=HG)
                        vec.reciprocal(rd1[:, :, :], tok[:, :, :, F1]).then_inc(s_on1, 1)
                        v.wait_ge(s_on1, 2 * o + 2)
                        vec.tensor_tensor(attn1[:, b * TPB + 4 * c:b * TPB + 4 * c + 4, ds(g * (HG * F1), HG * F1)]
                                          .rearrange("p t (h f) -> p t h f", h=HG), tok[:, :, :, 0:F1],
                                          rd1[:, :, :].unsqueeze(3).broadcast_to([P, 4, HG, F1]), ALU.mult).then_inc(s_on1, 1)
            for c in range(4):
                v.wait_ge(s_a1t, c + 1)
                vec.tensor_copy(turned[:, c * 512:(c + 1) * 512], psM[:, c % 2, :]).then_inc(s_a1s, 1)
            for c in range(4):
                v.wait_ge(s_wo1, c + 1)
                r = inner[:, 4 * c:4 * c + 4, :].rearrange("p t d -> p (t d)")
                vec.tensor_tensor(r, r, psS[:, c, :], ALU.add).then_inc(s_wo1x, 1)
            norm_vector(v, n2, 0, gcol[:, 2:3], gcol[:, 3:4], start=((s_wo1x, 4),))
            for c in range(4):
                v.wait_ge(s_dn1, c + 1)
                r = inner[:, 4 * c:4 * c + 4, :].rearrange("p t d -> p (t d)")
                vec.tensor_tensor(r, r, psO[c % 2][:, :], ALU.add).then_inc(s_dx1, 1)
            v.wait_ge(s_dx1, 4)
            vec.tensor_tensor(inner[:, :, :], inner[:, :, :], b2r[:, :].unsqueeze(1).broadcast_to([P, NT, D]), ALU.add).then_inc(s_dx1, 1)
            norm_vector(v, n3, start=((s_dx1, 5),))
            v.wait_ge(n3.vec, n3.steps_vec)
            vec.tensor_tensor(outer[:, :, :], outer[:, :, :], normed[:, :, :], ALU.add).then_inc(s_r1, 1)
            if debug == 1:
                return
            norm_vector(v, n4, start=((s_r1, 1),))
            v.wait_ge(s_c2l, 32)
            v.wait_ge(s_cs2, 4 + 2 * B + E + 3 + B)
            with v.Fori(0, L) as l:
                v.wait_ge(s_wsh, 2 * l + 2)
                vec.tensor_tensor(wal[:, :, :], wst[:, :, :], wah[:, :, :], ALU.subtract).then_inc(s_wsl, 1)
                vec.tensor_tensor(wrl[:, :], wrs[:, :], wrh[:, :], ALU.subtract).then_inc(s_wsl, 1)
                norm_vector(v, n5, l, fcol[:, ds(l)])
                with v.Fori(0, NKV) as g:
                    for b in range(B):
                        it = (l * NKV + g) * B + b
                        for t in range(TPB):
                            u = it * TPB + t
                            v.wait_ge(s_pj, u + 1)
                            pr = psS[:, 3, 0:5 * HD].rearrange("p (h f) -> p h f", h=5)
                            c_t = cosT[:, t, :].unsqueeze(1).broadcast_to([P, 5, HD])
                            s_lo = sinT[:, t, 0:HD // 2].unsqueeze(1).broadcast_to([P, 5, HD // 2])
                            s_hi_ = sinT[:, t, HD // 2:HD].unsqueeze(1).broadcast_to([P, 5, HD // 2])
                            vec.tensor_tensor(rope_a[:, :, :], pr, c_t, ALU.mult).then_inc(s_rp, 1)
                            vec.tensor_tensor(rope_b[:, :, 0:HD // 2], pr[:, :, HD // 2:HD], s_lo, ALU.mult).then_inc(s_rp, 1)
                            vec.tensor_tensor(rope_b[:, :, HD // 2:HD], pr[:, :, 0:HD // 2], s_hi_, ALU.mult).then_inc(s_rp, 1)
                            vec.tensor_copy(vv[b][:, t, :], psS[:, 3, 5 * HD:6 * HD]).then_inc(s_rp, 1)
                            v.wait_ge(s_rp, 8 * u + 4)
                            vec.tensor_tensor(roped[:, :, :], rope_a[:, :, :], rope_b[:, :, :], ALU.add).then_inc(s_rp, 1)
                            v.wait_ge(s_hi, 2 * u + 2)
                            vec.tensor_tensor(tql[:, :, :], roped[:, 0:GQ, :], tqh[:, :, 0, :], ALU.subtract).then_inc(s_rp, 1)
                            vec.tensor_tensor(tkk[:, 1, :], roped[:, GQ, :], tkk[:, 0, :], ALU.subtract).then_inc(s_rp, 1)
                            v.wait_ge(s_tt, 3 * u + 2)
                            vec.tensor_copy(qs2[b][0:HD, t, :, :], psM[0:HD, 1, :].rearrange("p (h n) -> p h n", h=GQ)).then_inc(s_rp, 1)
                            for h in range(GQ):
                                v.wait_ge(s_ms, 4 * u + h + 1)
                                keys = (t + 1) * P
                                if keys <= 512:
                                    src = psM[:, h % 2, 0:keys]
                                else:
                                    src = psM[:, :, :].rearrange("p a n -> p (a n)")[:, 0:keys]
                                vec.tensor_reduce(mx2[:, h:h + 1], src, AX.X, ALU.max).then_inc(s_mr, 1)
                            v.wait_ge(s_mt, u + 1)
                            vec.tensor_tensor(qs2[b][HD:HD + GQ, t, :, :], psS[0:GQ, 3, 0:P].unsqueeze(1).broadcast_to([GQ, GQ, P]),
                                              blk[0:GQ, 0:GQ, :], ALU.mult).then_inc(s_mw, 1)
                        for t in range(TPB):
                            tau, T = it * TPB + t, b * TPB + t
                            v.wait_ge(s_dn, tau + 3)
                            if t == 0:
                                v.wait_ge(s_pv, it * TRI[TPB] + 5)
                            vec.reciprocal(rden[:, :], psO[t % 2][:, 256:512]).then_inc(s_rd, 1)
                            v.wait_ge(s_rd, tau + 1)
                            vec.tensor_tensor(att[:, t % 2, :], psO[t % 2][:, 0:256], rden[:, :], ALU.mult).then_inc(s_at, 1)
                            v.wait_ge(s_wo, tau + 1)
                            v.wait_ge(s_wx, tau + 2)
                            vec.tensor_tensor(inner[:, T, :], inner[:, T, :], psO[t % 2][:, 0:D], ALU.add).then_inc(s_wx, 1)
                v.wait_ge(s_wx, (l * NKV * B + NKV * B) * TPB + 2)
                vec.tensor_scalar(inner[:, :, :], inner[:, :, :], 100.0, -100.0, ALU.min, ALU.max).then_inc(s_cl1, 1)
                norm_vector(v, n6, l, fcol[:, ds(l + L)])

                k = 0

                def route(ins):
                    nonlocal k
                    k += 1
                    ins.then_inc(s_rv, 1)
                    if k < N_ROUTE:
                        v.wait_ge(s_rv, N_ROUTE * l + k)

                def over(x):
                    return x[:, :].unsqueeze(2).broadcast_to([P, NT, E])

                v.wait_ge(s_rl, l + 1)
                lg = psO[0][:, 0:NT * E].rearrange("p (t e) -> p t e", t=NT)
                first_of = order[:, :].unsqueeze(1).broadcast_to([P, NT, E])
                route(vec.tensor_reduce(r1[0][:, :], lg, AX.X, ALU.max))
                route(vec.tensor_tensor(rt[0][:, :, :], lg, over(r1[0]), ALU.subtract))
                v.wait_ge(s_re, l + 1)
                route(vec.tensor_reduce(r1[0][:, :], rt[0][:, :, :], AX.X, ALU.max))
                route(vec.tensor_tensor(rt[1][:, :, :], rt[0][:, :, :], over(r1[0]), ALU.is_equal))
                route(vec.tensor_tensor(rt[2][:, :, :], rt[1][:, :, :], first_of, ALU.mult))
                route(vec.tensor_reduce(r1[1][:, :], rt[2][:, :, :], AX.X, ALU.max))
                route(vec.tensor_tensor(rt[1][:, :, :], rt[2][:, :, :], over(r1[1]), ALU.is_equal))
                route(vec.scalar_tensor_tensor(out=rt[3][:, :, :], in0=rt[1][:, :, :], scalar=-2.0, in1=rt[0][:, :, :],
                                               op0=ALU.mult, op1=ALU.add))
                route(vec.tensor_reduce(r1[2][:, :], rt[3][:, :, :], AX.X, ALU.max))
                route(vec.tensor_tensor(rt[4][:, :, :], rt[3][:, :, :], over(r1[2]), ALU.is_equal))
                route(vec.tensor_tensor(rt[2][:, :, :], rt[4][:, :, :], first_of, ALU.mult))
                route(vec.tensor_reduce(r1[1][:, :], rt[2][:, :, :], AX.X, ALU.max))
                route(vec.tensor_tensor(rt[4][:, :, :], rt[2][:, :, :], over(r1[1]), ALU.is_equal))
                route(vec.tensor_tensor(rt[5][:, :, :], rt[1][:, :, :], rt[4][:, :, :], ALU.add))
                route(vec.tensor_tensor(rt[5][:, :, :], rt[5][:, :, :], rt[0][:, :, :], ALU.mult))
                route(vec.tensor_tensor(r1[3][:, :], r1[0][:, :], r1[2][:, :], ALU.add))
                route(vec.reciprocal(r1[3][:, :], r1[3][:, :]))
                route(vec.tensor_tensor(comb[:, :, :], rt[5][:, :, :], over(r1[3]), ALU.mult))
                assert k == N_ROUTE
                with v.Fori(0, E // 2) as ep:
                    for ee in range(2):
                        le = (l * (E // 2) + ep) * 2 + ee

                        def hidden(c):
                            j = le * 4 + c
                            for f in range(2):
                                n = j * 2 + f
                                v.wait_ge(s_si, n + 3)
                                v.wait_ge(s_hh, n + 1)
                                v.wait_ge(s_hl, n + 1)
                                vec.tensor_tensor(hid[:, f, :], gate[:, f, :], psS[:, 2 + f, :], ALU.mult).then_inc(s_hf, 1)
                            for f in range(2):
                                v.wait_ge(s_hh, j * 2 + f + 3)
                                vec.tensor_tensor(hidl[:, c % 2, f, :], hid[:, f, :], hidh[:, c % 2, f, :], ALU.subtract).then_inc(s_hl, 1)

                        def add(c):
                            j = le * 4 + c
                            v.wait_ge(s_rv, N_ROUTE * l + N_ROUTE)
                            v.wait_ge(s_yd, j + 9)
                            v.wait_ge(s_yx, j + 2)
                            for i in range(4):
                                T = 4 * c + i
                                ins = vec.scalar_tensor_tensor(
                                    out=inner[:, T, :], in0=psO[c % 2][:, i * D:(i + 1) * D],
                                    scalar=comb[:, T, ds(ep * 2 + ee)], in1=inner[:, T, :], op0=ALU.mult, op1=ALU.add)
                            ins.then_inc(s_yx, 1)

                        hidden(0)
                        for c in range(4):
                            if c < 3:
                                hidden(c + 1)
                            add(c)
                v.wait_ge(s_yx, (l * E + E) * 4 + 2)
                vec.tensor_scalar(inner[:, :, :], inner[:, :, :], 100.0, -100.0, ALU.min, ALU.max).then_inc(s_cl2, 1)
            norm_vector(v, n7, start=((s_cl2, L + 1),))
            v.wait_ge(n7.vec, n7.steps_vec)
            vec.tensor_tensor(outer[:, :, :], outer[:, :, :], normed[:, :, :], ALU.add).then_inc(s_r2, 1)


_INS = ["L0_attn_inputs", "L0_attn_ln1_g", "L0_attn_ln1_b", "L0_attn_Wq", "L0_attn_Wk", "L0_attn_Wv", "L0_attn_Whq",
        "L0_attn_Whk", "L0_attn_Wo", "L0_attn_ln2_g", "L0_attn_ln2_b", "L0_attn_W1", "L0_attn_b1", "L0_attn_W2",
        "L0_attn_b2", "L0_ffn_ln1_w", "L0_ffn_ln2_w", "L0_ffn_wq", "L0_ffn_wk", "L0_ffn_wv", "L0_ffn_wo", "L0_ffn_wr",
        "L0_ffn_wg", "L0_ffn_wu", "L0_ffn_wd"]


def rope_tables():
    inv = (1.0 / np.float32(10000.0) ** (np.arange(0, HD, 2, dtype=np.float32) / np.float32(HD))).astype(np.float32)
    f = np.arange(SEQ, dtype=np.float32)[:, None] * inv
    c, s = np.cos(f).astype(np.float32), np.sin(f).astype(np.float32)
    return np.concatenate([c, c], 1), np.concatenate([-s, s], 1)


def kernel(**inputs):
    import concourse.bacc as bacc
    from concourse.bass_utils import run_bass_kernel_spmd as run

    nc = bacc.Bacc("TRN2", target_bir_lowering=False, num_devices=1)
    arrays, args = {}, []
    cos, sin = rope_tables()
    for name, a in [(n, inputs[n]) for n in _INS] + [("rope_cos", cos), ("rope_sin", sin)]:
        a = np.ascontiguousarray(a)
        arrays[f"in_{name}"] = a
        args.append(nc.dram_tensor(f"in_{name}", a.shape, mybir.dt.from_np(a.dtype), kind="ExternalInput").ap())
    args.append(nc.dram_tensor("out_0", (B, SEQ, D), F32, kind="ExternalOutput").ap())
    program(nc, *args)
    r = run(nc, [arrays], core_ids=[0])
    return r.results[0]["out_0"]
```

```python
from contextlib import ExitStack

import numpy as np

import concourse.bass as bass
from concourse import mybir

F32 = mybir.dt.float32
F32R = mybir.dt.float32r
BF16 = mybir.dt.bfloat16
ALU = mybir.AluOpType
ACT = mybir.ActivationFunctionType
AX = mybir.AxisListType

P = 128
B, SEQ, D = 2, 1024, 128
TPB = SEQ // P
NT = B * TPB
H1, F1, NB, MLP = 16, 8, 32, 512
HG = 4
NG1 = H1 // HG
MCH = MLP // P
CLUSTER = 0.1
L, NH, NKV, HD, FF, E = 4, 16, 4, 64, 256, 8
GQ = NH // NKV
CG = GQ * HD + 2 * HD
WE = 2 * FF + 2 * D
TRI = [t * (t + 1) // 2 for t in range(TPB + 1)]
NEG = -1.0e9


def max_pieces(t):
    keys = (t + 1) * P
    return [(h, k0, min(k0 + 512, keys)) for h in range(GQ) for k0 in range(0, keys, 512)]


PIECES = [sum(len(max_pieces(i)) for i in range(t)) for t in range(TPB + 1)]
MAXED = [PIECES[t] + sum(1 for i in range(t) if len(max_pieces(i)) > GQ) for t in range(TPB + 1)]
STEPS = [(t, kt) for t in range(TPB) for kt in range(t + 1)]


def attention_order(attend, prepare):
    rank = {what: i for i, what in enumerate("PRNMHLDOSV")}
    handover = 130
    plan = {}

    def stage(engine, name, cost, *after):
        plan[engine, name] = (cost, [a for a in after if a])

    if attend:
        for i, (t, kt) in enumerate(STEPS):
            def back(engine, what, k):
                return (engine, (what, *STEPS[i - k])) if i >= k else None

            stage("tensor", ("S", t, kt), 430 + 210 * (kt == t), back("scalar", "S", 2), back("tensor", "S", 1))
            stage("scalar", ("S", t, kt), 490, ("tensor", ("S", t, kt)), back("tensor", "V", 4), back("gpsimd", "S", 4),
                  back("scalar", "S", 1))
            stage("gpsimd", ("S", t, kt), 1225 * (kt > 0), ("scalar", ("S", t, kt)), back("gpsimd", "S", 1),
                  ("tensor", ("D", t - 2)) if kt == 1 and t > 1 else None)
            stage("tensor", ("V", t, kt), 430, ("scalar", ("S", t, kt)), back("tensor", "V", 1),
                  ("vector", ("O", t - 2)) if kt == 0 and t > 1 else None, ("tensor", ("D", 0)) if i == 0 else None)
        for t in range(TPB):
            stage("tensor", ("D", t), 430, ("gpsimd", ("S", t, t)), ("tensor", ("V", t, t)) if t else None)
            stage("vector", ("D", t), 2000, ("tensor", ("D", t)), ("tensor", ("V", t, t)))
            stage("tensor", ("O", t), 430, ("vector", ("D", t)))
            stage("vector", ("O", t), 200, ("tensor", ("O", t)))
    if prepare:
        for t in range(TPB):
            pieces, last = max_pieces(t), t - 1

            def tile(engine, what, k, *more):
                return (engine, (what, t - k, *more)) if t >= k else None

            stage("tensor", ("P", t), 480, tile("tensor", "R", 1), tile("scalar", "R", 1))
            stage("vector", ("P", t), 1450, ("tensor", ("P", t)))
            stage("scalar", ("H", t), 720, ("vector", ("P", t)))
            stage("vector", ("L", t), 500, ("scalar", ("H", t)), tile("tensor", "N", 2))
            stage("tensor", ("R", t), 640, ("vector", ("L", t)), tile("vector", "M", 1, len(max_pieces(last)) - 1))
            stage("scalar", ("R", t), 740, ("tensor", ("R", t)))
            for m, (_, k0, k1) in enumerate(pieces):
                stage("tensor", ("M", t, m), 60 + (k1 - k0) / 2.4 + 60 * (k1 == (t + 1) * P), ("scalar", ("R", t)),
                      tile("vector", "M", 0, m - 2) if m > 1 else None, tile("tensor", "M", 0, m - 1) if m else None)
                stage("vector", ("M", t, m), 70 + 1.04 * (k1 - k0) + 150 * (m >= GQ and m == len(pieces) - 1), ("tensor", ("M", t, m)))
            stage("tensor", ("N", t), 430, ("vector", ("M", t, len(pieces) - 1)), tile("scalar", "N", 1))
            stage("scalar", ("N", t), 480, ("tensor", ("N", t)))

    end, free, order = {}, {}, {engine: [] for engine in ("tensor", "scalar", "vector", "gpsimd")}

    def start(key):
        return max([free.get(key[0], 0)] + [end[a] + handover * (a[0] != key[0]) for a in plan[key][1]])

    while len(end) < len(plan):
        ready = [key for key in plan if key not in end and all(a in end for a in plan[key][1])]
        key = min(ready, key=lambda key: (start(key), rank[key[1][0]]))
        end[key] = free[key[0]] = start(key) + plan[key][0]
        order[key[0]].append(key[1])
    return order


PREPARE = attention_order(False, True)
BOTH = attention_order(True, True)
ATTEND = attention_order(True, False)


def ds(i, n=1):
    return bass.ds(i, n)


class Norm:

    def __init__(self, sem, name, kind, eps, src, out, turned=None):
        self.square = None
        self.kind, self.eps, self.src, self.out, self.turned = kind, eps, src, out, turned
        self.vec, self.act, self.ten = sem(name + "_vec"), sem(name + "_act"), sem(name + "_ten")
        self.centred = 3 if kind == "ln" else 0
        self.var_ready = self.centred + 2
        self.out_ready = self.centred + 4
        self.steps_vec = self.out_ready + (0 if turned is None else (8 if turned == "split" else 4))
        self.steps_act = 2 + (4 if turned == "split" else 0)
        self.steps_ten = 4 if turned else 0

    def full(self, c):
        return self.out_ready + ([1, 2, 4, 6][c] if self.turned == "split" else c + 1)


def program(nc, x_in, ln1_g, ln1_b, Wq, Wk, Wv, Whq, Whk, Wo, ln2_g, ln2_b, W1, b1, W2, b2,
            f_ln1, f_ln2, wq, wk, wv, wo, wr, wg, wu, wd, cos_in, sin_in, out, debug=None):
    with ExitStack() as ctx:
        def sem(name):
            return ctx.enter_context(nc.semaphore(name))

        def sb(name, shape, dt=F32, where=ctx):
            return where.enter_context(nc.sbuf_tensor(name, shape, dt))

        psS = ctx.enter_context(nc.psum_tensor("psS", [P, 4, 512], F32))
        psO = [ctx.enter_context(nc.psum_tensor(f"psO{i}", [P, 512], F32)) for i in range(2)]
        psM = ctx.enter_context(nc.psum_tensor("psM", [P, 2, 512], F32))
        psU, psP = psS[:, 2, :], psS[:, 3, :]

        outer = sb("outer", [P, NT, D])
        inner = sb("inner", [P, NT, D])
        normed = sb("normed", [P, NT, D])
        tot = sb("tot", [P, NT])
        mean = sb("mean", [P, NT])
        vsum = sb("vsum", [P, NT])
        veps = sb("veps", [P, NT])
        std = sb("std", [P, NT])
        rstd = sb("rstd", [P, NT])
        ident = sb("ident", [P, P])
        identb = sb("identb", [P, P], BF16)
        blk = sb("blk", [TPB, TPB, P])
        xw = sb("xw", [P, 2, 512])
        gcol = sb("gcol", [P, 4])
        fcol = sb("fcol", [P, 2 * L])

        s_x = sem("x_loaded")
        s_const = sem("constants_made")
        s_w1 = sem("first_weights_loaded")
        s_out = sem("out_stored")

        n0 = Norm(sem, "n0", "ln", 1e-5, outer, inner)
        n1 = Norm(sem, "n1", "ln", 1e-6, inner, normed, "whole")
        n2 = Norm(sem, "n2", "ln", 1e-6, inner, normed, "whole")
        n3 = Norm(sem, "n3", "ln", 1e-5, inner, normed)
        n4 = Norm(sem, "n4", "ln", 1e-5, outer, inner)
        n5 = Norm(sem, "n5", "rms", 1e-5, inner, normed, "split")
        n6 = Norm(sem, "n6", "rms", 1e-5, inner, normed, "split")
        n7 = Norm(sem, "n7", "ln", 1e-5, inner, normed)

        first = ExitStack()
        xT = sb("xT", [P, NT * P], where=first)
        w_qkv = sb("w_qkv", [P, 3, P], where=first)
        bd = sb("bd", [P, 2, H1 * NB], where=first)
        wo1 = sb("wo1", [P, D], where=first)
        w_up = sb("w_up", [P, MLP], where=first)
        w_dn = sb("w_dn", [P, MCH, D], where=first)
        b1c = sb("b1c", [P, MCH], where=first)
        b2r = sb("b2r", [P, D], where=first)
        qkv = sb("qkv", [P, NT, 3 * P], where=first)
        turned = sb("turned", [P, NT * P], where=first)
        qb = sb("qb", [P, NT, H1 * NB], where=first)
        kb = sb("kb", [P, NT, H1 * NB], where=first)
        smm = sb("smm", [P, 2, H1], where=first)
        sms = sb("sms", [P, 2, H1], where=first)
        smr = sb("smr", [P, 2, H1], where=first)
        tmq = sb("tmq", [P, HG, P], F32R, where=first)
        tmk = sb("tmk", [P, HG, P], F32R, where=first)
        qst = sb("qst", [P, HG, SEQ], F32R, where=first)
        kst = sb("kst", [P, HG, SEQ], F32R, where=first)
        v32 = sb("v32", [P, TPB, HG, 32], where=first)
        mx1 = sb("mx1", [P, HG, TPB], where=first)
        pr1 = sb("pr1", [P, 2, HG, 512], where=first)
        osb = xw
        rd1 = sb("rd1", [P, 4, HG], where=first)
        attn1 = normed
        relu1 = pr1
        square1 = pr1[:, 0, :, :].rearrange("p h n -> p (h n)").rearrange("p (t d) -> p t d", t=NT)
        first.close()

        second = ExitStack()
        xh = sb("xh", [P, NT * P], F32R, where=second)
        xl = sb("xl", [P, NT * P], F32R, where=second)
        wst = sb("wst", [P, NKV, CG], where=second)
        wah = sb("wah", [P, NKV, CG], F32R, where=second)
        wal = sb("wal", [P, NKV, CG], F32R, where=second)
        wos = sb("wos", [P, NKV, 2, D], where=second)
        cosT = sb("cosT", [P, TPB, HD], where=second)
        sinT = sb("sinT", [P, TPB, HD], where=second)
        maskq = sb("maskq", [P, P], BF16, where=second)
        maskk = sb("maskk", [P, P], BF16, where=second)
        ones64 = sb("ones64", [P, HD], where=second)
        qs2 = [sb(f"qs2_{b}", [P, TPB, GQ, P], F32R, where=second) for b in range(B)]
        ks = [sb(f"ks_{b}", [P, 2, SEQ], F32R, where=second) for b in range(B)]
        tql = sb("tql", [P, 2, GQ, 2, HD], F32R, where=second)
        tkk = sb("tkk", [P, 4, HD], F32R, where=second)
        identr = sb("identr", [P, P], F32R, where=second)
        vv = [sb(f"vv_{b}", [P, TPB, HD], where=second) for b in range(B)]
        mxp = sb("mxp", [P, GQ, 2], where=second)
        prob = sb("prob", [P, 4, 512], where=second)
        psum_k = sb("psum_k", [P, 2, 512], where=second)
        rden = sb("rden", [P, 256], where=second)
        att = sb("att", [P, 2, 256], where=second)
        wrs = sb("wrs", [P, E], where=second)
        wrh = sb("wrh", [P, E], F32R, where=second)
        wrl = sb("wrl", [P, E], F32R, where=second)
        comb = sb("comb", [P, NT, E], where=second)
        order = sb("order", [P, E], where=second)
        est = sb("est", [P, WE], where=second)
        eh = [sb(f"eh{i}", [P, WE], F32R, where=second) for i in range(2)]
        el = [sb(f"el{i}", [P, WE], F32R, where=second) for i in range(2)]
        attn_only = ExitStack()
        rope_a = sb("rope_a", [P, 5, HD], where=attn_only)
        rope_b = sb("rope_b", [P, 5, HD], where=attn_only)
        roped = sb("roped", [P, 5, HD], where=attn_only)
        tqh = sb("tqh", [P, GQ, 2, HD], F32R, where=attn_only)
        qs1 = [sb(f"qs1_{b}", [P, TPB, GQ, P], F32R, where=attn_only) for b in range(B)]
        attn_only.close()
        expert_only = ExitStack()
        square2 = sb("square2", [P, NT, D], where=expert_only)[:, :, :]
        rt = [sb(f"rt{i}", [P, NT, E], where=expert_only) for i in range(6)]
        r1 = [sb(f"r1_{i}", [P, NT], where=expert_only) for i in range(4)]
        gate = sb("gate", [P, 2, 512], where=expert_only)
        hid = sb("hid", [P, 2, 512], where=expert_only)
        hidh = sb("hidh", [P, 2, 2, 512], F32R, where=expert_only)
        hidl = sb("hidl", [P, 2, 2, 512], F32R, where=expert_only)
        expert_only.close()
        second.close()
        for n in (n0, n1, n2, n3):
            n.square = square1
        for n in (n4, n5, n6, n7):
            n.square = square2

        s_qkv, s_qkv_sb = sem("qkv_in_psum"), sem("qkv_in_sbuf")
        s_turn, s_turn_sb = sem("turned_in_psum"), sem("turned_in_sbuf")
        s_lg, s_sma, s_sme, s_smb = sem("logits_in_psum"), sem("cluster_max_off"), sem("cluster_exp"), sem("cluster_normed")
        s_v32c, s_v32 = sem("v32_constants"), sem("v32_filled")
        s_tmc, s_tmh, s_tml = sem("stack1_constants"), sem("stack1_high"), sem("stack1_low")
        s_tt1, s_st, s_stv = sem("stacks1_turned"), sem("q_stack1_stored"), sem("k_stack1_stored")
        s_mm1, s_mr1, s_mt1, s_mw1 = sem("max1_scores"), sem("max1_taken"), sem("max1_turned"), sem("max1_rows_written")
        s_qk1, s_ex1, s_pv1 = sem("scores1"), sem("exp1"), sem("pv1")
        s_oc1, s_ot1, s_on1 = sem("out1_copied"), sem("out1_turned"), sem("out1_normed")
        s_a1t, s_a1s, s_wo1, s_wo1x = sem("attn1_turned"), sem("attn1_stored"), sem("wo1_in_psum"), sem("wo1_added")
        s_up1, s_re1, s_dn1, s_dx1 = sem("up1_in_psum"), sem("relu1"), sem("down1_in_psum"), sem("down1_added")
        s_r1, s_r2 = sem("outer1_updated"), sem("outer2_updated")

        s_cs2, s_cs1, s_c2l = sem("constants2_made"), sem("constants1_zeroed"), sem("constants2_loaded")
        s_aw, s_ew = sem("attention_weights_loaded"), sem("expert_weights_loaded")
        s_wsh, s_wsl = sem("attention_weights_high"), sem("attention_weights_low")
        s_pj, s_rp, s_hi = sem("qkv2_in_psum"), sem("rope_steps"), sem("stack2_high")
        s_tt, s_sa = sem("stacks2_turned"), sem("stacks2_stored")
        s_ms, s_mr, s_mt, s_mw = sem("max2_scores"), sem("max2_taken"), sem("max2_in_psum"), sem("q_low_stack_stored")
        s_qk, s_ex, s_su, s_pv = sem("scores2"), sem("exp2"), sem("probabilities_summed"), sem("pv2")
        s_dn, s_rd, s_at, s_wo, s_wx = (sem("denominator_in_psum"), sem("denominator_inverted"),
                                        sem("attention_normed"), sem("wo2_in_psum"), sem("wo2_added"))
        s_cl1, s_cl2 = sem("clipped_after_attention"), sem("clipped_after_experts")
        s_rl, s_rv, s_re = sem("router_logits_in_psum"), sem("router_steps"), sem("router_exp")
        s_eh, s_el = sem("expert_weights_high"), sem("expert_weights_low")
        s_gu, s_si, s_hf, s_hh, s_hl = (sem("gate_up_in_psum"), sem("silu"), sem("hidden_full"),
                                        sem("hidden_high"), sem("hidden_low"))
        s_yd, s_yx = sem("down2_in_psum"), sem("down2_added")
        N_ROUTE = 18
        N_CS2 = 7 + E + 4

        def b3(ap, n):
            return ap.unsqueeze(2).broadcast_to([P, NT, n])

        def norm_vector(v, n, run=0, gain=None, bias=None, start=()):
            for s, value in start:
                v.wait_ge(s, value)
            base, k = run * n.steps_vec, 0
            abase, tbase = run * n.steps_act, run * n.steps_ten

            def done(ins):
                nonlocal k
                k += 1
                ins.then_inc(n.vec, 1)

            def own():
                v.wait_ge(n.vec, base + k)

            x = n.src
            if n.kind == "ln":
                done(nc.vector.tensor_reduce(tot[:, :], n.src[:, :, :], AX.X, ALU.add))
                own()
                done(nc.vector.tensor_scalar(mean[:, :], tot[:, :], 1.0 / D, None, ALU.mult))
                own()
                done(nc.vector.tensor_tensor(normed[:, :, :], n.src[:, :, :], b3(mean[:, :], D), ALU.subtract))
                x = normed
            v.wait_ge(n.act, abase + 1)
            done(nc.vector.tensor_reduce(vsum[:, :], n.square, AX.X, ALU.add))
            own()
            done(nc.vector.tensor_scalar(veps[:, :], vsum[:, :], 1.0 / D, n.eps, ALU.mult, ALU.add))
            v.wait_ge(n.act, abase + 2)
            done(nc.vector.reciprocal(rstd[:, :], std[:, :]))
            own()
            done(nc.vector.tensor_tensor(n.out[:, :, :], x[:, :, :], b3(rstd[:, :], D), ALU.mult))

            def whole(c, dst):
                v.wait_ge(n.ten, tbase + c + 1)
                if bias is None:
                    done(nc.vector.tensor_scalar(dst, psM[:, c % 2, :], gain, None, ALU.mult))
                else:
                    done(nc.vector.tensor_scalar(dst, psM[:, c % 2, :], gain, bias, ALU.mult, ALU.add))

            def low(c):
                v.wait_ge(n.act, abase + 3 + c)
                done(nc.vector.tensor_tensor(xl[:, c * 512:(c + 1) * 512], xw[:, c % 2, :],
                                             xh[:, c * 512:(c + 1) * 512], ALU.subtract))

            if n.turned == "whole":
                for c in range(4):
                    whole(c, xT[:, c * 512:(c + 1) * 512])
            if n.turned == "split":
                whole(0, xw[:, 0, :])
                whole(1, xw[:, 1, :])
                for c in range(4):
                    low(c)
                    if c < 2:
                        own()
                        whole(c + 2, xw[:, c % 2, :])

        def norm_scalar(a, n, run=0, start=()):
            base, vbase = run * n.steps_act, run * n.steps_vec
            x = n.src
            if n.kind == "ln":
                a.wait_ge(n.vec, vbase + n.centred)
                x = normed
            for s, value in start:
                a.wait_ge(s, value)
            nc.scalar.activation(n.square, x[:, :, :], ACT.Square).then_inc(n.act, 1)
            a.wait_ge(n.vec, vbase + n.var_ready)
            nc.scalar.activation(std[:, :], veps[:, :], ACT.Sqrt).then_inc(n.act, 1)
            if n.turned == "split":
                for c in range(4):
                    a.wait_ge(n.vec, vbase + n.full(c))
                    nc.scalar.activation(xh[:, c * 512:(c + 1) * 512], xw[:, c % 2, :],
                                         ACT.Copy).then_inc(n.act, 1)

        def norm_tensor(t, n, run=0):
            vbase = run * n.steps_vec
            t.wait_ge(n.vec, vbase + n.out_ready)
            for c in range(4):
                if c >= 2:
                    t.wait_ge(n.vec, vbase + n.full(c - 2))
                for i in range(4):
                    ins = nc.tensor.transpose(psM[:, c % 2, i * P:(i + 1) * P], normed[:, 4 * c + i, :], ident[:, :])
                ins.then_inc(n.ten, 1)

        block = ctx.enter_context(nc.Block())

        @block.sync
        def _(sp):
            sp.dma_start(outer[:, :, :], x_in.rearrange("b (t p) d -> p (b t) d", p=P)).then_inc(s_x, 16)
            for i, w in enumerate((Wq, Wk, Wv)):
                sp.dma_start(w_qkv[:, i, :], w.rearrange("d h f -> d (h f)")).then_inc(s_w1, 16)
            for i, c in enumerate((ln1_g, ln1_b, ln2_g, ln2_b)):
                sp.dma_start(gcol[:, i:i + 1], c.rearrange("(d a) -> d a", a=1)).then_inc(s_w1, 16)
            for l in range(L):
                sp.dma_start(fcol[:, l:l + 1], f_ln1[l].rearrange("(d a) -> d a", a=1)).then_inc(s_w1, 16)
                sp.dma_start(fcol[:, L + l:L + l + 1], f_ln2[l].rearrange("(d a) -> d a", a=1)).then_inc(s_w1, 16)
            sp.dma_start(wo1[:, :], Wo.rearrange("h f d -> (h f) d")).then_inc(s_w1, 16)
            sp.dma_start(w_up[:, :], W1).then_inc(s_w1, 16)
            sp.dma_start(w_dn[:, :, :], W2.rearrange("(c p) d -> p c d", p=P)).then_inc(s_w1, 16)
            for m in range(MCH):
                sp.dma_start(b1c[:, m:m + 1], b1[m * P:(m + 1) * P].rearrange("(p a) -> p a", a=1)).then_inc(s_w1, 16)
            sp.dma_start(b2r[:, :], b2.rearrange("(a d) -> a d", a=1).broadcast_to([P, D])).then_inc(s_w1, 16)
            sp.wait_ge(s_const, 1)
            for i, w in enumerate((Whq, Whk)):
                for h in range(H1):
                    sp.dma_start(bd[h * F1:(h + 1) * F1, i, h * NB:(h + 1) * NB], w[h]).then_inc(s_w1, 16)
            sp.wait_ge(s_r1, 1)
            if debug == 1:
                sp.dma_start(out.rearrange("b (t p) d -> p (b t) d", p=P), outer[:, :, :]).then_inc(s_out, 16)
                sp.wait_ge(s_out, 16)
                return
            sp.dma_start(cosT[:, :, :], cos_in.rearrange("(t p) f -> p t f", p=P)).then_inc(s_c2l, 16)
            sp.dma_start(sinT[:, :, :], sin_in.rearrange("(t p) f -> p t f", p=P)).then_inc(s_c2l, 16)
            with sp.Fori(0, L) as l:
                sp.wait_ge(s_cl1, l + 1)
                for g in range(NKV):
                    q0 = g * GQ * HD
                    sp.dma_start(wst[:, g, 0:GQ * HD], wq[ds(l), :, q0:q0 + GQ * HD].rearrange("a d n -> (a d) n")).then_inc(s_aw, 16)
                    sp.dma_start(wst[:, g, GQ * HD:(GQ + 1) * HD], wk[ds(l), :, g * HD:(g + 1) * HD].rearrange("a d n -> (a d) n")).then_inc(s_aw, 16)
                    sp.dma_start(wst[:, g, (GQ + 1) * HD:CG], wv[ds(l), :, g * HD:(g + 1) * HD].rearrange("a d n -> (a d) n")).then_inc(s_aw, 16)
                    for q in range(2):
                        for i in range(2):
                            r0 = q0 + (2 * q + i) * HD
                            sp.dma_start(wos[q * HD:(q + 1) * HD, g, i, :], wo[ds(l), r0:r0 + HD, :].rearrange("a f d -> (a f) d")).then_inc(s_aw, 16)
                sp.dma_start(wrs[:, :], wr[ds(l), :, :].rearrange("a d e -> (a d) e")).then_inc(s_aw, 16)
                with sp.Fori(0, E) as e:
                    sp.wait_ge(s_el, l * E + e + 1)
                    sp.dma_start(est[:, 0:FF], wg[ds(l), ds(e), :, :].rearrange("a e d n -> (a e d) n")).then_inc(s_ew, 16)
                    sp.dma_start(est[:, FF:2 * FF], wu[ds(l), ds(e), :, :].rearrange("a e d n -> (a e d) n")).then_inc(s_ew, 16)
                    for f in range(2):
                        sp.dma_start(est[:, 2 * FF + f * D:2 * FF + (f + 1) * D],
                                     wd[ds(l), ds(e), f * P:(f + 1) * P, :].rearrange("a e p d -> (a e p) d")).then_inc(s_ew, 16)
            sp.wait_ge(s_r2, 1)
            sp.dma_start(out.rearrange("b (t p) d -> p (b t) d", p=P), outer[:, :, :]).then_inc(s_out, 16)
            sp.wait_ge(s_out, 16)

        N_W1 = 16 * (3 + 4 + 2 * L + 4 + MCH + 2 * H1)
        N_AW = 16 * (7 * NKV + 1)

        @block.gpsimd
        def _(g_):
            g = nc.gpsimd
            g_.sem_inc(s_su, 4)
            g.memset(bd[:, :, :], 0.0).then_inc(s_const, 1)
            g.memset(ident[:, :], 0.0).then_inc(s_cs1, 1)
            g.memset(blk[:, :, :], 0.0).then_inc(s_cs1, 1)
            g_.wait_ge(s_cs1, 2)
            g.affine_select(out=ident[:, :], in_=ident[:, :], compare_op=ALU.not_equal, fill=1.0, base=0,
                            pattern=[[-1, P]], channel_multiplier=1).then_inc(s_const, 1)
            g.affine_select(out=blk[:, :, :], in_=blk[:, :, :], compare_op=ALU.not_equal, fill=-1.0, base=0,
                            pattern=[[-1, TPB], [0, P]], channel_multiplier=1).then_inc(s_const, 1)
            g.memset(v32[:, :, :, :], 0.0).then_inc(s_v32c, 1)
            g_.wait_ge(s_v32c, 1)
            g.memset(v32[:, :, :, F1:F1 + 1], 1.0).then_inc(s_v32c, 1)
            g.memset(tmq[:, :, 96:104].bitcast(F32), 0.0).then_inc(s_tmc, 1)
            g.memset(tmk[:, :, 96:104].bitcast(F32), 1.0).then_inc(s_tmc, 1)
            if debug == 1:
                return
            g_.wait_ge(s_r1, 1)
            g.memset(maskq[:, :], 0.0).then_inc(s_cs2, 1)
            g.memset(maskk[:, :], 0.0).then_inc(s_cs2, 1)
            g.memset(ones64[:, :], 1.0).then_inc(s_cs2, 1)
            g.memset(identb[:, :], 0.0).then_inc(s_cs2, 1)
            g.memset(tql[:, :, :, :, :].bitcast(F32), 0.0).then_inc(s_cs2, 1)
            g.memset(tkk[:, :, :].bitcast(F32), 0.0).then_inc(s_cs2, 1)
            g.tensor_scalar(identr[:, :], ident[:, :], 1.0, 1.0, ALU.mult, ALU.mult).then_inc(s_cs2, 1)
            for e in range(E):
                g.memset(order[:, e:e + 1], float(E - e)).then_inc(s_cs2, 1)
            g_.wait_ge(s_cs2, 7 + E)
            g.affine_select(out=identb[:, :], in_=identb[:, :], compare_op=ALU.not_equal, fill=1.0, base=0,
                            pattern=[[-1, P]], channel_multiplier=1).then_inc(s_cs2, 1)
            g.affine_select(out=maskq[:, :], in_=maskq[:, :], compare_op=ALU.is_ge, fill=NEG, base=0,
                            pattern=[[-1, P]], channel_multiplier=1).then_inc(s_cs2, 1)
            g.affine_select(out=maskk[:, :], in_=maskk[:, :], compare_op=ALU.is_ge, fill=NEG, base=0,
                            pattern=[[1, P]], channel_multiplier=-1).then_inc(s_cs2, 1)
            g.memset(tkk[:, 2, 0:1].bitcast(F32), -1.0).then_inc(s_cs2, 1)
            with g_.Fori(0, L) as l:
                with g_.Fori(0, NKV) as gg:
                    for b in range(B):
                        it = (l * NKV + gg) * B + b
                        for t in range(1, TPB):
                            for kt in range(1, t + 1):
                                i = TRI[t] + kt
                                n = it * TRI[TPB] + i
                                g_.wait_ge(s_ex, n + 5)
                                if kt == 1:
                                    g_.wait_ge(s_dn, it * TPB + t + 1)
                                    before = prob[:, (i - 1) % 4, :]
                                else:
                                    g_.wait_ge(s_su, n + 4)
                                    before = psum_k[:, t % 2, :]
                                g.tensor_tensor(psum_k[:, t % 2, :], before, prob[:, i % 4, :],
                                                ALU.add).then_inc(s_su, 1 if kt > 1 else 2 + (t == 1))
                with g_.Fori(0, E // 2) as ep:
                    for ee in range(2):
                        le = (l * (E // 2) + ep) * 2 + ee
                        g_.wait_ge(s_eh, le + 1)
                        g.tensor_tensor(el[ee][:, :], est[:, :], eh[ee][:, :], ALU.subtract).then_inc(s_el, 1)

        @block.scalar
        def _(a):
            act = nc.scalar.activation
            a.sem_inc(s_ex1, 2)
            a.sem_inc(s_st, 1)
            a.sem_inc(s_ex, 4)
            a.sem_inc(s_sa, 1)
            a.sem_inc(s_mw, 1)
            a.sem_inc(s_si, 2)
            a.sem_inc(s_hh, 2)
            a.wait_ge(s_x, 16)
            norm_scalar(a, n0)
            norm_scalar(a, n1)
            for T in range(NT):
                a.wait_ge(s_qkv, T + 1)
                act(qkv[:, T, :], psS[:, T % 4, 0:3 * P], ACT.Copy).then_inc(s_qkv_sb, 1)
            for u in range(2 * NT):
                dst = (qb, kb)[u // NT][:, u % NT, :]
                a.wait_ge(s_sma, 2 * u + 2)
                act(dst, dst, ACT.Exp).then_inc(s_sme, 1)
            a.wait_ge(s_tmc, 2)
            a.wait_ge(s_smb, 3 * 2 * NT)
            with a.Fori(0, NG1) as g:
                for b in range(B):
                    it = g * B + b
                    for t in range(TPB):
                        u, T = it * TPB + t, b * TPB + t
                        qh = qb[:, T, ds(g * (HG * NB), HG * NB)].rearrange("p (h n) -> p h n", h=HG)
                        kh = kb[:, T, ds(g * (HG * NB), HG * NB)].rearrange("p (h n) -> p h n", h=HG)
                        qq = qkv[:, T, ds(g * (HG * F1), HG * F1)].rearrange("p (h f) -> p h f", h=HG)
                        kk = qkv[:, T, ds(g * (HG * F1) + P, HG * F1)].rearrange("p (h f) -> p h f", h=HG)
                        a.wait_ge(s_tt1, 2 * u + 1)
                        act(tmq[:, :, 0:64].rearrange("p h (r n) -> p h r n", r=2),
                            qh.unsqueeze(2).broadcast_to([P, HG, 2, NB]), ACT.Copy, scale=CLUSTER).then_inc(s_tmh, 1)
                        act(tmq[:, :, 104:120].rearrange("p h (r n) -> p h r n", r=2),
                            qq.unsqueeze(2).broadcast_to([P, HG, 2, F1]), ACT.Copy, scale=float(F1) ** -0.5).then_inc(s_tmh, 1)
                        act(tmk[:, :, 0:32], kh, ACT.Copy).then_inc(s_tmh, 1)
                        act(tmk[:, :, 64:96], kh, ACT.Copy).then_inc(s_tmh, 1)
                        act(tmk[:, :, 104:112], kk, ACT.Copy).then_inc(s_tmh, 1)
                        act(tmk[:, :, 120:128], kk, ACT.Copy).then_inc(s_tmh, 1)
                        a.wait_ge(s_tt1, 2 * u + 2)
                        act(qst[:, :, t * P:(t + 1) * P], psM[:, 0, :].rearrange("p (h n) -> p h n", h=HG),
                            ACT.Copy).then_inc(s_st, 1)
                    for c in range(2):
                        for kt in range(TPB):
                            for pair in range(2):
                                step = (it * 2 + c) * TPB + kt
                                a.wait_ge(s_qk1, 2 * step + pair + 1)
                                a.wait_ge(s_pv1, step + 1)
                                act(pr1[:, kt % 2, 2 * pair:2 * pair + 2, :], psS[:, 2 * pair:2 * pair + 2, :],
                                    ACT.Exp).then_inc(s_ex1, 1)
            norm_scalar(a, n2)
            for c in range(4):
                for m in range(MCH):
                    n = c * MCH + m
                    a.wait_ge(s_up1, n + 1)
                    if c >= 2:
                        a.wait_ge(s_dn1, c - 1)
                    act(relu1[:, c % 2, m, :], psS[:, n % 4, :], ACT.Relu, bias=b1c[:, m:m + 1]).then_inc(s_re1, 1)
            norm_scalar(a, n3)
            if debug == 1:
                return
            norm_scalar(a, n4)
            with a.Fori(0, L) as l:
                a.wait_ge(s_aw, N_AW * l + N_AW)
                act(wah[:, :, :], wst[:, :, :], ACT.Copy).then_inc(s_wsh, 1)
                act(wrh[:, :], wrs[:, :], ACT.Copy).then_inc(s_wsh, 1)
                norm_scalar(a, n5, l, start=((n4.vec, n4.out_ready), (s_cl2, l + 1)))

                def head(order, g, b, g_next, b_next):
                    it = (l * NKV + g) * B + b
                    it_next = (l * NKV + g_next) * B + b_next
                    for what, t, *more in order["scalar"]:
                        u = it_next * TPB + t
                        if what == "H":
                            a.wait_ge(s_rp, 7 * u + 5)
                            act(tqh[:, :, :, :], roped[:, 0:GQ, :].unsqueeze(2).broadcast_to([P, GQ, 2, HD]),
                                ACT.Copy).then_inc(s_hi, 1)
                            act(tkk[:, 0:4:3, :], roped[:, GQ:GQ + 1, :].broadcast_to([P, 2, HD]), ACT.Copy).then_inc(s_hi, 1)
                        elif what == "R":
                            a.wait_ge(s_tt, 2 * u + 1)
                            act(qs1[b_next][:, t, :, :], psM[:, 0, :].rearrange("p (h n) -> p h n", h=GQ),
                                ACT.Copy).then_inc(s_sa, 1)
                            a.wait_ge(s_tt, 2 * u + 2)
                            act(ks[b_next][:, :, t * P:(t + 1) * P], psP[:, 0:2 * P].rearrange("p (a n) -> p a n", a=2),
                                ACT.Copy).then_inc(s_sa, 1)
                        elif what == "N":
                            a.wait_ge(s_mt, u + 3)
                            act(qs2[b_next][:, t, :, :], psU.rearrange("p (h n) -> p h n", h=GQ), ACT.Copy).then_inc(s_mw, 1)
                        elif what == "S":
                            i = TRI[t] + more[0]
                            n = it * TRI[TPB] + i
                            a.wait_ge(s_qk, n + 1)
                            a.wait_ge(s_pv, n + 1)
                            a.wait_ge(s_su, n + 1)
                            act(prob[:, i % 4, :], psS[:, i % 2, :], ACT.Exp, scale=float(HD) ** -0.5).then_inc(s_ex, 1)

                head(PREPARE, 0, 0, 0, 0)
                with a.Fori(0, NKV - 1) as g:
                    head(BOTH, g, 0, g, 1)
                    head(BOTH, g, 1, g + 1, 0)
                head(BOTH, NKV - 1, 0, NKV - 1, 1)
                head(ATTEND, NKV - 1, 1, 0, 0)
                norm_scalar(a, n6, l, start=((s_cl1, l + 2),))
                a.wait_ge(s_rv, N_ROUTE * l + 2)
                act(rt[0][:, :, :], rt[0][:, :, :], ACT.Exp).then_inc(s_re, 1)
                with a.Fori(0, E // 2) as ep:
                    for ee in range(2):
                        le = (l * (E // 2) + ep) * 2 + ee
                        a.wait_ge(s_ew, 64 * le + 64)
                        a.wait_ge(s_yd, 4 * le + 4)
                        act(eh[ee][:, :], est[:, :], ACT.Copy).then_inc(s_eh, 1)
                        for c in range(4):
                            j = le * 4 + c
                            for f in range(2):
                                n = j * 2 + f
                                a.wait_ge(s_gu, n + 1)
                                a.wait_ge(s_hf, n + 1)
                                act(gate[:, f, :], psS[:, f, :], ACT.Silu).then_inc(s_si, 1)
                            a.wait_ge(s_yd, j + 7)
                            for f in range(2):
                                a.wait_ge(s_hf, j * 2 + f + 3)
                                act(hidh[:, c % 2, f, :], hid[:, f, :], ACT.Copy).then_inc(s_hh, 1)
            norm_scalar(a, n7, 0)

        @block.tensor
        def _(t_):
            mm = nc.tensor.matmul
            t_.sem_inc(s_tt1, 1)
            t_.sem_inc(s_pv1, 2)
            t_.sem_inc(s_pv, 4)
            t_.sem_inc(s_mt, 2)
            t_.sem_inc(s_dn, 2)
            t_.sem_inc(s_yd, 8)
            t_.wait_ge(s_const, 3)
            norm_tensor(t_, n1)
            t_.wait_ge(s_w1, N_W1)
            for T in range(NT):
                t_.wait_ge(n1.vec, n1.full(T // 4))
                if T >= 4:
                    t_.wait_ge(s_qkv_sb, T - 3)
                mm(psS[:, T % 4, 0:3 * P], xT[:, T * P:(T + 1) * P], w_qkv[:, :, :].rearrange("p a n -> p (a n)"),
                   start=True, stop=True).then_inc(s_qkv, 1)
            for side in range(2):
                for c in range(4):
                    n = side * 4 + c
                    t_.wait_ge(s_qkv_sb, 4 * c + 4)
                    if n >= 2:
                        t_.wait_ge(s_turn_sb, n - 1)
                    for i in range(4):
                        ins = nc.tensor.transpose(psM[:, n % 2, i * P:(i + 1) * P], qkv[:, 4 * c + i, side * P:(side + 1) * P], ident[:, :])
                    ins.then_inc(s_turn, 1)
                    if side == 0 or c < 0:
                        continue
                for T in range(NT):
                    u = side * NT + T
                    t_.wait_ge(s_turn_sb, side * 4 + T // 4 + 1)
                    if u >= 2:
                        t_.wait_ge(s_sma, 2 * (u - 2) + 2)
                    mm(psO[u % 2][:, :], turned[:, T * P:(T + 1) * P], bd[:, side, :], start=True, stop=True).then_inc(s_lg, 1)
            with t_.Fori(0, NG1) as g:
                for b in range(B):
                    it = g * B + b
                    t_.wait_ge(s_on1, 4 * it + 1)
                    for t in range(TPB):
                        u = it * TPB + t
                        t_.wait_ge(s_tml, 4 * u + 4)
                        t_.wait_ge(s_st, u + 1)
                        for h in range(HG):
                            ins = nc.tensor.transpose(psM[:, 0, h * P:(h + 1) * P], tmq[:, h, :].bitcast(F32), ident[:, :])
                        ins.then_inc(s_tt1, 1)
                        t_.wait_ge(s_stv, u + 1)
                        for h in range(HG):
                            ins = nc.tensor.transpose(psM[:, 1, h * P:(h + 1) * P], tmk[:, h, :].bitcast(F32), ident[:, :])
                        ins.then_inc(s_tt1, 1)
                    t_.wait_ge(s_st, it * TPB + TPB + 1)
                    t_.wait_ge(s_stv, it * TPB + TPB + 1)
                    for h in range(HG):
                        for t in range(TPB):
                            m = (it * HG + h) * TPB + t
                            t_.wait_ge(s_mr1, m + 1)
                            for kc in range(2):
                                dst = psM[:, kc, :] if t % 2 == 0 else psS[:, kc, :]
                                ins = mm(dst, qst[:, h, t * P:(t + 1) * P], kst[:, h, kc * 512:(kc + 1) * 512], start=True, stop=True)
                            ins.then_inc(s_mm1, 1)
                        t_.wait_ge(s_mr1, (it * HG + h) * TPB + TPB + 2)
                        t_.wait_ge(s_mw1, it * HG + h + 1)
                        nc.tensor.transpose(psO[h % 2][0:TPB, 0:P], mx1[:, h, :], ident[:, :]).then_inc(s_mt1, 1)
                    t_.wait_ge(s_mw1, it * HG + HG + 2)
                    t_.wait_ge(s_v32, it + 1)

                    def scores(c, kt):
                        for pair in range(2):
                            q = ((it * 2 + c) * TPB + kt) * 2 + pair
                            t_.wait_ge(s_ex1, q + 1)
                            for i in range(2):
                                h = 2 * pair + i
                                ins = mm(psS[:, h, :], kst[:, h, kt * P:(kt + 1) * P], qst[:, h, c * 512:(c + 1) * 512],
                                         start=True, stop=True)
                            ins.then_inc(s_qk1, 1)

                    def result(c):
                        o = it * 2 + c
                        t_.wait_ge(s_oc1, o + 3)
                        for i in range(4):
                            ins = nc.tensor.transpose(psM[:, c, i * P:(i + 1) * P], osb[:, c, i * P:(i + 1) * P], ident[:, :])
                        ins.then_inc(s_ot1, 1)

                    scores(0, 0)
                    for c in range(2):
                        for kt in range(TPB):
                            if c * TPB + kt + 1 < 2 * TPB:
                                scores(c + (kt + 1) // TPB, (kt + 1) % TPB)
                            step = (it * 2 + c) * TPB + kt
                            t_.wait_ge(s_ex1, 2 * step + 4)
                            if kt == 0:
                                t_.wait_ge(s_oc1, it * 2 + c + 1)
                            for h in range(HG):
                                ins = mm(psO[c][32 * h:32 * h + 32, :], v32[:, kt, h, :], pr1[:, kt % 2, h, :],
                                         start=(kt == 0), stop=(kt == TPB - 1))
                            ins.then_inc(s_pv1, 1)
                            if c == 1 and kt == 2:
                                result(0)
                    result(1)
            for c in range(4):
                t_.wait_ge(s_on1, 4 * NG1 * B + 1)
                if c >= 2:
                    t_.wait_ge(s_a1s, c - 1)
                for i in range(4):
                    ins = nc.tensor.transpose(psM[:, c % 2, i * P:(i + 1) * P], attn1[:, 4 * c + i, :], ident[:, :])
                ins.then_inc(s_a1t, 1)
            for c in range(4):
                t_.wait_ge(s_a1s, c + 1)
                for i in range(4):
                    T = 4 * c + i
                    ins = mm(psS[:, c, i * P:(i + 1) * P], turned[:, T * P:(T + 1) * P], wo1[:, :], start=True, stop=True)
                ins.then_inc(s_wo1, 1)
            norm_tensor(t_, n2)

            def up1(c):
                t_.wait_ge(n2.vec, n2.full(c))
                for m in range(MCH):
                    n = c * MCH + m
                    if n >= 4:
                        t_.wait_ge(s_re1, n - 3)
                    mm(psS[:, n % 4, :], w_up[:, m * P:(m + 1) * P], xT[:, c * 512:(c + 1) * 512],
                       start=True, stop=True).then_inc(s_up1, 1)

            up1(0)
            for c in range(4):
                if c < 3:
                    up1(c + 1)
                t_.wait_ge(s_re1, 4 * c + 4)
                if c >= 2:
                    t_.wait_ge(s_dx1, c - 1)
                for i in range(4):
                    for m in range(MCH):
                        ins = mm(psO[c % 2][:, i * P:(i + 1) * P], relu1[:, c % 2, m, i * P:(i + 1) * P], w_dn[:, m, :],
                                 start=(m == 0), stop=(m == MCH - 1))
                ins.then_inc(s_dn1, 1)
            if debug == 1:
                return

            t_.wait_ge(s_cs2, N_CS2)
            with t_.Fori(0, L) as l:
                norm_tensor(t_, n5, l)

                def project(u, t, b, g):
                    T = b * TPB + t
                    wh = wah[:, ds(g), :].rearrange("p a n -> p (a n)")
                    wl = wal[:, ds(g), :].rearrange("p a n -> p (a n)")
                    t_.wait_ge(s_sa, 2 * u + 1)
                    mm(psP[:, 0:CG], xh[:, T * P:(T + 1) * P], wh, start=True, stop=False)
                    mm(psP[:, 0:CG], xh[:, T * P:(T + 1) * P], wl, start=False, stop=False)
                    mm(psP[:, 0:CG], xl[:, T * P:(T + 1) * P], wh, start=False, stop=True).then_inc(s_pj, 1)

                def turn(u, it, t):
                    t_.wait_ge(s_rp, 7 * u + 6)
                    t_.wait_ge(s_mr, it * MAXED[TPB] + MAXED[t] + 1)
                    for h in range(GQ):
                        ins = mm(psM[:, 0, h * P:(h + 1) * P], tqh[:, h, :, :].rearrange("p a n -> p (a n)"), identr[:, :],
                                 start=(h == 0), stop=(h == GQ - 1), skip_group_check=True)
                    ins.then_inc(s_tt, 1)
                    for i in range(2):
                        ins = mm(psP[:, i * P:(i + 1) * P], tkk[:, 2 * i:2 * i + 2, :].rearrange("p a n -> p (a n)"), identr[:, :],
                                 start=(i == 0), stop=(i == 1), skip_group_check=True)
                    ins.then_inc(s_tt, 1)

                def maximum(u, it, t, b, m):
                    if m == 0:
                        t_.wait_ge(s_sa, 2 * u + 3)
                    if m >= 2:
                        t_.wait_ge(s_mr, it * MAXED[TPB] + MAXED[t] + m)
                    h, k0, k1 = max_pieces(t)[m]
                    diagonal = k1 == (t + 1) * P
                    ins = mm(psM[:, m % 2, 0:k1 - k0], qs1[b][:, t, h, :], ks[b][:, 0, k0:k1], start=True, stop=not diagonal)
                    if diagonal:
                        ins = mm(psM[:, m % 2, k1 - k0 - P:k1 - k0], identb[:, :], maskq[:, :], start=False, stop=True)
                    ins.then_inc(s_ms, 1)

                def turn_low(u, it, t):
                    t_.wait_ge(s_mr, it * MAXED[TPB] + MAXED[t + 1] + 1)
                    t_.wait_ge(s_mw, u + 1)
                    for h in range(GQ):
                        ins = mm(psU[:, h * P:(h + 1) * P], tql[:, t % 2, h, :, :].rearrange("p a n -> p (a n)"), identr[:, :],
                                 start=(h == 0), stop=(h == GQ - 1), skip_group_check=True)
                    ins.then_inc(s_mt, 1)

                def scores2(it, t, kt, b):
                    i = TRI[t] + kt
                    if i == 0:
                        t_.wait_ge(s_mw, it * TPB + TPB + 1)
                    t_.wait_ge(s_ex, it * TRI[TPB] + i + 3)
                    tile = slice(kt * P, (kt + 1) * P)
                    mm(psS[:, i % 2, :], ks[b][:, 0, tile], qs1[b][:, t, :, :].rearrange("p h n -> p (h n)"), start=True, stop=False)
                    ins = mm(psS[:, i % 2, :], ks[b][:, 1, tile], qs2[b][:, t, :, :].rearrange("p h n -> p (h n)"),
                             start=False, stop=(kt < t))
                    if kt == t:
                        ins = mm(psS[:, i % 2, :], identb[:, :], maskk[:, :].unsqueeze(1).broadcast_to([P, GQ, P]), start=False, stop=True)
                    ins.then_inc(s_qk, 1)

                def values(it, t, kt, b):
                    i = TRI[t] + kt
                    t_.wait_ge(s_ex, it * TRI[TPB] + i + 5)
                    if kt == 0:
                        t_.wait_ge(s_wx, it * TPB + t + 1)
                    for q in range(2):
                        ins = mm(psO[t % 2][q * HD:(q + 1) * HD, 0:256], vv[b][:, kt, :], prob[:, i % 4, q * 256:(q + 1) * 256],
                                 start=(kt == 0), stop=(kt == t))
                    ins.then_inc(s_pv, 1)

                def denominator(it, t):
                    total = prob[:, 0, :] if t == 0 else psum_k[:, t % 2, :]
                    if t > 0:
                        t_.wait_ge(s_su, it * TRI[TPB] + TRI[t] + t + 5)
                    else:
                        t_.wait_ge(s_ex, it * TRI[TPB] + 5)
                        t_.wait_ge(s_wx, it * TPB + 1)
                    for q in range(2):
                        ins = mm(psO[t % 2][q * HD:(q + 1) * HD, 256:512], ones64[:, :], total[:, q * 256:(q + 1) * 256],
                                 start=True, stop=True)
                    ins.then_inc(s_dn, 1)

                def out_projection(it, t, g):
                    t_.wait_ge(s_at, it * TPB + t + 2)
                    for i in range(2):
                        ins = mm(psO[t % 2][:, 0:D], att[:, t % 2, i * P:(i + 1) * P],
                                 wos[:, ds(g), i, :].rearrange("p a d -> p (a d)"), start=(i == 0), stop=(i == 1))
                    ins.then_inc(s_wo, 1)

                def head(order, g, b, g_next, b_next):
                    it = (l * NKV + g) * B + b
                    it_next = (l * NKV + g_next) * B + b_next
                    for what, t, *more in order["tensor"]:
                        u = it_next * TPB + t
                        if what == "P":
                            project(u, t, b_next, g_next)
                        elif what == "R":
                            turn(u, it_next, t)
                        elif what == "M":
                            maximum(u, it_next, t, b_next, *more)
                        elif what == "N":
                            turn_low(u, it_next, t)
                        elif what == "S":
                            scores2(it, t, *more, b)
                        elif what == "V":
                            values(it, t, *more, b)
                        elif what == "D":
                            denominator(it, t)
                        elif what == "O":
                            out_projection(it, t, g)

                t_.wait_ge(n5.vec, n5.steps_vec * l + n5.steps_vec)
                t_.wait_ge(s_wsl, 2 * l + 2)
                head(PREPARE, 0, 0, 0, 0)
                with t_.Fori(0, NKV - 1) as g:
                    head(BOTH, g, 0, g, 1)
                    head(BOTH, g, 1, g + 1, 0)
                head(BOTH, NKV - 1, 0, NKV - 1, 1)
                head(ATTEND, NKV - 1, 1, 0, 0)
                norm_tensor(t_, n6, l)
                t_.wait_ge(n6.vec, n6.steps_vec * l + n6.steps_vec)
                for T in range(NT):
                    ts = slice(T * P, (T + 1) * P)
                    o = psO[0][:, T * E:(T + 1) * E]
                    mm(o, xh[:, ts], wrh[:, :], start=True, stop=False)
                    mm(o, xh[:, ts], wrl[:, :], start=False, stop=False)
                    ins = mm(o, xl[:, ts], wrh[:, :], start=False, stop=True)
                ins.then_inc(s_rl, 1)
                with t_.Fori(0, E // 2) as ep:
                    for ee in range(2):
                        le = (l * (E // 2) + ep) * 2 + ee

                        def up2(c):
                            cs = slice(c * 512, (c + 1) * 512)
                            for f in range(2):
                                n = (le * 4 + c) * 2 + f
                                t_.wait_ge(s_si, n + 1)
                                t_.wait_ge(s_hf, n + 1)
                                for bank, w0 in ((f, f * P), (2 + f, FF + f * P)):
                                    mm(psS[:, bank, :], eh[ee][:, w0:w0 + P], xh[:, cs], start=True, stop=False)
                                    mm(psS[:, bank, :], eh[ee][:, w0:w0 + P], xl[:, cs], start=False, stop=False)
                                    ins = mm(psS[:, bank, :], el[ee][:, w0:w0 + P], xh[:, cs], start=False, stop=True)
                                ins.then_inc(s_gu, 1)

                        def down2(c):
                            j = le * 4 + c
                            t_.wait_ge(s_hl, 2 * j + 4)
                            t_.wait_ge(s_yx, j + 1)
                            for i in range(4):
                                o = psO[c % 2][:, i * D:(i + 1) * D]
                                hs = slice(i * P, (i + 1) * P)
                                for f in range(2):
                                    w0 = 2 * FF + f * D
                                    mm(o, hidh[:, c % 2, f, hs], eh[ee][:, w0:w0 + D], start=(f == 0), stop=False)
                                    mm(o, hidh[:, c % 2, f, hs], el[ee][:, w0:w0 + D], start=False, stop=False)
                                    ins = mm(o, hidl[:, c % 2, f, hs], eh[ee][:, w0:w0 + D], start=False, stop=(f == 1))
                            ins.then_inc(s_yd, 1)

                        t_.wait_ge(s_el, le + 2)
                        up2(0)
                        for c in range(4):
                            if c < 3:
                                up2(c + 1)
                            down2(c)

        @block.vector
        def _(v):
            vec = nc.vector
            v.sem_inc(s_on1, 1)
            v.sem_inc(s_stv, 1)
            v.sem_inc(s_mr1, 2)
            v.sem_inc(s_mw1, 2)
            v.sem_inc(s_oc1, 2)
            v.sem_inc(s_mr, 1)
            v.sem_inc(s_at, 1)
            v.sem_inc(s_wx, 2)
            v.sem_inc(s_cl1, 1)
            v.sem_inc(s_cl2, 1)
            v.sem_inc(s_hf, 2)
            v.sem_inc(s_hl, 2)
            v.sem_inc(s_yx, 2)
            v.sem_inc(s_el, 1)
            v.wait_ge(s_x, 16)
            norm_vector(v, n0)
            v.wait_ge(s_w1, N_W1)
            norm_vector(v, n1, 0, gcol[:, 0:1], gcol[:, 1:2], start=((n0.vec, n0.steps_vec),))
            for n in range(8):
                v.wait_ge(s_turn, n + 1)
                if n == 4:
                    v.wait_ge(s_lg, NT)
                vec.tensor_copy(turned[:, (n % 4) * 512:(n % 4 + 1) * 512], psM[:, n % 2, :]).then_inc(s_turn_sb, 1)
                if n == 3:
                    softmax_from, softmax_to = 0, NT
                elif n == 7:
                    softmax_from, softmax_to = NT, 2 * NT
                else:
                    continue

                def off(u):
                    dst = (qb, kb)[u // NT][:, u % NT, :].rearrange("p (h n) -> p h n", h=H1)
                    lg = psO[u % 2][:, :].rearrange("p (h n) -> p h n", h=H1)
                    v.wait_ge(s_lg, u + 1)
                    vec.tensor_reduce(smm[:, u % 2, :], lg, AX.X, ALU.max).then_inc(s_sma, 1)
                    v.wait_ge(s_sma, 2 * u + 1)
                    vec.tensor_tensor(dst, lg, smm[:, u % 2, :].unsqueeze(2).broadcast_to([P, H1, NB]), ALU.subtract).then_inc(s_sma, 1)

                off(softmax_from)
                for u in range(softmax_from, softmax_to):
                    if u + 1 < softmax_to:
                        off(u + 1)
                    dst = (qb, kb)[u // NT][:, u % NT, :].rearrange("p (h n) -> p h n", h=H1)
                    v.wait_ge(s_sme, u + 1)
                    vec.tensor_reduce(sms[:, u % 2, :], dst, AX.X, ALU.add).then_inc(s_smb, 1)
                    v.wait_ge(s_smb, 3 * u + 1)
                    vec.reciprocal(smr[:, u % 2, :], sms[:, u % 2, :]).then_inc(s_smb, 1)
                    v.wait_ge(s_smb, 3 * u + 2)
                    vec.tensor_tensor(dst, dst, smr[:, u % 2, :].unsqueeze(2).broadcast_to([P, H1, NB]), ALU.mult).then_inc(s_smb, 1)
            v.wait_ge(s_smb, 3 * 2 * NT)
            v.wait_ge(s_v32c, 2)
            v.wait_ge(s_qkv_sb, NT)
            with v.Fori(0, NG1) as g:
                for b in range(B):
                    it = g * B + b
                    vec.tensor_copy(v32[:, :, :, 0:F1],
                                    qkv[:, b * TPB:(b + 1) * TPB, ds(g * (HG * F1) + 2 * P, HG * F1)]
                                    .rearrange("p t (h f) -> p t h f", h=HG)).then_inc(s_v32, 1)
                    for t in range(TPB):
                        u, T = it * TPB + t, b * TPB + t
                        qh = qb[:, T, ds(g * (HG * NB), HG * NB)].rearrange("p (h n) -> p h n", h=HG)
                        kh = kb[:, T, ds(g * (HG * NB), HG * NB)].rearrange("p (h n) -> p h n", h=HG)
                        qq = qkv[:, T, ds(g * (HG * F1), HG * F1)].rearrange("p (h f) -> p h f", h=HG)
                        kk = qkv[:, T, ds(g * (HG * F1) + P, HG * F1)].rearrange("p (h f) -> p h f", h=HG)
                        v.wait_ge(s_tmh, 6 * u + 6)
                        vec.scalar_tensor_tensor(out=tmq[:, :, 64:96], in0=qh, scalar=CLUSTER, in1=tmq[:, :, 0:32],
                                                 op0=ALU.mult, op1=ALU.subtract).then_inc(s_tml, 1)
                        vec.scalar_tensor_tensor(out=tmq[:, :, 120:128], in0=qq, scalar=float(F1) ** -0.5, in1=tmq[:, :, 104:112],
                                                 op0=ALU.mult, op1=ALU.subtract).then_inc(s_tml, 1)
                        vec.tensor_tensor(tmk[:, :, 32:64], kh, tmk[:, :, 0:32], ALU.subtract).then_inc(s_tml, 1)
                        vec.tensor_tensor(tmk[:, :, 112:120], kk, tmk[:, :, 104:112], ALU.subtract).then_inc(s_tml, 1)
                        v.wait_ge(s_tt1, 2 * u + 3)
                        vec.tensor_copy(kst[:, :, t * P:(t + 1) * P], psM[:, 1, :].rearrange("p (h n) -> p h n", h=HG)).then_inc(s_stv, 1)
                    for h in range(HG):
                        for t in range(TPB):
                            m = (it * HG + h) * TPB + t
                            v.wait_ge(s_mm1, m + 1)
                            src = psM[:, :, :] if t % 2 == 0 else psS[:, 0:2, :]
                            vec.tensor_reduce(mx1[:, h, t:t + 1], src, AX.XY, ALU.max).then_inc(s_mr1, 1)
                        v.wait_ge(s_mt1, it * HG + h + 1)
                        vec.tensor_tensor(qst[96:104, h, :].rearrange("p (t n) -> p t n", t=TPB),
                                          psO[h % 2][0:TPB, 0:P].unsqueeze(1).broadcast_to([TPB, TPB, P]),
                                          blk[0:TPB, :, :], ALU.mult).then_inc(s_mw1, 1)
                    for c in range(2):
                        o = it * 2 + c
                        v.wait_ge(s_pv1, o * TPB + TPB + 2)
                        vec.tensor_copy(osb[:, c, :], psO[c][:, :]).then_inc(s_oc1, 1)
                        v.wait_ge(s_ot1, o + 1)
                        tok = psM[:, c, :].rearrange("p (t h f) -> p t h f", t=4, h=HG)
                        vec.reciprocal(rd1[:, :, :], tok[:, :, :, F1]).then_inc(s_on1, 1)
                        v.wait_ge(s_on1, 2 * o + 2)
                        vec.tensor_tensor(attn1[:, b * TPB + 4 * c:b * TPB + 4 * c + 4, ds(g * (HG * F1), HG * F1)]
                                          .rearrange("p t (h f) -> p t h f", h=HG), tok[:, :, :, 0:F1],
                                          rd1[:, :, :].unsqueeze(3).broadcast_to([P, 4, HG, F1]), ALU.mult).then_inc(s_on1, 1)
            for c in range(4):
                v.wait_ge(s_a1t, c + 1)
                vec.tensor_copy(turned[:, c * 512:(c + 1) * 512], psM[:, c % 2, :]).then_inc(s_a1s, 1)
            for c in range(4):
                v.wait_ge(s_wo1, c + 1)
                r = inner[:, 4 * c:4 * c + 4, :].rearrange("p t d -> p (t d)")
                vec.tensor_tensor(r, r, psS[:, c, :], ALU.add).then_inc(s_wo1x, 1)
            norm_vector(v, n2, 0, gcol[:, 2:3], gcol[:, 3:4], start=((s_wo1x, 4),))
            for c in range(4):
                v.wait_ge(s_dn1, c + 1)
                r = inner[:, 4 * c:4 * c + 4, :].rearrange("p t d -> p (t d)")
                vec.tensor_tensor(r, r, psO[c % 2][:, :], ALU.add).then_inc(s_dx1, 1)
            v.wait_ge(s_dx1, 4)
            vec.tensor_tensor(inner[:, :, :], inner[:, :, :], b2r[:, :].unsqueeze(1).broadcast_to([P, NT, D]), ALU.add).then_inc(s_dx1, 1)
            norm_vector(v, n3, start=((s_dx1, 5),))
            v.wait_ge(n3.vec, n3.steps_vec)
            vec.tensor_tensor(outer[:, :, :], outer[:, :, :], normed[:, :, :], ALU.add).then_inc(s_r1, 1)
            if debug == 1:
                return
            norm_vector(v, n4, start=((s_r1, 1),))
            v.wait_ge(s_c2l, 32)
            v.wait_ge(s_cs2, N_CS2)
            with v.Fori(0, L) as l:
                v.wait_ge(s_wsh, 2 * l + 2)
                vec.tensor_tensor(wal[:, :, :], wst[:, :, :], wah[:, :, :], ALU.subtract).then_inc(s_wsl, 1)
                vec.tensor_tensor(wrl[:, :], wrs[:, :], wrh[:, :], ALU.subtract).then_inc(s_wsl, 1)
                norm_vector(v, n5, l, fcol[:, ds(l)])

                def head(order, g, b, g_next, b_next):
                    it = (l * NKV + g) * B + b
                    it_next = (l * NKV + g_next) * B + b_next
                    for what, t, *more in order["vector"]:
                        u, tau = it_next * TPB + t, it * TPB + t
                        if what == "P":
                            v.wait_ge(s_pj, u + 1)
                            pr = psP[:, 0:5 * HD].rearrange("p (h f) -> p h f", h=5)
                            c_t = cosT[:, t, :].unsqueeze(1).broadcast_to([P, 5, HD])
                            s_lo = sinT[:, t, 0:HD // 2].unsqueeze(1).broadcast_to([P, 5, HD // 2])
                            s_hi_ = sinT[:, t, HD // 2:HD].unsqueeze(1).broadcast_to([P, 5, HD // 2])
                            vec.tensor_tensor(rope_a[:, :, :], pr, c_t, ALU.mult).then_inc(s_rp, 1)
                            vec.tensor_tensor(rope_b[:, :, 0:HD // 2], pr[:, :, HD // 2:HD], s_lo, ALU.mult).then_inc(s_rp, 1)
                            vec.tensor_tensor(rope_b[:, :, HD // 2:HD], pr[:, :, 0:HD // 2], s_hi_, ALU.mult).then_inc(s_rp, 1)
                            vec.tensor_copy(vv[b_next][:, t, :], psP[:, 5 * HD:6 * HD]).then_inc(s_rp, 1)
                            v.wait_ge(s_rp, 7 * u + 4)
                            vec.tensor_tensor(roped[:, :, :], rope_a[:, :, :], rope_b[:, :, :], ALU.add).then_inc(s_rp, 1)
                        elif what == "L":
                            v.wait_ge(s_hi, 2 * u + 2)
                            vec.tensor_tensor(tkk[:, 1, :], roped[:, GQ, :], tkk[:, 0, :], ALU.subtract).then_inc(s_rp, 1)
                            v.wait_ge(s_mt, u + 1)
                            vec.tensor_tensor(tql[:, t % 2, :, 1, :], roped[:, 0:GQ, :], tqh[:, :, 0, :], ALU.subtract).then_inc(s_rp, 1)
                        elif what == "M":
                            m, pieces = more[0], max_pieces(t)
                            joined, done = len(pieces) > GQ, it_next * MAXED[TPB] + MAXED[t] + 1
                            if m == 0 and joined:
                                v.wait_ge(s_mr, done)
                            h, k0, k1 = pieces[m]
                            v.wait_ge(s_ms, it_next * PIECES[TPB] + PIECES[t] + m + 1)
                            dst = mxp[:, h, m % 2:m % 2 + 1] if joined else tql[:, t % 2, h, 0, 0:1]
                            vec.tensor_reduce(dst, psM[:, m % 2, 0:k1 - k0], AX.X, ALU.max).then_inc(s_mr, 1)
                            if joined and m == len(pieces) - 1:
                                v.wait_ge(s_mr, done + len(pieces))
                                vec.tensor_tensor(tql[:, t % 2, :, 0, 0], mxp[:, :, 0], mxp[:, :, 1], ALU.max).then_inc(s_mr, 1)
                        elif what == "D":
                            normalise(it, t)
                        elif what == "O":
                            v.wait_ge(s_wo, tau + 1)
                            v.wait_ge(s_wx, tau + 2)
                            vec.tensor_tensor(inner[:, b * TPB + t, :], inner[:, b * TPB + t, :], psO[t % 2][:, 0:D],
                                              ALU.add).then_inc(s_wx, 1)

                def normalise(it, t):
                    v.wait_ge(s_dn, it * TPB + t + 3)
                    if t == 0:
                        v.wait_ge(s_pv, it * TRI[TPB] + 5)
                    v.wait_ge(s_at, it * TPB + t + 1)
                    vec.reciprocal(rden[:, :], psO[t % 2][:, 256:512]).then_inc(s_rd, 1)
                    v.wait_ge(s_rd, it * TPB + t + 1)
                    vec.tensor_tensor(att[:, t % 2, :], psO[t % 2][:, 0:256], rden[:, :], ALU.mult).then_inc(s_at, 1)

                head(PREPARE, 0, 0, 0, 0)
                with v.Fori(0, NKV - 1) as g:
                    head(BOTH, g, 0, g, 1)
                    head(BOTH, g, 1, g + 1, 0)
                head(BOTH, NKV - 1, 0, NKV - 1, 1)
                head(ATTEND, NKV - 1, 1, 0, 0)
                v.wait_ge(s_wx, (l * NKV * B + NKV * B) * TPB + 2)
                vec.tensor_scalar(inner[:, :, :], inner[:, :, :], 100.0, -100.0, ALU.min, ALU.max).then_inc(s_cl1, 1)
                norm_vector(v, n6, l, fcol[:, ds(l + L)])

                k = 0

                def route(ins):
                    nonlocal k
                    k += 1
                    ins.then_inc(s_rv, 1)
                    if k < N_ROUTE:
                        v.wait_ge(s_rv, N_ROUTE * l + k)

                def over(x):
                    return x[:, :].unsqueeze(2).broadcast_to([P, NT, E])

                v.wait_ge(s_rl, l + 1)
                lg = psO[0][:, 0:NT * E].rearrange("p (t e) -> p t e", t=NT)
                first_of = order[:, :].unsqueeze(1).broadcast_to([P, NT, E])
                route(vec.tensor_reduce(r1[0][:, :], lg, AX.X, ALU.max))
                route(vec.tensor_tensor(rt[0][:, :, :], lg, over(r1[0]), ALU.subtract))
                v.wait_ge(s_re, l + 1)
                route(vec.tensor_reduce(r1[0][:, :], rt[0][:, :, :], AX.X, ALU.max))
                route(vec.tensor_tensor(rt[1][:, :, :], rt[0][:, :, :], over(r1[0]), ALU.is_equal))
                route(vec.tensor_tensor(rt[2][:, :, :], rt[1][:, :, :], first_of, ALU.mult))
                route(vec.tensor_reduce(r1[1][:, :], rt[2][:, :, :], AX.X, ALU.max))
                route(vec.tensor_tensor(rt[1][:, :, :], rt[2][:, :, :], over(r1[1]), ALU.is_equal))
                route(vec.scalar_tensor_tensor(out=rt[3][:, :, :], in0=rt[1][:, :, :], scalar=-2.0, in1=rt[0][:, :, :],
                                               op0=ALU.mult, op1=ALU.add))
                route(vec.tensor_reduce(r1[2][:, :], rt[3][:, :, :], AX.X, ALU.max))
                route(vec.tensor_tensor(rt[4][:, :, :], rt[3][:, :, :], over(r1[2]), ALU.is_equal))
                route(vec.tensor_tensor(rt[2][:, :, :], rt[4][:, :, :], first_of, ALU.mult))
                route(vec.tensor_reduce(r1[1][:, :], rt[2][:, :, :], AX.X, ALU.max))
                route(vec.tensor_tensor(rt[4][:, :, :], rt[2][:, :, :], over(r1[1]), ALU.is_equal))
                route(vec.tensor_tensor(rt[5][:, :, :], rt[1][:, :, :], rt[4][:, :, :], ALU.add))
                route(vec.tensor_tensor(rt[5][:, :, :], rt[5][:, :, :], rt[0][:, :, :], ALU.mult))
                route(vec.tensor_tensor(r1[3][:, :], r1[0][:, :], r1[2][:, :], ALU.add))
                route(vec.reciprocal(r1[3][:, :], r1[3][:, :]))
                route(vec.tensor_tensor(comb[:, :, :], rt[5][:, :, :], over(r1[3]), ALU.mult))
                assert k == N_ROUTE
                with v.Fori(0, E // 2) as ep:
                    for ee in range(2):
                        le = (l * (E // 2) + ep) * 2 + ee

                        def hidden(c):
                            j = le * 4 + c
                            for f in range(2):
                                n = j * 2 + f
                                v.wait_ge(s_si, n + 3)
                                v.wait_ge(s_hh, n + 1)
                                v.wait_ge(s_hl, n + 1)
                                vec.tensor_tensor(hid[:, f, :], gate[:, f, :], psS[:, 2 + f, :], ALU.mult).then_inc(s_hf, 1)
                            for f in range(2):
                                v.wait_ge(s_hh, j * 2 + f + 3)
                                vec.tensor_tensor(hidl[:, c % 2, f, :], hid[:, f, :], hidh[:, c % 2, f, :], ALU.subtract).then_inc(s_hl, 1)

                        def add(c):
                            j = le * 4 + c
                            v.wait_ge(s_rv, N_ROUTE * l + N_ROUTE)
                            v.wait_ge(s_yd, j + 9)
                            v.wait_ge(s_yx, j + 2)
                            for i in range(4):
                                T = 4 * c + i
                                ins = vec.scalar_tensor_tensor(
                                    out=inner[:, T, :], in0=psO[c % 2][:, i * D:(i + 1) * D],
                                    scalar=comb[:, T, ds(ep * 2 + ee)], in1=inner[:, T, :], op0=ALU.mult, op1=ALU.add)
                            ins.then_inc(s_yx, 1)

                        hidden(0)
                        for c in range(4):
                            if c < 3:
                                hidden(c + 1)
                            add(c)
                v.wait_ge(s_yx, (l * E + E) * 4 + 2)
                vec.tensor_scalar(inner[:, :, :], inner[:, :, :], 100.0, -100.0, ALU.min, ALU.max).then_inc(s_cl2, 1)
            norm_vector(v, n7, start=((s_cl2, L + 1),))
            v.wait_ge(n7.vec, n7.steps_vec)
            vec.tensor_tensor(outer[:, :, :], outer[:, :, :], normed[:, :, :], ALU.add).then_inc(s_r2, 1)


_INS = ["L0_attn_inputs", "L0_attn_ln1_g", "L0_attn_ln1_b", "L0_attn_Wq", "L0_attn_Wk", "L0_attn_Wv", "L0_attn_Whq",
        "L0_attn_Whk", "L0_attn_Wo", "L0_attn_ln2_g", "L0_attn_ln2_b", "L0_attn_W1", "L0_attn_b1", "L0_attn_W2",
        "L0_attn_b2", "L0_ffn_ln1_w", "L0_ffn_ln2_w", "L0_ffn_wq", "L0_ffn_wk", "L0_ffn_wv", "L0_ffn_wo", "L0_ffn_wr",
        "L0_ffn_wg", "L0_ffn_wu", "L0_ffn_wd"]


def rope_tables():
    inv = (1.0 / np.float32(10000.0) ** (np.arange(0, HD, 2, dtype=np.float32) / np.float32(HD))).astype(np.float32)
    f = np.arange(SEQ, dtype=np.float32)[:, None] * inv
    c, s = np.cos(f).astype(np.float32), np.sin(f).astype(np.float32)
    return np.concatenate([c, c], 1), np.concatenate([-s, s], 1)


def kernel(**inputs):
    import concourse.bacc as bacc
    from concourse.bass_utils import run_bass_kernel_spmd as run

    nc = bacc.Bacc("TRN2", target_bir_lowering=False, num_devices=1)
    arrays, args = {}, []
    cos, sin = rope_tables()
    for name, a in [(n, inputs[n]) for n in _INS] + [("rope_cos", cos), ("rope_sin", sin)]:
        a = np.ascontiguousarray(a)
        arrays[f"in_{name}"] = a
        args.append(nc.dram_tensor(f"in_{name}", a.shape, mybir.dt.from_np(a.dtype), kind="ExternalInput").ap())
    args.append(nc.dram_tensor("out_0", (B, SEQ, D), F32, kind="ExternalOutput").ap())
    program(nc, *args)
    r = run(nc, [arrays], core_ids=[0])
    return r.results[0]["out_0"]
```

```python
from contextlib import ExitStack

import numpy as np

import concourse.bass as bass
from concourse import mybir

F32 = mybir.dt.float32
F32R = mybir.dt.float32r
BF16 = mybir.dt.bfloat16
ALU = mybir.AluOpType
ACT = mybir.ActivationFunctionType
AX = mybir.AxisListType

P = 128
B, SEQ, D = 2, 1024, 128
TPB = SEQ // P
NT = B * TPB
H1, F1, NB, MLP = 16, 8, 32, 512
HG = 4
NG1 = H1 // HG
MCH = MLP // P
CLUSTER = 0.1
L, NH, NKV, HD, FF, E = 4, 16, 4, 64, 256, 8
GQ = NH // NKV
CG = GQ * HD + 2 * HD
WE = 2 * FF + 2 * D
TRI = [t * (t + 1) // 2 for t in range(TPB + 1)]
NEG = -1.0e9


def max_pieces(t):
    keys = (t + 1) * P
    return [(h, k0, min(k0 + 512, keys)) for h in range(GQ) for k0 in range(0, keys, 512)]


PIECES = [sum(len(max_pieces(i)) for i in range(t)) for t in range(TPB + 1)]
MAXED = [PIECES[t] + sum(1 for i in range(t) if len(max_pieces(i)) > GQ) for t in range(TPB + 1)]
SLOT = [PIECES[t] + 2 * t for t in range(TPB + 1)]
STEPS = [(t, kt) for t in range(TPB) for kt in range(t + 1)]


def planned(plan, priority, handover):
    end, free, order = {}, {}, {engine: [] for engine in ("tensor", "scalar", "vector", "gpsimd")}

    def start(key):
        return max([free.get(key[0], 0)] + [end[a] + handover * (a[0] != key[0]) for a in plan[key][1]])

    while len(end) < len(plan):
        ready = [key for key in plan if key not in end and all(a in end for a in plan[key][1])]
        key = min(ready, key=lambda key: (start(key), priority.index(key[1][0])))
        end[key] = free[key[0]] = start(key) + plan[key][0]
        order[key[0]].append(key[1])
    return order


def cluster_order(attend, prepare):
    plan = {}

    def stage(engine, name, cost, *after):
        plan[engine, name] = (cost, [a for a in after if a])

    if attend:
        for j in range(2 * TPB):
            for h in range(HG):
                i = j * HG + h
                stage("tensor", ("S", i), 214, ("scalar", ("S", i - 3)) if i > 2 else None, ("tensor", ("S", i - 1)) if i else None)
                stage("scalar", ("S", i), 490, ("tensor", ("S", i)), ("tensor", ("V", j - 2)) if j > 1 else None,
                      ("scalar", ("S", i - 1)) if i else None)
            stage("tensor", ("V", j), 600, ("scalar", ("S", j * HG + HG - 1)), ("tensor", ("V", j - 1)) if j else None)
        for c in range(2):
            stage("vector", ("C", c), 720, ("tensor", ("V", c * TPB + TPB - 1)))
            stage("tensor", ("C", c), 860, ("vector", ("C", c)))
            stage("vector", ("D", c), 450, ("tensor", ("C", c)))
    if prepare:
        for t in range(TPB):
            stage("scalar", ("H", t), 1370, ("tensor", ("T", t - 2)) if t > 1 else None, ("scalar", ("H", t - 1)) if t else None)
            stage("vector", ("L", t), 600, ("scalar", ("H", t)))
            stage("tensor", ("T", t), 1240, ("vector", ("L", t)), ("scalar", ("E", t - 1)) if t else None,
                  ("vector", ("E", t - 2)) if t > 1 else None)
            stage("scalar", ("E", t), 480, ("tensor", ("T", t)))
            stage("vector", ("E", t), 540, ("tensor", ("T", t)))
        for m in range(N_MAX1):
            stage("tensor", ("M", m), 290, ("scalar", ("E", TPB - 1)), ("vector", ("E", TPB - 1)),
                  ("vector", ("M", m - 3)) if m > 2 else None, ("tensor", ("M", m - 1)) if m else None)
            stage("vector", ("M", m), 600, ("tensor", ("M", m)))
        stage("vector", ("J",), 100, ("vector", ("M", N_MAX1 - 1)))
        stage("tensor", ("J",), 220, ("vector", ("J",)))
        stage("scalar", ("J",), 200, ("tensor", ("J",)))
    return planned(plan, "JVLMECHSTD", 160)


N_S1 = 2 * TPB * HG
N_MAX1 = HG * TPB * 2
CLUSTER_PREPARE = cluster_order(False, True)
CLUSTER_BOTH = cluster_order(True, True)
CLUSTER_ATTEND = cluster_order(True, False)


def attention_order(prepare, carried=True, carry=True, begun=True, begin=False, start=False):
    plan = {}

    def stage(engine, name, cost, *after):
        plan[engine, name] = (cost, [a for a in after if a])

    for i, (t, kt) in enumerate(STEPS):
        def back(engine, what, k):
            return (engine, (what, *STEPS[i - k])) if i >= k else None

        stage("tensor", ("S", t, kt), 430 + 210 * (kt == t), ("scalar", ("N", t)) if start and kt == 0 else None, back("scalar", "S", 2), back("tensor", "S", 1))
        stage("scalar", ("S", t, kt), 490, ("tensor", ("S", t, kt)), back("tensor", "V", 4), back("gpsimd", "S", 4),
              back("scalar", "S", 1))
        stage("gpsimd", ("S", t, kt), 1225 * (kt > 0), ("scalar", ("S", t, kt)), back("gpsimd", "S", 1),
              ("tensor", ("D", t - 2)) if kt == 1 and t > (0 if carried else 1) else None)
        stage("tensor", ("V", t, kt), 430, ("scalar", ("S", t, kt)), back("tensor", "V", 1),
              ("vector", ("O", t - 2)) if kt == 0 and t > (0 if carried else 1) else None, ("tensor", ("D", 0)) if i == 0 else None)
    if carried:
        stage("gpsimd", ("S", -1, -1), 1225)
    for t in range(-1 if carried else 0, TPB - 1 if carry else TPB):
        stage("tensor", ("D", t), 344, ("gpsimd", ("S", t, t)), ("tensor", ("V", t, t)) if t > 0 else None)
        stage("vector", ("D", t), 1800, ("tensor", ("D", t)), ("tensor", ("V", t, t)) if t >= 0 else None)
        stage("tensor", ("O", t), 430, ("vector", ("D", t)))
        stage("vector", ("O", t), 200, ("tensor", ("O", t)))
    if prepare:
        tiles = 2 * TPB if start else TPB

        def project(t):
            stage("tensor", ("P", t), 480, *[("tensor", ("R", t - 1)), ("scalar", ("R", t - 1))] * (t > 0),
                  ("tensor", ("V", TPB - 1, 0)) if t == tiles else None)
            stage("vector", ("P", t), 1450, ("tensor", ("P", t)))
            stage("scalar", ("H", t), 720, ("vector", ("P", t)))
            stage("vector", ("L", t), 500, ("scalar", ("H", t)), ("tensor", ("N", t - 2)) if t > 1 else None)

        if begin:
            project(tiles)
        for t in range(tiles):
            pieces = max_pieces(t % TPB)

            def tile(engine, what, k, *more):
                return (engine, (what, t - k, *more)) if t >= k else None

            if t or not begun:
                project(t)
            stage("tensor", ("R", t), 640, ("vector", ("L", t)) if t or not begun else None, tile("tensor", "N", 1))
            stage("scalar", ("R", t), 740, ("tensor", ("R", t)))
            for m, (_, k0, k1) in enumerate(pieces):
                stage("tensor", ("M", t, m), 42 + (k1 - k0) / 3.43 + 42 * (k1 == (t % TPB + 1) * P), ("scalar", ("R", t)),
                      tile("vector", "M", 0, m - 3) if m > 2 else None, tile("scalar", "N", 1), tile("tensor", "M", 0, m - 1) if m else None)
                stage("vector", ("M", t, m), 70 + 1.04 * (k1 - k0) + 150 * (m >= GQ and m == len(pieces) - 1), ("tensor", ("M", t, m)))
            stage("tensor", ("N", t), 430, ("vector", ("M", t, len(pieces) - 1)))
            stage("scalar", ("N", t), 480, ("tensor", ("N", t)))

    return planned(plan, "PHRMNLODSV", 100)


FIRST = attention_order(True, carried=False, begun=False, begin=True, start=True)
MIDDLE = attention_order(True, begin=True)
LAST_PREPARE = attention_order(True)
LAST = attention_order(False, carry=False)


def ds(i, n=1):
    return bass.ds(i, n)


def head_after(g, b, n):
    return (g + (b + n) // B, (b + n) % B) if b + n >= B else (g, b + n)


def head_before(g, b):
    return (g - 1, 1) if b == 0 else (g, 0)


class Norm:

    def __init__(self, sem, name, kind, eps, src, out, turned=None):
        self.square = None
        self.kind, self.eps, self.src, self.out, self.turned = kind, eps, src, out, turned
        self.vec, self.act, self.ten = sem(name + "_vec"), sem(name + "_act"), sem(name + "_ten")
        self.centred = 6 if kind == "ln" else 0
        self.var_ready = self.centred + 5
        self.out_ready = self.centred + 10
        self.steps_vec = self.out_ready + (0 if turned is None else (8 if turned == "split" else 4))
        self.steps_act = 5 + (4 if turned == "split" else 0)
        self.steps_ten = 4 if turned else 0

    def full(self, c):
        return self.out_ready + ([1, 2, 4, 6][c] if self.turned == "split" else c + 1)


def program(nc, x_in, ln1_g, ln1_b, Wq, Wk, Wv, Whq, Whk, Wo, ln2_g, ln2_b, W1, b1, W2, b2,
            f_ln1, f_ln2, wq, wk, wv, wo, wr, wg, wu, wd, cos_in, sin_in, out):
    with ExitStack() as ctx:
        def sem(name):
            return ctx.enter_context(nc.semaphore(name))

        def sb(name, shape, dt=F32, where=ctx):
            return where.enter_context(nc.sbuf_tensor(name, shape, dt))

        psA = ctx.enter_context(nc.psum_tensor("psA", [P, 6, 512], F32))
        psS, psM = psA[:, 0:4, :], psA[:, 4:6, :]
        psO = [ctx.enter_context(nc.psum_tensor(f"psO{i}", [P, 512], F32)) for i in range(2)]
        psG, psC, acc = psA[:, 0:3, :], psA[:, 3, :], [psO[0][:, :], psO[1][:, :], psA[:, 4, :], psA[:, 5, :]]
        psS1, psM1 = psA[:, 0:3, :], psA[:, 3:6, :]
        psP, ring = psA[:, 3, :], [psA[:, i, :] for i in (2, 4, 5)]

        outer = sb("outer", [P, NT, D])
        inner = sb("inner", [P, NT, D])
        normed = sb("normed", [P, NT, D])
        tot = sb("tot", [P, NT])
        mean = sb("mean", [P, NT])
        vsum = sb("vsum", [P, NT])
        veps = sb("veps", [P, NT])
        std = sb("std", [P, NT])
        rstd = sb("rstd", [P, NT])
        ident = sb("ident", [P, P])
        identb = sb("identb", [P, P], BF16)
        identr = sb("identr", [P, P], F32R)
        xw = sb("xw", [P, 2, 512])
        gcol = sb("gcol", [P, 4])
        fcol = sb("fcol", [P, 2 * L])

        s_x = sem("x_loaded")
        s_const = sem("constants_made")
        s_gain, s_w1 = sem("first_projection_loaded"), sem("first_weights_loaded")
        s_out = sem("out_stored")

        n0 = Norm(sem, "n0", "ln", 1e-5, outer, inner)
        n1 = Norm(sem, "n1", "ln", 1e-6, inner, normed, "whole")
        n2 = Norm(sem, "n2", "ln", 1e-6, inner, normed, "whole")
        n3 = Norm(sem, "n3", "ln", 1e-5, inner, normed)
        n4 = Norm(sem, "n4", "ln", 1e-5, outer, inner)
        n5 = Norm(sem, "n5", "rms", 1e-5, inner, normed, "split")
        n6 = Norm(sem, "n6", "rms", 1e-5, inner, normed, "split")
        n7 = Norm(sem, "n7", "ln", 1e-5, inner, normed)

        first = ExitStack()
        wo1 = sb("wo1", [P, D], where=first)
        b1c = sb("b1c", [P, MCH], where=first)
        b2r = sb("b2r", [P, D], where=first)
        qkv = sb("qkv", [P, NT, 3 * P], where=first)
        qb = sb("qb", [P, NT, H1 * NB], where=first)
        kb = sb("kb", [P, NT, H1 * NB], where=first)
        tmq = sb("tmq", [P, 2, HG, P], F32R, where=first)
        tmk = sb("tmk", [P, 2, HG, P], F32R, where=first)
        mxp1 = sb("mxp1", [P, HG * TPB, 2], where=first)
        mxq1 = sb("mxq1", [P, HG * TPB], where=first)
        mrow = sb("mrow", [HG * TPB, P], F32R, where=first)
        qst = [sb("qst_0", [P, HG, SEQ], F32R, where=first)]
        kst = [sb("kst_0", [P, HG, SEQ], F32R, where=first)]
        pr1 = sb("pr1", [P, 2, HG, 512], where=first)
        osb = xw
        rd1 = sb("rd1", [P, 4, HG], where=first)
        attn1 = normed
        relu1 = pr1
        square1 = pr1[:, 0, :, :].rearrange("p h n -> p (h n)").rearrange("p (t d) -> p t d", t=NT)
        around = ExitStack()
        xT = sb("xT", [P, NT * P], where=around)
        turned = sb("turned", [P, NT * P], where=around)
        w_qkv = sb("w_qkv", [P, 3, P], where=around)
        bd = sb("bd", [P, 2, H1 * NB], where=around)
        smm = sb("smm", [P, 2, H1], where=around)
        sms = sb("sms", [P, 2, H1], where=around)
        smr = sb("smr", [P, 2, H1], where=around)
        around.close()
        qst.append(sb("qst_1", [P, HG, SEQ], F32R, where=first))
        kst.append(sb("kst_1", [P, HG, SEQ], F32R, where=first))
        w_up = bd[:, 0, :]
        w_dn = bd[:, 1, :].rearrange("p (c d) -> p c d", c=MCH)
        v32 = outer[:, :, :].rearrange("p (i t) (h f) -> p i t h f", i=2, h=HG)
        first.close()

        second = ExitStack()
        xh = sb("xh", [P, NT * P], F32R, where=second)
        xl = sb("xl", [P, NT * P], F32R, where=second)
        wst = sb("wst", [P, NKV, CG], where=second)
        wah = sb("wah", [P, NKV, CG], F32R, where=second)
        wal = sb("wal", [P, NKV, CG], F32R, where=second)
        wos = sb("wos", [P, NKV, 2, D], where=second)
        cosT = sb("cosT", [P, TPB, HD], where=second)
        sinT = sb("sinT", [P, TPB, HD], where=second)
        maskq = sb("maskq", [P, P], BF16, where=second)
        maskk = sb("maskk", [P, P], BF16, where=second)
        ones64 = sb("ones64", [P, HD], where=second)
        qs2 = [sb(f"qs2_{b}", [P, TPB, GQ, P], F32R, where=second) for b in range(B)]
        ks = [sb(f"ks_{b}", [P, 2, SEQ], F32R, where=second) for b in range(B)]
        tql = sb("tql", [P, 2, GQ, 2, HD], F32R, where=second)
        tkk = sb("tkk", [P, 4, HD], F32R, where=second)
        vv = [sb(f"vv_{b}", [P, TPB, HD], where=second) for b in range(B)]
        mxp = sb("mxp", [P, GQ, 2], where=second)
        prob = sb("prob", [P, 4, 512], where=second)
        psum_k = sb("psum_k", [P, 2, 512], where=second)
        rden = sb("rden", [P, 256], where=second)
        att = sb("att", [P, 2, 256], where=second)
        wrs = sb("wrs", [P, E], where=second)
        wrp = sb("wrp", [P, 2, E], F32R, where=second)
        comb = sb("comb", [P, NT, E], where=second)
        order = sb("order", [P, E], where=second)
        selcol = sb("selcol", [P, E], where=second)
        sel = sb("sel", [P, 2, P], F32R, where=second)
        zeros = sb("zeros", [P, P], F32R, where=second)
        est = sb("est", [P, WE], where=second)
        eh = [sb(f"eh{i}", [P, WE], F32R, where=second) for i in range(2)]
        el = [sb(f"el{i}", [P, WE], F32R, where=second) for i in range(2)]
        attn_only = ExitStack()
        rope_a = sb("rope_a", [P, 5, HD], where=attn_only)
        rope_b = sb("rope_b", [P, 5, HD], where=attn_only)
        roped = sb("roped", [P, 5, HD], where=attn_only)
        tqh = sb("tqh", [P, GQ, 2, HD], F32R, where=attn_only)
        qs1 = [sb(f"qs1_{b}", [P, TPB, GQ, P], F32R, where=attn_only) for b in range(B)]
        attn_only.close()
        expert_only = ExitStack()
        rt = [sb(f"rt{i}", [P, NT, E], where=expert_only) for i in range(6)]
        r1 = [sb(f"r1_{i}", [P, NT], where=expert_only) for i in range(4)]
        gate = sb("gate", [P, 2, 512], where=expert_only)
        hid = sb("hid", [P, 4, 512], where=expert_only)
        hidh = sb("hidh", [P, 4, 512], F32R, where=expert_only)
        hidl = sb("hidl", [P, 4, 512], F32R, where=expert_only)
        norm_only = ExitStack()
        square2 = sb("square2", [P, NT, D], where=norm_only)[:, :, :]
        norm_only.close()
        combT = sb("combT", [P, NT * P], F32R, where=expert_only)
        expert_only.close()
        second.close()
        for n in (n0, n1, n2, n3):
            n.square = square1
        for n in (n4, n5, n6, n7):
            n.square = square2

        s_qkv, s_qkv_sb = sem("qkv_in_psum"), sem("qkv_in_sbuf")
        s_turn, s_turn_sb = sem("turned_in_psum"), sem("turned_in_sbuf")
        s_lg, s_sma, s_sme, s_smb = sem("logits_in_psum"), sem("cluster_max_off"), sem("cluster_exp"), sem("cluster_sum_inverted")
        s_smn = sem("cluster_normed")
        s_v32c, s_v32 = sem("v32_constants"), sem("v32_filled")
        s_tmc, s_tmh, s_tml = sem("stack1_constants"), sem("stack1_high"), sem("stack1_low")
        s_tt1, s_st, s_stv = sem("stacks1_turned"), sem("q_stack1_stored"), sem("k_stack1_stored")
        s_mm1, s_mr1, s_mt1, s_mc1 = sem("max1_scores"), sem("max1_taken"), sem("max1_turned"), sem("max1_copied")
        s_row, s_w2 = sem("max1_in_stack"), sem("mlp_weights_loaded")
        s_qk1, s_ex1, s_pv1 = sem("scores1"), sem("exp1"), sem("pv1")
        s_oc1, s_ot1, s_on1 = sem("out1_copied"), sem("out1_turned"), sem("out1_normed")
        s_a1t, s_a1s, s_wo1, s_wo1x = sem("attn1_turned"), sem("attn1_stored"), sem("wo1_in_psum"), sem("wo1_added")
        s_up1, s_re1, s_dn1, s_dx1 = sem("up1_in_psum"), sem("relu1"), sem("down1_in_psum"), sem("down1_added")
        s_r1, s_r2 = sem("outer1_updated"), sem("outer2_updated")

        s_cs2, s_cs1, s_c2l = sem("constants2_made"), sem("constants1_zeroed"), sem("constants2_loaded")
        s_aw, s_ew = sem("attention_weights_loaded"), sem("expert_weights_loaded")
        s_wsh, s_wsl = sem("attention_weights_high"), sem("attention_weights_low")
        s_pj, s_rp, s_hi = sem("qkv2_in_psum"), sem("rope_steps"), sem("stack2_high")
        s_tt, s_sa = sem("stacks2_turned"), sem("stacks2_stored")
        s_ms, s_mr, s_mt, s_mw = sem("max2_scores"), sem("max2_taken"), sem("max2_in_psum"), sem("q_low_stack_stored")
        s_qk, s_ex, s_su, s_pv = sem("scores2"), sem("exp2"), sem("probabilities_summed"), sem("pv2")
        s_dn, s_rd, s_at, s_wo, s_wx = (sem("denominator_in_psum"), sem("denominator_inverted"),
                                        sem("attention_normed"), sem("wo2_in_psum"), sem("wo2_added"))
        s_cl1, s_cl2 = sem("clipped_after_attention"), sem("clipped_after_experts")
        s_rl, s_rv, s_re = sem("router_logits_in_psum"), sem("router_steps"), sem("router_exp")
        s_eh, s_el = sem("expert_weights_high"), sem("expert_weights_low")
        s_gu, s_si, s_hf, s_hh, s_hl = (sem("gate_up_in_psum"), sem("silu"), sem("hidden_full"),
                                        sem("hidden_high"), sem("hidden_low"))
        s_cb, s_hc, s_se = sem("routing_weights_in_psum"), sem("hidden_weighted"), sem("expert_selected")
        s_cz = sem("routing_rows_zeroed")
        s_ct, s_cth, s_ctl = sem("routing_weights_turned"), sem("routing_weights_high"), sem("routing_weights_low")
        s_yd, s_yc, s_yt, s_yx = sem("down2_in_psum"), sem("experts_copied"), sem("experts_turned"), sem("experts_added")
        N_ROUTE = 19
        N_UNIT = 8
        AHEAD = 3
        PV_FREE = 2 * TPB + 2
        N_CS2 = 8 + E + 4

        def norm_vector(v, n, run=0, gain=None, bias=None, start=()):
            for s, value in start:
                v.wait_ge(s, value)
            base, k = run * n.steps_vec, 0
            abase, tbase = run * n.steps_act, run * n.steps_ten

            def done(ins):
                nonlocal k
                k += 1
                ins.then_inc(n.vec, 1)

            def own():
                v.wait_ge(n.vec, base + k)

            x = n.src
            if n.kind == "ln":
                done(nc.vector.tensor_reduce(tot[:, :], n.src[:, :, :], AX.X, ALU.add))
                own()
                done(nc.vector.tensor_scalar(mean[:, :], tot[:, :], 1.0 / D, None, ALU.mult))
                own()
                for c in range(4):
                    ts = slice(4 * c, 4 * c + 4)
                    done(nc.vector.tensor_tensor(normed[:, ts, :], n.src[:, ts, :], mean[:, ts].unsqueeze(2).broadcast_to([P, 4, D]),
                                                 ALU.subtract))
                x = normed
            for c in range(4):
                v.wait_ge(n.act, abase + c + 1)
                done(nc.vector.tensor_reduce(vsum[:, 4 * c:4 * c + 4], n.square[:, 4 * c:4 * c + 4, :], AX.X, ALU.add))
            own()
            done(nc.vector.tensor_scalar(veps[:, :], vsum[:, :], 1.0 / D, n.eps, ALU.mult, ALU.add))
            v.wait_ge(n.act, abase + 5)
            done(nc.vector.reciprocal(rstd[:, :], std[:, :]))
            own()
            for c in range(4):
                ts = slice(4 * c, 4 * c + 4)
                done(nc.vector.tensor_tensor(n.out[:, ts, :], x[:, ts, :], rstd[:, ts].unsqueeze(2).broadcast_to([P, 4, D]), ALU.mult))

            def whole(c, dst):
                v.wait_ge(n.ten, tbase + c + 1)
                if bias is None:
                    done(nc.vector.tensor_scalar(dst, psM[:, c % 2, :], gain, None, ALU.mult))
                else:
                    done(nc.vector.tensor_scalar(dst, psM[:, c % 2, :], gain, bias, ALU.mult, ALU.add))

            def low(c):
                v.wait_ge(n.act, abase + 6 + c)
                done(nc.vector.tensor_tensor(xl[:, c * 512:(c + 1) * 512], xw[:, c % 2, :],
                                             xh[:, c * 512:(c + 1) * 512], ALU.subtract))

            if n.turned == "whole":
                for c in range(4):
                    whole(c, xT[:, c * 512:(c + 1) * 512])
            if n.turned == "split":
                whole(0, xw[:, 0, :])
                whole(1, xw[:, 1, :])
                for c in range(4):
                    low(c)
                    if c < 2:
                        own()
                        whole(c + 2, xw[:, c % 2, :])

        def norm_scalar(a, n, run=0, start=()):
            base, vbase = run * n.steps_act, run * n.steps_vec
            x = n.src
            for s, value in start:
                a.wait_ge(s, value)
            for c in range(4):
                if n.kind == "ln":
                    a.wait_ge(n.vec, vbase + n.centred - 3 + c)
                    x = normed
                nc.scalar.activation(n.square[:, 4 * c:4 * c + 4, :], x[:, 4 * c:4 * c + 4, :], ACT.Square).then_inc(n.act, 1)
            a.wait_ge(n.vec, vbase + n.var_ready)
            nc.scalar.activation(std[:, :], veps[:, :], ACT.Sqrt).then_inc(n.act, 1)
            if n.turned == "split":
                for c in range(4):
                    a.wait_ge(n.vec, vbase + n.full(c))
                    nc.scalar.activation(xh[:, c * 512:(c + 1) * 512], xw[:, c % 2, :],
                                         ACT.Copy).then_inc(n.act, 1)

        def norm_tensor(t, n, run=0):
            vbase = run * n.steps_vec
            for c in range(4):
                t.wait_ge(n.vec, vbase + n.out_ready - 3 + c)
                if c >= 2:
                    t.wait_ge(n.vec, vbase + n.full(c - 2))
                for i in range(4):
                    ins = nc.tensor.transpose(psM[:, c % 2, i * P:(i + 1) * P], normed[:, 4 * c + i, :], ident[:, :])
                ins.then_inc(n.ten, 1)

        block = ctx.enter_context(nc.Block())

        @block.sync
        def _(sp):
            sp.dma_start(outer[:, :, :], x_in.rearrange("b (t p) d -> p (b t) d", p=P)).then_inc(s_x, 16)
            for i, c in enumerate((ln1_g, ln1_b, ln2_g, ln2_b)):
                sp.dma_start(gcol[:, i:i + 1], c.rearrange("(d a) -> d a", a=1)).then_inc(s_gain, 16)
            for i, w in enumerate((Wq, Wk, Wv)):
                sp.dma_start(w_qkv[:, i, :], w.rearrange("d h f -> d (h f)")).then_inc(s_gain, 16)
            sp.wait_ge(s_const, 1)
            for i, w in enumerate((Whq, Whk)):
                for h in range(H1):
                    sp.dma_start(bd[h * F1:(h + 1) * F1, i, h * NB:(h + 1) * NB], w[h]).then_inc(s_w1, 16)
            for l in range(L):
                sp.dma_start(fcol[:, l:l + 1], f_ln1[l].rearrange("(d a) -> d a", a=1)).then_inc(s_w1, 16)
                sp.dma_start(fcol[:, L + l:L + l + 1], f_ln2[l].rearrange("(d a) -> d a", a=1)).then_inc(s_w1, 16)
            sp.dma_start(wo1[:, :], Wo.rearrange("h f d -> (h f) d")).then_inc(s_w1, 16)
            for m in range(MCH):
                sp.dma_start(b1c[:, m:m + 1], b1[m * P:(m + 1) * P].rearrange("(p a) -> p a", a=1)).then_inc(s_w1, 16)
            sp.dma_start(b2r[:, :], b2.rearrange("(a d) -> a d", a=1).broadcast_to([P, D])).then_inc(s_w1, 16)
            with sp.Fori(0, NG1) as g:
                for b in range(B):
                    it = g * B + b
                    sp.wait_ge(s_mc1, it + 2)
                    sp.dma_start(qst[b][96:97, :, :].bitcast(F32).rearrange("a h (t n) -> a (h t) n", t=TPB),
                                 mrow[:, :].bitcast(F32)).then_inc(s_row, 16)
            sp.wait_ge(s_pv1, NG1 * B * 2 * TPB + PV_FREE)
            sp.dma_start(w_up, W1).then_inc(s_w2, 16)
            sp.dma_start(w_dn, W2.rearrange("(c p) d -> p c d", p=P)).then_inc(s_w2, 16)
            sp.dma_start(outer[:, :, :], x_in.rearrange("b (t p) d -> p (b t) d", p=P)).then_inc(s_x, 16)
            sp.dma_start(cosT[:, :, :], cos_in.rearrange("(t p) f -> p t f", p=P)).then_inc(s_c2l, 16)
            sp.dma_start(sinT[:, :, :], sin_in.rearrange("(t p) f -> p t f", p=P)).then_inc(s_c2l, 16)
            with sp.Fori(0, L) as l:
                sp.wait_ge(s_cl1, l + 1)
                for g in range(NKV):
                    q0 = g * GQ * HD
                    sp.dma_start(wst[:, g, 0:GQ * HD], wq[ds(l), :, q0:q0 + GQ * HD].rearrange("a d n -> (a d) n")).then_inc(s_aw, 16)
                    sp.dma_start(wst[:, g, GQ * HD:(GQ + 1) * HD], wk[ds(l), :, g * HD:(g + 1) * HD].rearrange("a d n -> (a d) n")).then_inc(s_aw, 16)
                    sp.dma_start(wst[:, g, (GQ + 1) * HD:CG], wv[ds(l), :, g * HD:(g + 1) * HD].rearrange("a d n -> (a d) n")).then_inc(s_aw, 16)
                    for q in range(2):
                        for i in range(2):
                            r0 = q0 + (2 * q + i) * HD
                            sp.dma_start(wos[q * HD:(q + 1) * HD, g, i, :], wo[ds(l), r0:r0 + HD, :].rearrange("a f d -> (a f) d")).then_inc(s_aw, 16)
                sp.dma_start(wrs[:, :], wr[ds(l), :, :].rearrange("a d e -> (a d) e")).then_inc(s_aw, 16)
                sp.wait_ge(s_r1, 1)
                with sp.Fori(0, E) as e:
                    sp.wait_ge(s_el, l * E + e + 1)
                    sp.dma_start(est[:, 0:FF], wg[ds(l), ds(e), :, :].rearrange("a e d n -> (a e d) n")).then_inc(s_ew, 16)
                    sp.dma_start(est[:, FF:2 * FF], wu[ds(l), ds(e), :, :].rearrange("a e d n -> (a e d) n")).then_inc(s_ew, 16)
                    for f in range(2):
                        sp.dma_start(est[:, 2 * FF + f * D:2 * FF + (f + 1) * D],
                                     wd[ds(l), ds(e), f * P:(f + 1) * P, :].rearrange("a e p d -> (a e p) d")).then_inc(s_ew, 16)
            sp.wait_ge(s_r2, 1)
            sp.dma_start(out.rearrange("b (t p) d -> p (b t) d", p=P), outer[:, :, :]).then_inc(s_out, 16)
            sp.wait_ge(s_out, 16)

        N_GAIN = 16 * (4 + 3)
        N_W1 = 16 * (2 * L + 2 + MCH + 2 * H1)
        N_AW = 16 * (7 * NKV + 1)

        @block.gpsimd
        def _(g_):
            g = nc.gpsimd
            g_.sem_inc(s_su, 4)
            g_.sem_inc(s_hl, 4)
            g.memset(bd[:, :, :], 0.0).then_inc(s_const, 1)
            g.memset(ident[:, :], 0.0).then_inc(s_cs1, 1)
            g_.wait_ge(s_cs1, 1)
            g.affine_select(out=ident[:, :], in_=ident[:, :], compare_op=ALU.not_equal, fill=1.0, base=0,
                            pattern=[[-1, P]], channel_multiplier=1).then_inc(s_const, 1)
            g_.wait_ge(s_const, 2)
            g.tensor_scalar(identr[:, :], ident[:, :], 1.0, 1.0, ALU.mult, ALU.mult).then_inc(s_const, 1)
            g.memset(tmq[:, :, :, 96:104].bitcast(F32), 0.0).then_inc(s_tmc, 1)
            g.memset(tmk[:, :, :, 96:104].bitcast(F32), 1.0).then_inc(s_tmc, 1)
            g_.wait_ge(n0.vec, n0.centred)
            g.memset(outer[:, :, :], 0.0).then_inc(s_v32c, 1)
            g_.wait_ge(s_v32c, 1)
            g.memset(v32[:, :, :, :, F1:F1 + 1], 1.0).then_inc(s_v32c, 1)
            for u in range(2 * NT):
                dst = (qb, kb)[u // NT][:, u % NT, :].rearrange("p (h n) -> p h n", h=H1)
                g_.wait_ge(s_smb, 2 * u + 2)
                g.tensor_tensor(dst, dst, smr[:, u % 2, :].unsqueeze(2).broadcast_to([P, H1, NB]), ALU.mult).then_inc(s_smn, 1)
            g_.wait_ge(s_v32c, 2)
            g_.wait_ge(s_qkv_sb, NT)
            with g_.Fori(0, NG1) as gg:
                for b in range(B):
                    it = gg * B + b
                    g_.wait_ge(s_pv1, it * 2 * TPB + 2)
                    g.tensor_copy(v32[:, b, :, :, 0:F1],
                                  qkv[:, b * TPB:(b + 1) * TPB, ds(gg * (HG * F1) + 2 * P, HG * F1)]
                                  .rearrange("p t (h f) -> p t h f", h=HG)).then_inc(s_v32, 1)
            g_.wait_ge(s_r1, 1)
            g.memset(maskq[:, :], 0.0).then_inc(s_cs2, 1)
            g.memset(maskk[:, :], 0.0).then_inc(s_cs2, 1)
            g.memset(ones64[:, :], 1.0).then_inc(s_cs2, 1)
            g.memset(identb[:, :], 0.0).then_inc(s_cs2, 1)
            g.memset(tql[:, :, :, :, :].bitcast(F32), 0.0).then_inc(s_cs2, 1)
            g.memset(tkk[:, :, :].bitcast(F32), 0.0).then_inc(s_cs2, 1)
            g.memset(zeros[:, :].bitcast(F32), 0.0).then_inc(s_cs2, 1)
            g.tensor_tensor(selcol[:, :], ident[:, 0:E], ident[:, 32:32 + E], ALU.add).then_inc(s_cs2, 1)
            for e in range(E):
                g.memset(order[:, e:e + 1], float(E - e)).then_inc(s_cs2, 1)
            g_.wait_ge(s_cs2, 8 + E)
            g.affine_select(out=identb[:, :], in_=identb[:, :], compare_op=ALU.not_equal, fill=1.0, base=0,
                            pattern=[[-1, P]], channel_multiplier=1).then_inc(s_cs2, 1)
            g.affine_select(out=maskq[:, :], in_=maskq[:, :], compare_op=ALU.is_ge, fill=NEG, base=0,
                            pattern=[[-1, P]], channel_multiplier=1).then_inc(s_cs2, 1)
            g.affine_select(out=maskk[:, :], in_=maskk[:, :], compare_op=ALU.is_ge, fill=NEG, base=0,
                            pattern=[[1, P]], channel_multiplier=-1).then_inc(s_cs2, 1)
            g.memset(tkk[:, 2, 0:1].bitcast(F32), -1.0).then_inc(s_cs2, 1)
            def ready(le, e, ee):
                g_.wait_ge(s_eh, le + 1)
                g.tensor_tensor(el[ee][:, :], est[:, :], eh[ee][:, :], ALU.subtract).then_inc(s_el, 1)
                g.tensor_copy(sel[:, ee, :], selcol[:, ds(e)].broadcast_to([P, P])).then_inc(s_se, 1)

            with g_.Fori(0, L) as l:
                ready(l * E, 0, 0)
                with g_.Fori(0, NKV) as gg:
                    for b in range(B):
                        it = (l * NKV + gg) * B + b
                        for t in range(1, TPB):
                            for kt in range(1, t + 1):
                                i = TRI[t] + kt
                                n = it * TRI[TPB] + i
                                g_.wait_ge(s_ex, n + 5)
                                if kt == 1:
                                    g_.wait_ge(s_dn, it * TPB + t + 1)
                                    before = prob[:, (i - 1) % 4, :]
                                else:
                                    g_.wait_ge(s_su, n + 4)
                                    before = psum_k[:, t % 2, :]
                                g.tensor_tensor(psum_k[:, t % 2, :], before, prob[:, i % 4, :],
                                                ALU.add).then_inc(s_su, 1 if kt > 1 else 2 + (t == 1))
                g_.wait_ge(n6.vec, n6.steps_vec * l + n6.var_ready)
                nothing = zeros[:, :].unsqueeze(1).broadcast_to([P, NT, P])
                g.tensor_tensor(combT[:, :].rearrange("p (a n) -> p a n", a=NT), nothing, nothing, ALU.add).then_inc(s_cz, 1)

                def experts(ep, last):
                    for ee in range(2):
                        e = ep * 2 + ee
                        for i in range(N_UNIT):
                            n = (l * E + e) * N_UNIT + i
                            g_.wait_ge(s_hh, n + 5)
                            g.tensor_tensor(hidl[:, i % 4, :], hid[:, i % 4, :], hidh[:, i % 4, :], ALU.subtract).then_inc(s_hl, 1)
                            if i == 4 and not (last and ee == 1):
                                ready(l * E + e + 1, e + 1, 1 - ee)

                with g_.Fori(0, E // 2 - 1) as ep:
                    experts(ep, False)
                experts(E // 2 - 1, True)

        @block.scalar
        def _(a):
            act = nc.scalar.activation
            a.sem_inc(s_ex1, 3)
            a.sem_inc(s_st, 1)
            a.sem_inc(s_mc1, 1)
            a.sem_inc(s_ex, 4)
            a.sem_inc(s_sa, 1)
            a.sem_inc(s_mw, 1)
            a.sem_inc(s_si, 2)
            a.sem_inc(s_hh, 4)
            a.wait_ge(s_x, 16)
            norm_scalar(a, n0)
            norm_scalar(a, n1)
            for T in range(NT):
                a.wait_ge(s_qkv, T + 1)
                act(qkv[:, T, :], psS[:, T % 4, 0:3 * P], ACT.Copy).then_inc(s_qkv_sb, 1)
            for u in range(2 * NT):
                dst = (qb, kb)[u // NT][:, u % NT, :]
                a.wait_ge(s_sma, 2 * u + 2)
                act(dst, dst, ACT.Exp).then_inc(s_sme, 1)
            a.wait_ge(s_tmc, 2)
            a.wait_ge(s_smn, 2 * NT)

            def heads(order, g, b, g_next, b_next):
                it, it_next = g * B + b, g_next * B + b_next
                for what, *i in order["scalar"]:
                    if what == "H":
                        t = i[0]
                        u, T = it_next * TPB + t, b_next * TPB + t
                        qh = qb[:, T, ds(g_next * (HG * NB), HG * NB)].rearrange("p (h n) -> p h n", h=HG)
                        kh = kb[:, T, ds(g_next * (HG * NB), HG * NB)].rearrange("p (h n) -> p h n", h=HG)
                        qq = qkv[:, T, ds(g_next * (HG * F1), HG * F1)].rearrange("p (h f) -> p h f", h=HG)
                        kk = qkv[:, T, ds(g_next * (HG * F1) + P, HG * F1)].rearrange("p (h f) -> p h f", h=HG)
                        a.wait_ge(s_tt1, 2 * u + 1)
                        act(tmq[:, t % 2, :, 0:64].rearrange("p h (r n) -> p h r n", r=2),
                            qh.unsqueeze(2).broadcast_to([P, HG, 2, NB]), ACT.Copy, scale=CLUSTER).then_inc(s_tmh, 1)
                        act(tmq[:, t % 2, :, 104:120].rearrange("p h (r n) -> p h r n", r=2),
                            qq.unsqueeze(2).broadcast_to([P, HG, 2, F1]), ACT.Copy, scale=float(F1) ** -0.5).then_inc(s_tmh, 1)
                        act(tmk[:, t % 2, :, :].rearrange("p h (r n) -> p h r n", r=2)[:, :, :, 0:NB],
                            kh.unsqueeze(2).broadcast_to([P, HG, 2, NB]), ACT.Copy).then_inc(s_tmh, 1)
                        act(tmk[:, t % 2, :, 96:128].rearrange("p h (r n) -> p h r n", r=2)[:, :, :, F1:2 * F1],
                            kk.unsqueeze(2).broadcast_to([P, HG, 2, F1]), ACT.Copy).then_inc(s_tmh, 1)
                    elif what == "E":
                        t = i[0]
                        a.wait_ge(s_tt1, 2 * (it_next * TPB + t) + 4)
                        act(qst[b_next][:, :, t * P:(t + 1) * P], psM1[:, 2 * t % 3, :].rearrange("p (h n) -> p h n", h=HG),
                            ACT.Copy).then_inc(s_st, 1)
                    elif what == "J":
                        a.wait_ge(s_mt1, it_next + 1)
                        act(mrow[:, :], psM1[0:HG * TPB, 2, 0:P], ACT.Copy, scale=-1.0).then_inc(s_mc1, 1)
                    elif what == "S":
                        n = i[0]
                        j, h = n // HG, n % HG
                        a.wait_ge(s_qk1, it * N_S1 + n + 1)
                        if h == 0:
                            a.wait_ge(s_pv1, it * 2 * TPB + j + PV_FREE - 1)
                        act(pr1[:, j % 2, h, :], psS1[:, n % 3, :], ACT.Exp).then_inc(s_ex1, 1)

            heads(CLUSTER_PREPARE, 0, 0, 0, 0)
            with a.Fori(0, NG1 - 1) as g:
                heads(CLUSTER_BOTH, g, 0, g, 1)
                heads(CLUSTER_BOTH, g, 1, g + 1, 0)
            heads(CLUSTER_BOTH, NG1 - 1, 0, NG1 - 1, 1)
            heads(CLUSTER_ATTEND, NG1 - 1, 1, 0, 0)
            norm_scalar(a, n2)
            for c in range(4):
                for m in range(MCH):
                    n = c * MCH + m
                    a.wait_ge(s_up1, n + 1)
                    if c >= 2:
                        a.wait_ge(s_dn1, c - 1)
                    act(relu1[:, c % 2, m, :], psS[:, n % 4, :], ACT.Relu, bias=b1c[:, m:m + 1]).then_inc(s_re1, 1)
            norm_scalar(a, n3)
            norm_scalar(a, n4)

            def split_high(le, ee):
                a.wait_ge(s_ew, 64 * le + 64)
                a.wait_ge(s_yd, N_UNIT * le + 4)
                act(eh[ee][:, :], est[:, :], ACT.Copy).then_inc(s_eh, 1)

            with a.Fori(0, L) as l:
                split_high(l * E, 0)
                a.wait_ge(s_aw, N_AW * l + N_AW)
                act(wah[:, :, :], wst[:, :, :], ACT.Copy).then_inc(s_wsh, 1)
                act(wrp[:, 0, :], wrs[:, :], ACT.Copy).then_inc(s_wsh, 1)
                norm_scalar(a, n5, l, start=((n4.vec, n4.out_ready), (s_cl2, l + 1)))

                def head(order, g, b, g_next, b_next):
                    it = (l * NKV + g) * B + b
                    it_next = (l * NKV + g_next) * B + b_next
                    for what, t, *more in order["scalar"]:
                        if what in "PHLRMN":
                            ahead, t = divmod(t, TPB)
                            (g_to, b_to), it_to = head_after(g_next, b_next, ahead), it_next + ahead
                            u = it_to * TPB + t
                        if what == "H":
                            a.wait_ge(s_rp, 7 * u + 5)
                            act(tqh[:, :, :, :], roped[:, 0:GQ, :].unsqueeze(2).broadcast_to([P, GQ, 2, HD]),
                                ACT.Copy).then_inc(s_hi, 1)
                            act(tkk[:, 0:4:3, :], roped[:, GQ:GQ + 1, :].broadcast_to([P, 2, HD]), ACT.Copy).then_inc(s_hi, 1)
                        elif what == "R":
                            a.wait_ge(s_tt, 2 * u + 1)
                            act(qs1[b_to][:, t, :, :], ring[SLOT[t] % 3].rearrange("p (h n) -> p h n", h=GQ),
                                ACT.Copy).then_inc(s_sa, 1)
                            a.wait_ge(s_tt, 2 * u + 2)
                            act(ks[b_to][:, :, t * P:(t + 1) * P], psP[:, 0:2 * P].rearrange("p (a n) -> p a n", a=2),
                                ACT.Copy).then_inc(s_sa, 1)
                        elif what == "N":
                            a.wait_ge(s_mt, u + 3)
                            act(qs2[b_to][:, t, :, :], ring[(SLOT[t + 1] - 1) % 3].rearrange("p (h n) -> p h n", h=GQ), ACT.Copy).then_inc(s_mw, 1)
                        elif what == "S":
                            i = TRI[t] + more[0]
                            n = it * TRI[TPB] + i
                            a.wait_ge(s_qk, n + 1)
                            a.wait_ge(s_pv, n + 1)
                            a.wait_ge(s_su, n + 1)
                            act(prob[:, i % 4, :], psS[:, i % 2, :], ACT.Exp, scale=float(HD) ** -0.5).then_inc(s_ex, 1)

                head(FIRST, 0, 0, 0, 0)
                with a.Fori(0, NKV - 2) as g:
                    head(MIDDLE, g, 1, g + 1, 0)
                    head(MIDDLE, g + 1, 0, g + 1, 1)
                head(MIDDLE, NKV - 2, 1, NKV - 1, 0)
                head(LAST_PREPARE, NKV - 1, 0, NKV - 1, 1)
                head(LAST, NKV - 1, 1, 0, 0)
                norm_scalar(a, n6, l, start=((s_cl1, l + 2),))
                a.wait_ge(s_rv, N_ROUTE * l + 3)
                act(rt[0][:, :, :], rt[0][:, :, :], ACT.Exp).then_inc(s_re, 1)

                def silu(n, i):
                    a.wait_ge(s_gu, n + 1)
                    a.wait_ge(s_hf, n + 1)
                    act(gate[:, i % 2, :], psG[:, 2 * i % 3, :], ACT.Silu).then_inc(s_si, 1)

                def experts(ep, last):
                    n0 = (l * (E // 2) + ep) * 2 * N_UNIT
                    for i in range(2 * N_UNIT):
                        if not (last and i == 2 * N_UNIT - 1):
                            silu(n0 + i + 1, (i + 1) % (2 * N_UNIT))
                        a.wait_ge(s_hc, n0 + i + 2)
                        a.wait_ge(s_yd, n0 + i + 9)
                        act(hidh[:, i % 4, :], hid[:, i % 4, :], ACT.Copy).then_inc(s_hh, 1)
                        if i % N_UNIT == 3 and not (last and i > N_UNIT):
                            le = (l * (E // 2) + ep) * 2 + i // N_UNIT
                            split_high(le + 1, 1 - i // N_UNIT)

                silu(l * E * N_UNIT, 0)
                a.wait_ge(s_cz, l + 1)
                for c in range(4):
                    a.wait_ge(s_ct, 4 * l + c + 1)
                    act(combT[0:E, c * 512:(c + 1) * 512], acc[c][0:E, :], ACT.Copy).then_inc(s_cth, 1)

                with a.Fori(0, E // 2 - 1) as ep:
                    experts(ep, False)
                experts(E // 2 - 1, True)
                for c in range(4):
                    a.wait_ge(s_yd, (l * E + E) * N_UNIT + 12)
                    act(hid[:, c, :], acc[c], ACT.Copy).then_inc(s_yc, 1)
            norm_scalar(a, n7, 0)

        @block.tensor
        def _(t_):
            mm = nc.tensor.matmul
            t_.sem_inc(s_tt1, 3)
            t_.sem_inc(s_pv1, PV_FREE)
            t_.sem_inc(s_pv, 4)
            t_.sem_inc(s_mt, 2)
            t_.sem_inc(s_dn, 2)
            t_.sem_inc(s_yd, 12)
            t_.wait_ge(s_const, 3)
            norm_tensor(t_, n1)
            t_.wait_ge(s_gain, N_GAIN)
            for T in range(NT):
                t_.wait_ge(n1.vec, n1.full(T // 4))
                if T >= 4:
                    t_.wait_ge(s_qkv_sb, T - 3)
                mm(psS[:, T % 4, 0:3 * P], xT[:, T * P:(T + 1) * P], w_qkv[:, :, :].rearrange("p a n -> p (a n)"),
                   start=True, stop=True).then_inc(s_qkv, 1)
            for n in range(8):
                side, c = n // 4, n % 4
                t_.wait_ge(s_qkv_sb, 4 * c + 4)
                if n >= 2:
                    t_.wait_ge(s_turn_sb, n - 1)
                for i in range(4):
                    ins = nc.tensor.transpose(psM[:, n % 2, i * P:(i + 1) * P], qkv[:, 4 * c + i, side * P:(side + 1) * P], ident[:, :])
                ins.then_inc(s_turn, 1)
            t_.wait_ge(s_w1, N_W1)
            for u in range(2 * NT):
                side, T = u // NT, u % NT
                t_.wait_ge(s_turn_sb, side * 4 + T // 4 + 1)
                if u >= 2:
                    t_.wait_ge(s_sma, 2 * (u - 2) + 2)
                mm(psO[u % 2][:, :], (turned, xT)[side][:, T * P:(T + 1) * P], bd[:, side, :], start=True, stop=True).then_inc(s_lg, 1)

            def heads(order, g, b, g_next, b_next):
                it, it_next = g * B + b, g_next * B + b_next
                for what, *i in order["tensor"]:
                    if what == "T":
                        u, t = it_next * TPB + i[0], i[0]
                        t_.wait_ge(s_tml, 4 * u + 4)
                        if t == 0:
                            t_.wait_ge(s_mc1, it_next + 1)
                        if t > 1:
                            t_.wait_ge(s_stv, u)
                        for h in range(HG):
                            ins = mm(psM1[:, 2 * t % 3, h * P:(h + 1) * P], tmq[:, t % 2, h, :], identr[:, :],
                                     start=True, stop=True)
                        ins.then_inc(s_tt1, 1)
                        if t > 0:
                            t_.wait_ge(s_st, u + 1)
                        for h in range(HG):
                            ins = mm(psM1[:, (2 * t + 1) % 3, h * P:(h + 1) * P], tmk[:, t % 2, h, :], identr[:, :],
                                     start=True, stop=True)
                        ins.then_inc(s_tt1, 1)
                    elif what == "M":
                        m = i[0]
                        h, t, half = m // (2 * TPB), m // 2 % TPB, m % 2
                        if m == 0:
                            t_.wait_ge(s_st, it_next * TPB + TPB + 1)
                            t_.wait_ge(s_stv, it_next * TPB + TPB + 1)
                        if m >= 3:
                            t_.wait_ge(s_mr1, it_next * (N_MAX1 + 1) + m - 1)
                        mm(psM1[:, (m + 1) % 3, :], qst[b_next][:, h, t * P:(t + 1) * P], kst[b_next][:, h, half * 512:(half + 1) * 512],
                           start=True, stop=True).then_inc(s_mm1, 1)
                    elif what == "J":
                        t_.wait_ge(s_mr1, it_next * (N_MAX1 + 1) + N_MAX1 + 2)
                        nc.tensor.transpose(psM1[0:HG * TPB, 2, 0:P], mxq1[:, :], ident[:, :]).then_inc(s_mt1, 1)
                    elif what == "S":
                        n = i[0]
                        c, kt, h = n // (TPB * HG), n // HG % TPB, n % HG
                        if n == 0:
                            t_.wait_ge(s_row, 16 * it + 16)
                        t_.wait_ge(s_ex1, it * N_S1 + max(n + 1, 3))
                        mm(psS1[:, n % 3, :], kst[b][:, h, kt * P:(kt + 1) * P], qst[b][:, h, c * 512:(c + 1) * 512],
                           start=True, stop=True).then_inc(s_qk1, 1)
                    elif what == "V":
                        j = i[0]
                        c, kt = j // TPB, j % TPB
                        step = it * 2 * TPB + j
                        t_.wait_ge(s_ex1, HG * step + HG + 3)
                        if j == 0:
                            t_.wait_ge(s_v32, it + 1)
                        if kt == 0:
                            t_.wait_ge(s_on1, 2 * (it * 2 + c) + 1)
                        for h in range(HG):
                            ins = mm(psO[c][32 * h:32 * h + 32, :], v32[:, b, kt, h, :], pr1[:, j % 2, h, :],
                                     start=(kt == 0), stop=(kt == TPB - 1))
                        ins.then_inc(s_pv1, 1)
                    elif what == "C":
                        c = i[0]
                        t_.wait_ge(s_oc1, it * 2 + c + 1)
                        for n in range(4):
                            ins = nc.tensor.transpose(psO[c][:, n * P:(n + 1) * P], osb[:, c, n * P:(n + 1) * P], ident[:, :])
                        ins.then_inc(s_ot1, 1)

            heads(CLUSTER_PREPARE, 0, 0, 0, 0)
            with t_.Fori(0, NG1 - 1) as g:
                heads(CLUSTER_BOTH, g, 0, g, 1)
                heads(CLUSTER_BOTH, g, 1, g + 1, 0)
            heads(CLUSTER_BOTH, NG1 - 1, 0, NG1 - 1, 1)
            heads(CLUSTER_ATTEND, NG1 - 1, 1, 0, 0)
            for c in range(4):
                t_.wait_ge(s_on1, 4 * NG1 * B + 3)
                if c >= 2:
                    t_.wait_ge(s_a1s, c - 1)
                for i in range(4):
                    ins = nc.tensor.transpose(psM[:, c % 2, i * P:(i + 1) * P], attn1[:, 4 * c + i, :], ident[:, :])
                ins.then_inc(s_a1t, 1)
            for c in range(4):
                t_.wait_ge(s_a1s, c + 1)
                for i in range(4):
                    T = 4 * c + i
                    ins = mm(psS[:, c, i * P:(i + 1) * P], turned[:, T * P:(T + 1) * P], wo1[:, :], start=True, stop=True)
                ins.then_inc(s_wo1, 1)
            norm_tensor(t_, n2)

            def up1(c):
                t_.wait_ge(n2.vec, n2.full(c))
                for m in range(MCH):
                    n = c * MCH + m
                    if n >= 4:
                        t_.wait_ge(s_re1, n - 3)
                    mm(psS[:, n % 4, :], w_up[:, m * P:(m + 1) * P], xT[:, c * 512:(c + 1) * 512],
                       start=True, stop=True).then_inc(s_up1, 1)

            t_.wait_ge(s_w2, 32)
            up1(0)
            for c in range(4):
                if c < 3:
                    up1(c + 1)
                t_.wait_ge(s_re1, 4 * c + 4)
                if c >= 2:
                    t_.wait_ge(s_dx1, c - 1)
                for i in range(4):
                    for m in range(MCH):
                        ins = mm(psO[c % 2][:, i * P:(i + 1) * P], relu1[:, c % 2, m, i * P:(i + 1) * P], w_dn[:, m, :],
                                 start=(m == 0), stop=(m == MCH - 1))
                ins.then_inc(s_dn1, 1)

            t_.wait_ge(s_cs2, N_CS2)
            with t_.Fori(0, L) as l:
                norm_tensor(t_, n5, l)

                def project(u, t, g, b):
                    T = b * TPB + t
                    wh = wah[:, ds(g), :].rearrange("p a n -> p (a n)")
                    wl = wal[:, ds(g), :].rearrange("p a n -> p (a n)")
                    t_.wait_ge(s_sa, 2 * u + 1)
                    mm(psP[:, 0:CG], xh[:, T * P:(T + 1) * P], wh, start=True, stop=False)
                    mm(psP[:, 0:CG], xh[:, T * P:(T + 1) * P], wl, start=False, stop=False)
                    mm(psP[:, 0:CG], xl[:, T * P:(T + 1) * P], wh, start=False, stop=True).then_inc(s_pj, 1)

                def turn(u, t):
                    t_.wait_ge(s_rp, 7 * u + 6)
                    if t == 0:
                        t_.wait_ge(s_mw, u + 1)
                    for h in range(GQ):
                        ins = mm(ring[SLOT[t] % 3][:, h * P:(h + 1) * P], tqh[:, h, :, :].rearrange("p a n -> p (a n)"), identr[:, :],
                                 start=True, stop=True)
                    ins.then_inc(s_tt, 1)
                    for i in range(2):
                        ins = mm(psP[:, i * P:(i + 1) * P], tkk[:, 2 * i:2 * i + 2, :].rearrange("p a n -> p (a n)"), identr[:, :],
                                 start=True, stop=True)
                    ins.then_inc(s_tt, 1)

                def maximum(u, it, t, b, m):
                    if m == 0:
                        t_.wait_ge(s_sa, 2 * u + 3)
                    if m == 1:
                        t_.wait_ge(s_mw, u + 1)
                    if m >= 3:
                        t_.wait_ge(s_mr, it * MAXED[TPB] + MAXED[t] + m - 1)
                    bank = ring[(SLOT[t] + 1 + m) % 3]
                    h, k0, k1 = max_pieces(t)[m]
                    diagonal = k1 == (t + 1) * P
                    ins = mm(bank[:, 0:k1 - k0], qs1[b][:, t, h, :], ks[b][:, 0, k0:k1], start=True, stop=not diagonal)
                    if diagonal:
                        ins = mm(bank[:, k1 - k0 - P:k1 - k0], identb[:, :], maskq[:, :], start=False, stop=True)
                    ins.then_inc(s_ms, 1)

                def turn_low(it, t):
                    t_.wait_ge(s_mr, it * MAXED[TPB] + MAXED[t + 1] + 1)
                    for h in range(GQ):
                        ins = mm(ring[(SLOT[t + 1] - 1) % 3][:, h * P:(h + 1) * P], tql[:, t % 2, h, :, :].rearrange("p a n -> p (a n)"), identr[:, :],
                                 start=True, stop=True)
                    ins.then_inc(s_mt, 1)

                def scores2(it, t, kt, b):
                    i = TRI[t] + kt
                    if kt == 0:
                        t_.wait_ge(s_mw, it * TPB + t + 2)
                    t_.wait_ge(s_ex, it * TRI[TPB] + i + 3)
                    tile = slice(kt * P, (kt + 1) * P)
                    mm(psS[:, i % 2, :], ks[b][:, 0, tile], qs1[b][:, t, :, :].rearrange("p h n -> p (h n)"), start=True, stop=False)
                    ins = mm(psS[:, i % 2, :], ks[b][:, 1, tile], qs2[b][:, t, :, :].rearrange("p h n -> p (h n)"),
                             start=False, stop=(kt < t))
                    if kt == t:
                        ins = mm(psS[:, i % 2, :], identb[:, :], maskk[:, :].unsqueeze(1).broadcast_to([P, GQ, P]), start=False, stop=True)
                    ins.then_inc(s_qk, 1)

                def values(it, t, kt, b):
                    i = TRI[t] + kt
                    t_.wait_ge(s_ex, it * TRI[TPB] + i + 5)
                    if kt == 0:
                        t_.wait_ge(s_wx, it * TPB + t + 1)
                    for q in range(2):
                        ins = mm(psO[t % 2][q * HD:(q + 1) * HD, 0:256], vv[b][:, kt, :], prob[:, i % 4, q * 256:(q + 1) * 256],
                                 start=(kt == 0), stop=(kt == t))
                    ins.then_inc(s_pv, 1)

                def denominator(it, t):
                    total = prob[:, 0, :] if t == 0 else psum_k[:, t % 2, :]
                    if t != 0:
                        t_.wait_ge(s_su, it * TRI[TPB] + (TRI[t] + t if t > 0 else -1) + 5)
                    else:
                        t_.wait_ge(s_ex, it * TRI[TPB] + 5)
                        t_.wait_ge(s_wx, it * TPB + 1)
                    for q in range(2):
                        ins = mm(psO[t % 2][q * HD:(q + 1) * HD, 256:512], ones64[:, :], total[:, q * 256:(q + 1) * 256],
                                 start=True, stop=True)
                    ins.then_inc(s_dn, 1)

                def out_projection(it, t, g):
                    t_.wait_ge(s_at, it * TPB + t + 2)
                    for i in range(2):
                        ins = mm(psO[t % 2][:, 0:D], att[:, t % 2, i * P:(i + 1) * P],
                                 wos[:, ds(g), i, :].rearrange("p a d -> p (a d)"), start=(i == 0), stop=(i == 1))
                    ins.then_inc(s_wo, 1)

                def head(order, g, b, g_next, b_next):
                    it = (l * NKV + g) * B + b
                    it_next = (l * NKV + g_next) * B + b_next
                    for what, t, *more in order["tensor"]:
                        if what in "PHLRMN":
                            ahead, t = divmod(t, TPB)
                            (g_to, b_to), it_to = head_after(g_next, b_next, ahead), it_next + ahead
                            u = it_to * TPB + t
                        if what == "P":
                            project(u, t, g_to, b_to)
                        elif what == "R":
                            turn(u, t)
                        elif what == "M":
                            maximum(u, it_to, t, b_to, *more)
                        elif what == "N":
                            turn_low(it_to, t)
                        elif what == "S":
                            scores2(it, t, *more, b)
                        elif what == "V":
                            values(it, t, *more, b)
                        elif what == "D":
                            denominator(it, t)
                        elif what == "O":
                            out_projection(it, t, head_before(g, b)[0] if t < 0 else g)

                t_.wait_ge(n5.vec, n5.steps_vec * l + n5.steps_vec)
                t_.wait_ge(s_wsl, 2 * l + 2)
                head(FIRST, 0, 0, 0, 0)
                with t_.Fori(0, NKV - 2) as g:
                    head(MIDDLE, g, 1, g + 1, 0)
                    head(MIDDLE, g + 1, 0, g + 1, 1)
                head(MIDDLE, NKV - 2, 1, NKV - 1, 0)
                head(LAST_PREPARE, NKV - 1, 0, NKV - 1, 1)
                head(LAST, NKV - 1, 1, 0, 0)
                norm_tensor(t_, n6, l)
                t_.wait_ge(n6.vec, n6.steps_vec * l + n6.steps_vec)
                for T in range(NT):
                    ts = slice(T * P, (T + 1) * P)
                    o, w = psO[0][:, T * 2 * E:(T + 1) * 2 * E], wrp[:, :, :].rearrange("p a e -> p (a e)")
                    mm(o, xh[:, ts], w, start=True, stop=False)
                    ins = mm(o, xl[:, ts], w, start=False, stop=True)
                ins.then_inc(s_rl, 1)
                def up2(ep, i):
                    pair, i = l * (E // 2) + ep + i // (2 * N_UNIT), i % (2 * N_UNIT)
                    n, ee, c, f = pair * 2 * N_UNIT + i, i // N_UNIT, i // 2 % 4, i % 2
                    cs = slice(c * 512, (c + 1) * 512)
                    if i % N_UNIT == 0:
                        t_.wait_ge(s_el, pair * 2 + ee + 2)
                    if i == 0:
                        t_.wait_ge(s_si, n + 2)
                    else:
                        t_.wait_ge(s_hf, n + 1)
                    expand(psG[:, 2 * i % 3, :], ee, f * P, cs)
                    if i == 0:
                        t_.wait_ge(s_hf, n + 2)
                    else:
                        t_.wait_ge(s_si, n + 2)
                    expand(psG[:, (2 * i + 1) % 3, :], ee, FF + f * P, cs).then_inc(s_gu, 1)

                def expand(dst, ee, w0, cs):
                    mm(dst, eh[ee][:, w0:w0 + P], xh[:, cs], start=True, stop=False)
                    mm(dst, eh[ee][:, w0:w0 + P], xl[:, cs], start=False, stop=False)
                    return mm(dst, el[ee][:, w0:w0 + P], xh[:, cs], start=False, stop=True)

                def weights(ep, i):
                    pair, i = l * (E // 2) + ep + i // (2 * N_UNIT), i % (2 * N_UNIT)
                    ee, c = i // N_UNIT, i // 2 % 4
                    if c == 0:
                        t_.wait_ge(s_se, pair * 2 + ee + 1)
                    t_.wait_ge(s_hc, pair * 2 * N_UNIT + i + 1)
                    mm(psC, sel[:, ee, :], combT[:, c * 512:(c + 1) * 512], start=True, stop=True).then_inc(s_cb, 1)

                def down2(ep, i):
                    n, ee, c, f = (l * (E // 2) + ep) * 2 * N_UNIT + i, i // N_UNIT, i // 2 % 4, i % 2
                    w0 = 2 * FF + f * D
                    t_.wait_ge(s_hl, n + 5)
                    mm(acc[c], eh[ee][:, w0:w0 + D], hidh[:, i % 4, :], start=False, stop=False, skip_group_check=True)
                    mm(acc[c], el[ee][:, w0:w0 + D], hidh[:, i % 4, :], start=False, stop=False, skip_group_check=True)
                    mm(acc[c], eh[ee][:, w0:w0 + D], hidl[:, i % 4, :], start=False, stop=True, skip_group_check=True).then_inc(s_yd, 1)

                def experts(ep, last):
                    for i in range(2 * N_UNIT):
                        more = i + AHEAD < (2 * N_UNIT if last else 3 * N_UNIT)
                        if more:
                            up2(ep, i + AHEAD)
                        down2(ep, i)
                        if more and (i + AHEAD) % 2 == 0:
                            weights(ep, i + AHEAD)

                up2(0, 0)
                up2(0, 1)
                t_.wait_ge(s_rv, N_ROUTE * l + N_ROUTE)
                for c in range(4):
                    for n in range(4):
                        ins = nc.tensor.transpose(acc[c][0:E, n * P:(n + 1) * P], comb[:, 4 * c + n, :], ident[:, :])
                    ins.then_inc(s_ct, 1)
                for c in range(4):
                    t_.wait_ge(s_ctl, 4 * l + c + 1)
                    mm(acc[c], zeros[:, :], xh[:, 0:512], start=True, stop=False, skip_group_check=True)

                weights(0, 0)
                up2(0, 2)
                weights(0, 2)
                with t_.Fori(0, E // 2 - 1) as ep:
                    experts(ep, False)
                experts(E // 2 - 1, True)
                for c in range(4):
                    t_.wait_ge(s_yc, 4 * l + c + 1)
                    for n in range(4):
                        ins = nc.tensor.transpose(psA[:, c, n * P:(n + 1) * P], hid[:, c, n * P:(n + 1) * P], ident[:, :])
                    ins.then_inc(s_yt, 1)

        @block.vector
        def _(v):
            vec = nc.vector
            v.sem_inc(s_on1, 3)
            v.sem_inc(s_stv, 1)
            v.sem_inc(s_mr1, 1)
            v.sem_inc(s_mr, 1)
            v.sem_inc(s_at, 1)
            v.sem_inc(s_wx, 2)
            v.sem_inc(s_cl1, 1)
            v.sem_inc(s_cl2, 1)
            v.sem_inc(s_hf, 2)
            v.sem_inc(s_hc, 1)
            v.sem_inc(s_el, 1)
            v.wait_ge(s_x, 16)
            norm_vector(v, n0)
            v.wait_ge(s_gain, N_GAIN)
            norm_vector(v, n1, 0, gcol[:, 0:1], gcol[:, 1:2], start=((n0.vec, n0.steps_vec),))
            for n in range(8):
                v.wait_ge(s_turn, n + 1)
                vec.tensor_copy((turned, xT)[n // 4][:, (n % 4) * 512:(n % 4 + 1) * 512], psM[:, n % 2, :]).then_inc(s_turn_sb, 1)

            def off(u):
                dst = (qb, kb)[u // NT][:, u % NT, :].rearrange("p (h n) -> p h n", h=H1)
                lg = psO[u % 2][:, :].rearrange("p (h n) -> p h n", h=H1)
                v.wait_ge(s_lg, u + 1)
                vec.tensor_reduce(smm[:, u % 2, :], lg, AX.X, ALU.max).then_inc(s_sma, 1)
                v.wait_ge(s_sma, 2 * u + 1)
                vec.tensor_tensor(dst, lg, smm[:, u % 2, :].unsqueeze(2).broadcast_to([P, H1, NB]), ALU.subtract).then_inc(s_sma, 1)

            off(0)
            for u in range(2 * NT):
                if u + 1 < 2 * NT:
                    off(u + 1)
                dst = (qb, kb)[u // NT][:, u % NT, :].rearrange("p (h n) -> p h n", h=H1)
                v.wait_ge(s_sme, u + 1)
                vec.tensor_reduce(sms[:, u % 2, :], dst, AX.X, ALU.add).then_inc(s_smb, 1)
                if u >= 2:
                    v.wait_ge(s_smn, u - 1)
                v.wait_ge(s_smb, 2 * u + 1)
                vec.reciprocal(smr[:, u % 2, :], sms[:, u % 2, :]).then_inc(s_smb, 1)
            v.wait_ge(s_smn, 2 * NT)

            def heads(order, g, b, g_next, b_next):
                it, it_next = g * B + b, g_next * B + b_next
                for what, *i in order["vector"]:
                    if what == "L":
                        t = i[0]
                        u, T = it_next * TPB + t, b_next * TPB + t
                        qh = qb[:, T, ds(g_next * (HG * NB), HG * NB)].rearrange("p (h n) -> p h n", h=HG)
                        kh = kb[:, T, ds(g_next * (HG * NB), HG * NB)].rearrange("p (h n) -> p h n", h=HG)
                        qq = qkv[:, T, ds(g_next * (HG * F1), HG * F1)].rearrange("p (h f) -> p h f", h=HG)
                        kk = qkv[:, T, ds(g_next * (HG * F1) + P, HG * F1)].rearrange("p (h f) -> p h f", h=HG)
                        tq, tk = tmq[:, t % 2, :, :], tmk[:, t % 2, :, :]
                        v.wait_ge(s_tmh, 4 * u + 4)
                        vec.scalar_tensor_tensor(out=tq[:, :, 64:96], in0=qh, scalar=CLUSTER, in1=tq[:, :, 0:32],
                                                 op0=ALU.mult, op1=ALU.subtract).then_inc(s_tml, 1)
                        vec.scalar_tensor_tensor(out=tq[:, :, 120:128], in0=qq, scalar=float(F1) ** -0.5, in1=tq[:, :, 104:112],
                                                 op0=ALU.mult, op1=ALU.subtract).then_inc(s_tml, 1)
                        vec.tensor_tensor(tk[:, :, 32:64], kh, tk[:, :, 0:32], ALU.subtract).then_inc(s_tml, 1)
                        vec.tensor_tensor(tk[:, :, 112:120], kk, tk[:, :, 104:112], ALU.subtract).then_inc(s_tml, 1)
                    elif what == "E":
                        t = i[0]
                        v.wait_ge(s_tt1, 2 * (it_next * TPB + t) + 5)
                        vec.tensor_copy(kst[b_next][:, :, t * P:(t + 1) * P],
                                        psM1[:, (2 * t + 1) % 3, :].rearrange("p (h n) -> p h n", h=HG)).then_inc(s_stv, 1)
                    elif what == "M":
                        m = i[0]
                        if m == 0:
                            v.wait_ge(s_mr1, it_next * (N_MAX1 + 1) + 1)
                        v.wait_ge(s_mm1, it_next * N_MAX1 + m + 1)
                        vec.tensor_reduce(mxp1[:, m // 2, m % 2:m % 2 + 1], psM1[:, (m + 1) % 3, :], AX.X, ALU.max).then_inc(s_mr1, 1)
                    elif what == "J":
                        v.wait_ge(s_mr1, it_next * (N_MAX1 + 1) + N_MAX1 + 1)
                        vec.tensor_tensor(mxq1[:, :], mxp1[:, :, 0], mxp1[:, :, 1], ALU.max).then_inc(s_mr1, 1)
                    elif what == "C":
                        c = i[0]
                        v.wait_ge(s_pv1, it * 2 * TPB + (c + 1) * TPB + PV_FREE)
                        vec.tensor_copy(osb[:, c, :], psO[c][:, :]).then_inc(s_oc1, 1)
                    elif what == "D":
                        c = i[0]
                        o = it * 2 + c
                        v.wait_ge(s_ot1, o + 1)
                        v.wait_ge(s_on1, 2 * o + 3)
                        tok = psO[c][:, :].rearrange("p (t h f) -> p t h f", t=4, h=HG)
                        vec.reciprocal(rd1[:, :, :], tok[:, :, :, F1]).then_inc(s_on1, 1)
                        v.wait_ge(s_on1, 2 * o + 4)
                        vec.tensor_tensor(attn1[:, b * TPB + 4 * c:b * TPB + 4 * c + 4, ds(g * (HG * F1), HG * F1)]
                                          .rearrange("p t (h f) -> p t h f", h=HG), tok[:, :, :, 0:F1],
                                          rd1[:, :, :].unsqueeze(3).broadcast_to([P, 4, HG, F1]), ALU.mult).then_inc(s_on1, 1)

            heads(CLUSTER_PREPARE, 0, 0, 0, 0)
            with v.Fori(0, NG1 - 1) as g:
                heads(CLUSTER_BOTH, g, 0, g, 1)
                heads(CLUSTER_BOTH, g, 1, g + 1, 0)
            heads(CLUSTER_BOTH, NG1 - 1, 0, NG1 - 1, 1)
            heads(CLUSTER_ATTEND, NG1 - 1, 1, 0, 0)
            for c in range(4):
                v.wait_ge(s_a1t, c + 1)
                vec.tensor_copy(turned[:, c * 512:(c + 1) * 512], psM[:, c % 2, :]).then_inc(s_a1s, 1)
            for c in range(4):
                v.wait_ge(s_wo1, c + 1)
                r = inner[:, 4 * c:4 * c + 4, :].rearrange("p t d -> p (t d)")
                vec.tensor_tensor(r, r, psS[:, c, :], ALU.add).then_inc(s_wo1x, 1)
            norm_vector(v, n2, 0, gcol[:, 2:3], gcol[:, 3:4], start=((s_wo1x, 4),))
            for c in range(4):
                v.wait_ge(s_dn1, c + 1)
                r = inner[:, 4 * c:4 * c + 4, :].rearrange("p t d -> p (t d)")
                vec.tensor_tensor(r, r, psO[c % 2][:, :], ALU.add).then_inc(s_dx1, 1)
            v.wait_ge(s_dx1, 4)
            vec.tensor_tensor(inner[:, :, :], inner[:, :, :], b2r[:, :].unsqueeze(1).broadcast_to([P, NT, D]), ALU.add).then_inc(s_dx1, 1)
            norm_vector(v, n3, start=((s_dx1, 5),))
            v.wait_ge(n3.vec, n3.steps_vec)
            v.wait_ge(s_x, 32)
            vec.tensor_tensor(outer[:, :, :], outer[:, :, :], normed[:, :, :], ALU.add).then_inc(s_r1, 1)
            norm_vector(v, n4, start=((s_r1, 1),))
            v.wait_ge(s_c2l, 32)
            v.wait_ge(s_cs2, N_CS2)
            with v.Fori(0, L) as l:
                v.wait_ge(s_wsh, 2 * l + 2)
                vec.tensor_tensor(wal[:, :, :], wst[:, :, :], wah[:, :, :], ALU.subtract).then_inc(s_wsl, 1)
                vec.tensor_tensor(wrp[:, 1, :], wrs[:, :], wrp[:, 0, :], ALU.subtract).then_inc(s_wsl, 1)
                norm_vector(v, n5, l, fcol[:, ds(l)])

                def head(order, g, b, g_next, b_next):
                    it = (l * NKV + g) * B + b
                    it_next = (l * NKV + g_next) * B + b_next
                    for what, t, *more in order["vector"]:
                        if what in "PHLRMN":
                            ahead, t = divmod(t, TPB)
                            (g_to, b_to), it_to = head_after(g_next, b_next, ahead), it_next + ahead
                            u = it_to * TPB + t
                        tau = it * TPB + t
                        if what == "P":
                            v.wait_ge(s_pj, u + 1)
                            pr = psP[:, 0:5 * HD].rearrange("p (h f) -> p h f", h=5)
                            c_t = cosT[:, t, :].unsqueeze(1).broadcast_to([P, 5, HD])
                            s_lo = sinT[:, t, 0:HD // 2].unsqueeze(1).broadcast_to([P, 5, HD // 2])
                            s_hi_ = sinT[:, t, HD // 2:HD].unsqueeze(1).broadcast_to([P, 5, HD // 2])
                            vec.tensor_tensor(rope_a[:, :, :], pr, c_t, ALU.mult).then_inc(s_rp, 1)
                            vec.tensor_tensor(rope_b[:, :, 0:HD // 2], pr[:, :, HD // 2:HD], s_lo, ALU.mult).then_inc(s_rp, 1)
                            vec.tensor_tensor(rope_b[:, :, HD // 2:HD], pr[:, :, 0:HD // 2], s_hi_, ALU.mult).then_inc(s_rp, 1)
                            vec.tensor_copy(vv[b_to][:, t, :], psP[:, 5 * HD:6 * HD]).then_inc(s_rp, 1)
                            v.wait_ge(s_rp, 7 * u + 4)
                            vec.tensor_tensor(roped[:, :, :], rope_a[:, :, :], rope_b[:, :, :], ALU.add).then_inc(s_rp, 1)
                        elif what == "L":
                            v.wait_ge(s_hi, 2 * u + 2)
                            vec.tensor_tensor(tkk[:, 1, :], roped[:, GQ, :], tkk[:, 0, :], ALU.subtract).then_inc(s_rp, 1)
                            v.wait_ge(s_mt, u + 1)
                            vec.tensor_tensor(tql[:, t % 2, :, 1, :], roped[:, 0:GQ, :], tqh[:, :, 0, :], ALU.subtract).then_inc(s_rp, 1)
                        elif what == "M":
                            m, pieces = more[0], max_pieces(t)
                            joined, done = len(pieces) > GQ, it_to * MAXED[TPB] + MAXED[t] + 1
                            if m == 0 and joined:
                                v.wait_ge(s_mr, done)
                            h, k0, k1 = pieces[m]
                            v.wait_ge(s_ms, it_to * PIECES[TPB] + PIECES[t] + m + 1)
                            dst = mxp[:, h, m % 2:m % 2 + 1] if joined else tql[:, t % 2, h, 0, 0:1]
                            vec.tensor_reduce(dst, ring[(SLOT[t] + 1 + m) % 3][:, 0:k1 - k0], AX.X, ALU.max).then_inc(s_mr, 1)
                            if joined and m == len(pieces) - 1:
                                v.wait_ge(s_mr, done + len(pieces))
                                vec.tensor_tensor(tql[:, t % 2, :, 0, 0], mxp[:, :, 0], mxp[:, :, 1], ALU.max).then_inc(s_mr, 1)
                        elif what == "D":
                            normalise(it, t)
                        elif what == "O":
                            v.wait_ge(s_wo, tau + 1)
                            v.wait_ge(s_wx, tau + 2)
                            T = (b * TPB + t) % NT
                            vec.tensor_tensor(inner[:, T, :], inner[:, T, :], psO[t % 2][:, 0:D], ALU.add).then_inc(s_wx, 1)

                def normalise(it, t):
                    v.wait_ge(s_dn, it * TPB + t + 3)
                    if t == 0:
                        v.wait_ge(s_pv, it * TRI[TPB] + 5)
                    v.wait_ge(s_at, it * TPB + t + 1)
                    vec.reciprocal(rden[:, :], psO[t % 2][:, 256:512]).then_inc(s_rd, 1)
                    v.wait_ge(s_rd, it * TPB + t + 1)
                    vec.tensor_tensor(att[:, t % 2, :], psO[t % 2][:, 0:256], rden[:, :], ALU.mult).then_inc(s_at, 1)

                head(FIRST, 0, 0, 0, 0)
                with v.Fori(0, NKV - 2) as g:
                    head(MIDDLE, g, 1, g + 1, 0)
                    head(MIDDLE, g + 1, 0, g + 1, 1)
                head(MIDDLE, NKV - 2, 1, NKV - 1, 0)
                head(LAST_PREPARE, NKV - 1, 0, NKV - 1, 1)
                head(LAST, NKV - 1, 1, 0, 0)
                v.wait_ge(s_wx, (l * NKV * B + NKV * B) * TPB + 2)
                vec.tensor_scalar(inner[:, :, :], inner[:, :, :], 100.0, -100.0, ALU.min, ALU.max).then_inc(s_cl1, 1)
                norm_vector(v, n6, l, fcol[:, ds(l + L)])

                k = 0

                def route(ins):
                    nonlocal k
                    k += 1
                    ins.then_inc(s_rv, 1)
                    if k < N_ROUTE:
                        v.wait_ge(s_rv, N_ROUTE * l + k)

                def over(x):
                    return x[:, :].unsqueeze(2).broadcast_to([P, NT, E])

                v.wait_ge(s_rl, l + 1)
                lg = rt[4][:, :, :]
                first_of = order[:, :].unsqueeze(1).broadcast_to([P, NT, E])
                route(vec.tensor_reduce(lg, psO[0][:, 0:NT * 2 * E].rearrange("p (t a e) -> p t e a", t=NT, a=2), AX.X, ALU.add))
                route(vec.tensor_reduce(r1[0][:, :], lg, AX.X, ALU.max))
                route(vec.tensor_tensor(rt[0][:, :, :], lg, over(r1[0]), ALU.subtract))
                v.wait_ge(s_re, l + 1)
                route(vec.tensor_reduce(r1[0][:, :], rt[0][:, :, :], AX.X, ALU.max))
                route(vec.tensor_tensor(rt[1][:, :, :], rt[0][:, :, :], over(r1[0]), ALU.is_equal))
                route(vec.tensor_tensor(rt[2][:, :, :], rt[1][:, :, :], first_of, ALU.mult))
                route(vec.tensor_reduce(r1[1][:, :], rt[2][:, :, :], AX.X, ALU.max))
                route(vec.tensor_tensor(rt[1][:, :, :], rt[2][:, :, :], over(r1[1]), ALU.is_equal))
                route(vec.scalar_tensor_tensor(out=rt[3][:, :, :], in0=rt[1][:, :, :], scalar=-2.0, in1=rt[0][:, :, :],
                                               op0=ALU.mult, op1=ALU.add))
                route(vec.tensor_reduce(r1[2][:, :], rt[3][:, :, :], AX.X, ALU.max))
                route(vec.tensor_tensor(rt[4][:, :, :], rt[3][:, :, :], over(r1[2]), ALU.is_equal))
                route(vec.tensor_tensor(rt[2][:, :, :], rt[4][:, :, :], first_of, ALU.mult))
                route(vec.tensor_reduce(r1[1][:, :], rt[2][:, :, :], AX.X, ALU.max))
                route(vec.tensor_tensor(rt[4][:, :, :], rt[2][:, :, :], over(r1[1]), ALU.is_equal))
                route(vec.tensor_tensor(rt[5][:, :, :], rt[1][:, :, :], rt[4][:, :, :], ALU.add))
                route(vec.tensor_tensor(rt[5][:, :, :], rt[5][:, :, :], rt[0][:, :, :], ALU.mult))
                route(vec.tensor_tensor(r1[3][:, :], r1[0][:, :], r1[2][:, :], ALU.add))
                route(vec.reciprocal(r1[3][:, :], r1[3][:, :]))
                route(vec.tensor_tensor(comb[:, :, :], rt[5][:, :, :], over(r1[3]), ALU.mult))
                assert k == N_ROUTE
                for c in range(4):
                    v.wait_ge(s_cth, 4 * l + c + 1)
                    cs = slice(c * 512, (c + 1) * 512)
                    vec.tensor_tensor(combT[32:32 + E, cs], acc[c][0:E, :], combT[0:E, cs], ALU.subtract).then_inc(s_ctl, 1)

                def experts(ep):
                    for i in range(2 * N_UNIT):
                        n = (l * (E // 2) + ep) * 2 * N_UNIT + i
                        v.wait_ge(s_si, n + 3)
                        v.wait_ge(s_hh, n + 1)
                        v.wait_ge(s_hl, n + 1)
                        vec.tensor_tensor(hid[:, i % 4, :], gate[:, i % 2, :], psG[:, (2 * i + 1) % 3, :], ALU.mult).then_inc(s_hf, 1)
                        v.wait_ge(s_hf, n + 3)
                        v.wait_ge(s_cb, (l * (E // 2) + ep) * N_UNIT + i // 2 + 1)
                        vec.tensor_tensor(hid[:, i % 4, :], hid[:, i % 4, :], psC, ALU.mult).then_inc(s_hc, 1)

                with v.Fori(0, E // 2) as ep:
                    experts(ep)
                for c in range(4):
                    v.wait_ge(s_yt, 4 * l + c + 1)
                    r = inner[:, 4 * c:4 * c + 4, :].rearrange("p t d -> p (t d)")
                    vec.tensor_tensor(r, r, psA[:, c, :], ALU.add).then_inc(s_yx, 1)
                v.wait_ge(s_yx, 4 * l + 4)
                vec.tensor_scalar(inner[:, :, :], inner[:, :, :], 100.0, -100.0, ALU.min, ALU.max).then_inc(s_cl2, 1)
            norm_vector(v, n7, start=((s_cl2, L + 1),))
            v.wait_ge(n7.vec, n7.steps_vec)
            vec.tensor_tensor(outer[:, :, :], outer[:, :, :], normed[:, :, :], ALU.add).then_inc(s_r2, 1)


_INS = ["L0_attn_inputs", "L0_attn_ln1_g", "L0_attn_ln1_b", "L0_attn_Wq", "L0_attn_Wk", "L0_attn_Wv", "L0_attn_Whq",
        "L0_attn_Whk", "L0_attn_Wo", "L0_attn_ln2_g", "L0_attn_ln2_b", "L0_attn_W1", "L0_attn_b1", "L0_attn_W2",
        "L0_attn_b2", "L0_ffn_ln1_w", "L0_ffn_ln2_w", "L0_ffn_wq", "L0_ffn_wk", "L0_ffn_wv", "L0_ffn_wo", "L0_ffn_wr",
        "L0_ffn_wg", "L0_ffn_wu", "L0_ffn_wd"]


def rope_tables():
    inv = (1.0 / np.float32(10000.0) ** (np.arange(0, HD, 2, dtype=np.float32) / np.float32(HD))).astype(np.float32)
    f = np.arange(SEQ, dtype=np.float32)[:, None] * inv
    c, s = np.cos(f).astype(np.float32), np.sin(f).astype(np.float32)
    return np.concatenate([c, c], 1), np.concatenate([-s, s], 1)


def kernel(**inputs):
    import concourse.bacc as bacc
    from concourse.bass_utils import run_bass_kernel_spmd as run

    nc = bacc.Bacc("TRN2", target_bir_lowering=False, num_devices=1)
    arrays, args = {}, []
    cos, sin = rope_tables()
    for name, a in [(n, inputs[n]) for n in _INS] + [("rope_cos", cos), ("rope_sin", sin)]:
        a = np.ascontiguousarray(a)
        arrays[f"in_{name}"] = a
        args.append(nc.dram_tensor(f"in_{name}", a.shape, mybir.dt.from_np(a.dtype), kind="ExternalInput").ap())
    args.append(nc.dram_tensor("out_0", (B, SEQ, D), F32, kind="ExternalOutput").ap())
    program(nc, *args)
    r = run(nc, [arrays], core_ids=[0])
    return r.results[0]["out_0"]
```
